# Optimizing a Trainium2 kernel written in Bass

```python
import numpy as np
import jax
import jax.numpy as jnp

def _softmax(x, axis=-1):
    return jax.nn.softmax(x, axis=axis)

def _gelu(x):
    return jax.nn.gelu(x, approximate=True)

def _silu(x):
    return jax.nn.silu(x)

def _sigmoid(x):
    return jax.nn.sigmoid(x)

def _layernorm(x, axis=-1, eps=1e-05):
    m = jnp.mean(x, axis=axis, keepdims=True)
    v = jnp.var(x, axis=axis, keepdims=True)
    return (x - m) / jnp.sqrt(v + eps)

def _scatter_add(tgt, idx, src, axis=0):
    return tgt.at[idx].add(src)

def _segment_sum(src, seg, n):
    return jax.ops.segment_sum(src, seg, n)
kernel_name = 'mk_hybrid_d1_jaxref_r4_762c19'

def setup_inputs(seed: int=0):
    np.random.seed(seed)
    _w = jnp.asarray

    def _L0_attn_a_setup():
        import jax, jax.numpy as jnp
        import numpy as np
        from jax import lax
        D_MODEL = 256
        D_STATE = 64
        HEADDIM = 64
        EXPAND = 2
        D_INNER = EXPAND * D_MODEL
        NHEADS = D_INNER // HEADDIM
        ROPE_FRACTION = min(0.5, HEADDIM / D_STATE)
        ROPE_DIM = int(ROPE_FRACTION * D_STATE)
        key = jax.random.key(seed)
        ks = jax.random.split(key, 8)
        B, L = (2, 512)
        d_in_proj = 2 * D_INNER + 2 * D_STATE + NHEADS
        x = jax.random.normal(ks[0], (B, L, D_MODEL), dtype=jnp.float32)
        W_in = jax.random.normal(ks[1], (D_MODEL, d_in_proj), dtype=jnp.float32) * 0.02
        W_out = jax.random.normal(ks[2], (D_INNER, D_MODEL), dtype=jnp.float32) * 0.02
        dt_bias = jax.random.normal(ks[3], (NHEADS,), dtype=jnp.float32) * 0.1
        A_log = jnp.log(jax.random.uniform(ks[4], (NHEADS,), minval=1.0, maxval=16.0, dtype=jnp.float32))
        D_skip = jnp.ones((NHEADS,), dtype=jnp.float32)
        norm_weight = jnp.ones((D_INNER,), dtype=jnp.float32)
        return {'x': x, 'W_in': W_in, 'W_out': W_out, 'dt_bias': dt_bias, 'A_log': A_log, 'D_skip': D_skip, 'norm_weight': norm_weight}
    _L0_attn_a_in = _L0_attn_a_setup()

    def _L0_attn_b_setup():
        import jax, jax.numpy as jnp
        import numpy as np
        B, L, D, H = (2, 256, 256, 8)
        HD = D // H

        def _deltanet(x, Wq, Wk, Wv, Wb, ln_w, ln_b):
            Bb, Ll, Dd = x.shape
            q = (x @ Wq).reshape(Bb, Ll, H, HD)
            k = (x @ Wk).reshape(Bb, Ll, H, HD)
            k = k / jnp.maximum(jnp.linalg.norm(k, axis=-1, keepdims=True), 1e-12)
            v = jax.nn.silu(x @ Wv).reshape(Bb, Ll, H, HD)
            beta = jax.nn.sigmoid(x @ Wb)
            qs = jnp.moveaxis(q, 1, 0)
            ks_ = jnp.moveaxis(k, 1, 0)
            vs = jnp.moveaxis(v, 1, 0)
            bs = jnp.moveaxis(beta, 1, 0)

            def step(S, inp):
                qt, kt, vt, bt = inp
                Sk = jnp.einsum('bhk,bhkv->bhv', kt, S)
                S = S + jnp.einsum('bh,bhk,bhv->bhkv', bt, kt, vt - Sk)
                ot = jnp.einsum('bhk,bhkv->bhv', qt, S)
                return (S, ot)
            S0 = jnp.zeros((Bb, H, HD, HD), x.dtype)
            _, os_ = jax.lax.scan(step, S0, (qs, ks_, vs, bs))
            o = jnp.moveaxis(os_, 0, 1).reshape(Bb, Ll, Dd)
            mu = jnp.mean(o, axis=-1, keepdims=True)
            var = jnp.var(o, axis=-1, keepdims=True)
            return (o - mu) / jnp.sqrt(var + 1e-05) * ln_w + ln_b
        key = jax.random.key(seed)
        ks = jax.random.split(key, 5)
        s = 1.0 / np.sqrt(D)
        x = jax.random.normal(ks[0], (B, L, D), jnp.float32)
        Wq = jax.random.uniform(ks[1], (D, D), jnp.float32, -s, s)
        Wk = jax.random.uniform(ks[2], (D, D), jnp.float32, -s, s)
        Wv = jax.random.uniform(ks[3], (D, D), jnp.float32, -s, s)
        Wb = jax.random.uniform(ks[4], (D, H), jnp.float32, -s, s)
        ln_w = jnp.ones((D,), jnp.float32)
        ln_b = jnp.zeros((D,), jnp.float32)
        return {'x': x, 'Wq': Wq, 'Wk': Wk, 'Wv': Wv, 'Wb': Wb, 'ln_w': ln_w, 'ln_b': ln_b}
    _L0_attn_b_in = _L0_attn_b_setup()

    def _L0_ffn_setup():
        import jax, jax.numpy as jnp
        import numpy as np
        D_IN, D_HID = (256, 1024)

        def _ternary(key, shape):
            return jax.random.randint(key, shape, -1, 2).astype(jnp.float32)

        def _tlin(x, w, s):
            return jnp.einsum('bsi,oi->bso', x, w) * s
        key = jax.random.key(seed)
        ks = jax.random.split(key, 12)
        inv = lambda fan: 1.0 / np.sqrt(fan).astype(np.float32)
        return {'x': jax.random.normal(ks[0], (4, 512, D_IN), dtype=jnp.float32), 'w1_w': _ternary(ks[1], (D_HID, D_IN)), 'w1_s': jax.random.uniform(ks[2], (D_HID,), dtype=jnp.float32) * inv(D_IN), 'w2_w': _ternary(ks[3], (D_HID, D_IN)), 'w2_s': jax.random.uniform(ks[4], (D_HID,), dtype=jnp.float32) * inv(D_IN), 'h1_w': _ternary(ks[5], (D_HID, D_HID)), 'h1_s': jax.random.uniform(ks[6], (D_HID,), dtype=jnp.float32) * inv(D_HID), 'h2_w': _ternary(ks[7], (D_HID, D_HID)), 'h2_s': jax.random.uniform(ks[8], (D_HID,), dtype=jnp.float32) * inv(D_HID), 'w3_w': _ternary(ks[9], (D_IN, D_HID)), 'w3_s': jax.random.uniform(ks[10], (D_IN,), dtype=jnp.float32) * inv(D_HID)}
    _L0_ffn_in = _L0_ffn_setup()
    _d = {'L0_attn_a_x': _L0_attn_a_in['x'], 'L0_attn_a_W_in': _L0_attn_a_in['W_in'], 'L0_attn_a_W_out': _L0_attn_a_in['W_out'], 'L0_attn_a_dt_bias': _L0_attn_a_in['dt_bias'], 'L0_attn_a_A_log': _L0_attn_a_in['A_log'], 'L0_attn_a_D_skip': _L0_attn_a_in['D_skip'], 'L0_attn_a_norm_weight': _L0_attn_a_in['norm_weight'], 'L0_attn_b_Wq': _L0_attn_b_in['Wq'], 'L0_attn_b_Wk': _L0_attn_b_in['Wk'], 'L0_attn_b_Wv': _L0_attn_b_in['Wv'], 'L0_attn_b_Wb': _L0_attn_b_in['Wb'], 'L0_attn_b_ln_w': _L0_attn_b_in['ln_w'], 'L0_attn_b_ln_b': _L0_attn_b_in['ln_b'], 'L0_ffn_w1_w': _L0_ffn_in['w1_w'], 'L0_ffn_w1_s': _L0_ffn_in['w1_s'], 'L0_ffn_w2_w': _L0_ffn_in['w2_w'], 'L0_ffn_w2_s': _L0_ffn_in['w2_s'], 'L0_ffn_h1_w': _L0_ffn_in['h1_w'], 'L0_ffn_h1_s': _L0_ffn_in['h1_s'], 'L0_ffn_h2_w': _L0_ffn_in['h2_w'], 'L0_ffn_h2_s': _L0_ffn_in['h2_s'], 'L0_ffn_w3_w': _L0_ffn_in['w3_w'], 'L0_ffn_w3_s': _L0_ffn_in['w3_s']}
    _x0 = _d['L0_attn_a_x']
    _d['L0_attn_a_x'] = jax.random.normal(jax.random.fold_in(jax.random.key(seed), 1), (8, 512, 256), dtype=_x0.dtype)
    del _x0
    return _d

def reference(L0_attn_a_x, L0_attn_a_W_in, L0_attn_a_W_out, L0_attn_a_dt_bias, L0_attn_a_A_log, L0_attn_a_D_skip, L0_attn_a_norm_weight, L0_attn_b_Wq, L0_attn_b_Wk, L0_attn_b_Wv, L0_attn_b_Wb, L0_attn_b_ln_w, L0_attn_b_ln_b, L0_ffn_w1_w, L0_ffn_w1_s, L0_ffn_w2_w, L0_ffn_w2_s, L0_ffn_h1_w, L0_ffn_h1_s, L0_ffn_h2_w, L0_ffn_h2_s, L0_ffn_w3_w, L0_ffn_w3_s):

    def _L0_attn_a_ref(x, W_in, W_out, dt_bias, A_log, D_skip, norm_weight):
        import jax, jax.numpy as jnp
        import numpy as np
        from jax import lax
        D_MODEL = 256
        D_STATE = 64
        HEADDIM = 64
        EXPAND = 2
        D_INNER = EXPAND * D_MODEL
        NHEADS = D_INNER // HEADDIM
        ROPE_FRACTION = min(0.5, HEADDIM / D_STATE)
        ROPE_DIM = int(ROPE_FRACTION * D_STATE)
        Bsz, L, _ = x.shape
        H, P, N = (NHEADS, HEADDIM, D_STATE)
        pairs = ROPE_DIM // 2
        zxbcdt = x @ W_in
        z = zxbcdt[..., :D_INNER]
        xs = zxbcdt[..., D_INNER:2 * D_INNER].reshape(Bsz, L, H, P)
        Bm = zxbcdt[..., 2 * D_INNER:2 * D_INNER + N]
        Cm = zxbcdt[..., 2 * D_INNER + N:2 * D_INNER + 2 * N]
        dt = jax.nn.softplus(zxbcdt[..., 2 * D_INNER + 2 * N:] + dt_bias)
        decay = jnp.exp(-jnp.exp(A_log) * dt)
        inv_freq = 1.0 / 10000.0 ** (jnp.arange(pairs, dtype=jnp.float32) / pairs)
        angle = dt[..., None] * inv_freq
        cos, sin = (jnp.cos(angle), jnp.sin(angle))

        def step(h, inp):
            dt_t, dec_t, B_t, C_t, x_t, cos_t, sin_t = inp
            hr = h[:, :, :ROPE_DIM, :].reshape(Bsz, H, pairs, 2, P)
            h1, h2 = (hr[..., 0, :], hr[..., 1, :])
            c, s = (cos_t[..., None], sin_t[..., None])
            rot = jnp.stack([c * h1 - s * h2, s * h1 + c * h2], axis=-2)
            h_rot = jnp.concatenate([rot.reshape(Bsz, H, ROPE_DIM, P), h[:, :, ROPE_DIM:, :]], axis=2)
            h_new = dec_t[..., None, None] * h_rot + dt_t[..., None, None] * B_t[:, None, :, None] * x_t[:, :, None, :]
            y_t = jnp.einsum('bhnp,bn->bhp', h_new, C_t)
            return (h_new, y_t)
        h0 = jnp.zeros((Bsz, H, N, P), x.dtype)
        lfirst = lambda a: jnp.moveaxis(a, 1, 0)
        inputs = (lfirst(dt), lfirst(decay), lfirst(Bm), lfirst(Cm), lfirst(xs), lfirst(cos), lfirst(sin))
        _, ys = lax.scan(step, h0, inputs)
        y = jnp.moveaxis(ys, 0, 1) + D_skip[None, None, :, None] * xs
        y = y.reshape(Bsz, L, D_INNER)
        y = y * jax.nn.silu(z)
        y = y * lax.rsqrt(jnp.mean(y * y, axis=-1, keepdims=True) + 1e-05) * norm_weight
        return y @ W_out

    def _L0_attn_b_ref(x, Wq, Wk, Wv, Wb, ln_w, ln_b):
        import jax, jax.numpy as jnp
        import numpy as np
        B, L, D, H = (2, 256, 256, 8)
        HD = D // H

        def _deltanet(x, Wq, Wk, Wv, Wb, ln_w, ln_b):
            Bb, Ll, Dd = x.shape
            q = (x @ Wq).reshape(Bb, Ll, H, HD)
            k = (x @ Wk).reshape(Bb, Ll, H, HD)
            k = k / jnp.maximum(jnp.linalg.norm(k, axis=-1, keepdims=True), 1e-12)
            v = jax.nn.silu(x @ Wv).reshape(Bb, Ll, H, HD)
            beta = jax.nn.sigmoid(x @ Wb)
            qs = jnp.moveaxis(q, 1, 0)
            ks_ = jnp.moveaxis(k, 1, 0)
            vs = jnp.moveaxis(v, 1, 0)
            bs = jnp.moveaxis(beta, 1, 0)

            def step(S, inp):
                qt, kt, vt, bt = inp
                Sk = jnp.einsum('bhk,bhkv->bhv', kt, S)
                S = S + jnp.einsum('bh,bhk,bhv->bhkv', bt, kt, vt - Sk)
                ot = jnp.einsum('bhk,bhkv->bhv', qt, S)
                return (S, ot)
            S0 = jnp.zeros((Bb, H, HD, HD), x.dtype)
            _, os_ = jax.lax.scan(step, S0, (qs, ks_, vs, bs))
            o = jnp.moveaxis(os_, 0, 1).reshape(Bb, Ll, Dd)
            mu = jnp.mean(o, axis=-1, keepdims=True)
            var = jnp.var(o, axis=-1, keepdims=True)
            return (o - mu) / jnp.sqrt(var + 1e-05) * ln_w + ln_b
        return _deltanet(x, Wq, Wk, Wv, Wb, ln_w, ln_b)

    def _L0_ffn_ref(x, w1_w, w1_s, w2_w, w2_s, h1_w, h1_s, h2_w, h2_s, w3_w, w3_s):
        import jax, jax.numpy as jnp
        import numpy as np
        D_IN, D_HID = (256, 1024)

        def _ternary(key, shape):
            return jax.random.randint(key, shape, -1, 2).astype(jnp.float32)

        def _tlin(x, w, s):
            return jnp.einsum('bsi,oi->bso', x, w) * s
        h = jax.nn.silu(_tlin(x, w1_w, w1_s)) * _tlin(x, w2_w, w2_s)
        h = jax.nn.gelu(_tlin(h, h1_w, h1_s), approximate=False)
        h = jax.nn.gelu(_tlin(h, h2_w, h2_s), approximate=False)
        return _tlin(h, w3_w, w3_s)
    x = L0_attn_a_x
    x = x + _L0_attn_a_ref(_layernorm(x, axis=-1), L0_attn_a_W_in, L0_attn_a_W_out, L0_attn_a_dt_bias, L0_attn_a_A_log, L0_attn_a_D_skip, L0_attn_a_norm_weight)
    x = x + _L0_ffn_ref(_layernorm(x, axis=-1), L0_ffn_w1_w, L0_ffn_w1_s, L0_ffn_w2_w, L0_ffn_w2_s, L0_ffn_h1_w, L0_ffn_h1_s, L0_ffn_h2_w, L0_ffn_h2_s, L0_ffn_w3_w, L0_ffn_w3_s)
    x = x + _L0_attn_b_ref(_layernorm(x, axis=-1), L0_attn_b_Wq, L0_attn_b_Wk, L0_attn_b_Wv, L0_attn_b_Wb, L0_attn_b_ln_w, L0_attn_b_ln_b)
    x = x + _L0_ffn_ref(_layernorm(x, axis=-1), L0_ffn_w1_w, L0_ffn_w1_s, L0_ffn_w2_w, L0_ffn_w2_s, L0_ffn_h1_w, L0_ffn_h1_s, L0_ffn_h2_w, L0_ffn_h2_s, L0_ffn_w3_w, L0_ffn_w3_s)
    return x

_drawn_inputs = setup_inputs


def setup_inputs(seed=0):
    import zlib

    import numpy as np

    out = dict(_drawn_inputs(seed))
    spreads = {'L0_attn_a_D_skip': (1.0, 0.2),
     'L0_attn_a_norm_weight': (1.0, 0.2),
     'L0_attn_b_ln_w': (1.0, 0.2),
     'L0_attn_b_ln_b': (0.0, 0.1)}
    factors = {}
    for name, (base, spread) in spreads.items():
        noise = np.random.default_rng([zlib.crc32(name.encode()), seed]).standard_normal(out[name].shape)
        drawn = base * np.exp(spread * noise) if base else spread * noise
        out[name] = jnp.asarray(drawn.astype(out[name].dtype))
    for name, factor in factors.items():
        out[name] = (out[name] * factor).astype(out[name].dtype)
    return out
```

```python
from contextlib import ExitStack

import concourse.bass as bass
from concourse import mybir

F32 = mybir.dt.float32
F32R = mybir.dt.float32r
BF16 = mybir.dt.bfloat16
ALU = mybir.AluOpType
ACT = mybir.ActivationFunctionType
AX = mybir.AxisListType

P = 128
B, L, D = 8, 512, 256
NT = L // P
EPS = 1e-5
H, HP, N = 8, 64, 64
DI = H * HP
PAIRS = 16
W_IN = 2 * DI + 2 * N + H
DH, HD = 8, 32
BLK = 32
NB = P // BLK
G = 2
W_QKVB = 3 * D + DH
HID = 1024
KT = HID // P
TOK = 256
UNITS = L // TOK
SLICES = 1 + KT + KT // 2 + KT // 2 + 1
HSLICES = KT + KT // 2 + KT // 2

PI = 3.141592653589793
TWO_PI_HI = 6.28125
TWO_PI_LO = 2 * PI - TWO_PI_HI
MAGIC = 1.5 * 2.0 ** 23
PI_SAFE = 3.1415925
FAR = 30000.0


class Signal:

    def __init__(self, handle, per_batch, credit=0):
        self.handle, self.per_batch, self.credit = handle, per_batch, credit

    def at(self, b, n):
        return b * self.per_batch + (n + self.credit)


class Own:

    def __init__(self, eng, sem):
        self.eng, self.sem, self.n = eng, sem, 0

    def restart(self):
        self.eng.sem_clear(self.sem)
        self.n = 0

    def __call__(self, ins):
        self.n += 1
        ins.then_inc(self.sem, 1)
        self.eng.wait_ge(self.sem, self.n)


def bcast(ap, axis, n):
    shape = list(ap.unsqueeze(axis).shape)
    shape[axis] = n
    return ap.unsqueeze(axis).broadcast_to(shape)


def hybrid_kernel(nc, x_in, w_in, w_out, dt_bias, a_log, d_skip, norm_w, wqkvb, ln_w, ln_b,
                  w1, w1s, w2, w2s, h1, h1s, h2, h2s, w3, w3s, a_scr, t_scr, out):
    with ExitStack() as ctx:
        def sb(name, shape, dt=F32):
            return ctx.enter_context(nc.sbuf_tensor(name, shape, dt))

        def sem(name):
            return ctx.enter_context(nc.semaphore(name))

        w1_sb = sb("w1_sb", [P, 2, HID], F32R)
        w2_sb = sb("w2_sb", [P, 2, HID], F32R)
        h1_sb = sb("h1_sb", [P, KT, HID], F32R)
        h2_sb = sb("h2_sb", [P, KT, HID], F32R)
        w3_sb = sb("w3_sb", [P, KT, D], F32R)
        win_sb = sb("win_sb", [P, 2, W_IN])
        wout_sb = sb("wout_sb", [P, 4, D])
        wqkvb_sb = sb("wqkvb_sb", [P, 2, W_QKVB])
        s1_sb = sb("s1_sb", [P, KT])
        s2_sb = sb("s2_sb", [P, KT])
        sh1_sb = sb("sh1_sb", [P, KT])
        sh2_sb = sb("sh2_sb", [P, KT])
        nw_sb = sb("nw_sb", [P, 4])
        w3s_row = sb("w3s_row", [P, D])
        lnw_row = sb("lnw_row", [P, D])
        lnb_row = sb("lnb_row", [P, D])
        bias_row = sb("bias_row", [P, H])
        a_row = sb("a_row", [P, H])
        d_row = sb("d_row", [P, H])
        ident = sb("ident", [P, P])
        ones = sb("ones", [P, P])
        tri = sb("tri", [P, P])
        stri = sb("stri", [P, P])
        far_i = sb("far_i", [P, P], BF16)
        past = sb("past", [P, 4, P], BF16)
        freq = sb("freq", [P, PAIRS])
        half_pi = sb("half_pi", [P, 1])
        neg_half = sb("neg_half", [P, 8])
        smask = sb("smask", [P, BLK])
        umask = sb("umask", [P, BLK])
        bdmask = sb("bdmask", [P, 4])
        x_sb = sb("x_sb", [P, NT, D])
        bst = sb("bst", [P, NT, 6])
        mv = sb("mv", [P, NT, 2])
        ve = sb("ve", [P, NT])
        rstd = sb("rstd", [P, NT])
        xf_hi = sb("xf_hi", [P, 2, 2, P], F32R)
        xf_lo = sb("xf_lo", [P, 2, 2, P], F32R)
        hA_hi = sb("hA_hi", [P, KT, TOK], F32R)
        hA_lo = sb("hA_lo", [P, KT, TOK], F32R)
        hB_hi = sb("hB_hi", [P, KT, TOK], F32R)
        hB_lo = sb("hB_lo", [P, KT, TOK], F32R)
        hid = sb("hid", [P, 2, 2, TOK])
        gate = sb("gate", [P, 2, TOK])
        xnf = sb("xnf", [P, 2, D])
        ffo = sb("ffo", [P, 2, D])

        with ExitStack() as ssm:
            def sa(name, shape, dt=F32):
                return ssm.enter_context(nc.sbuf_tensor(name, shape, dt))
            xn = sa("xn", [P, D])
            xT = sa("xT", [P, 2, P])
            sz = sa("sz", [P, DI])
            xs = sa("xs", [P, H, HP])
            bc = sa("bc", [P, 2, N])
            dtv = sa("dtv", [P, H])
            dtab = sa("dtab", [P, H])
            dte = sa("dte", [P, H])
            dtl = sa("dtl", [P, H])
            dta = sa("dta", [P, 2, H])
            seg = sa("seg", [P, H, P])
            sums = sa("sums", [P, 40])
            decays = sa("decays", [P, 3, H])
            phase = sa("phase", [P, H, PAIRS])
            ang = sa("ang", [P, 2, H, PAIRS])
            angk = sa("angk", [P, 2, H, PAIRS])
            angr = sa("angr", [P, H, PAIRS])
            anga = sa("anga", [P, H, PAIRS])
            cosT = sa("cosT", [P, H, PAIRS])
            sinT = sa("sinT", [P, H, PAIRS])
            hat = sa("hat", [P, 2, H, N])
            bT = sa("bT", [P, 4, P])
            cT = sa("cT", [P, 4, 2, P])
            dec = sa("dec", [P, H, P])
            xdt = sa("xdt", [P, H, HP])
            wrow = sa("wrow", [P, H])
            wx = sa("wx", [P, H, HP])
            xD = sa("xD", [P, H, HP])
            y = sa("y", [P, H, HP])
            yT = sa("yT", [P, 4, P])
            yss = sa("yss", [P, 1])
            yve = sa("yve", [P, 1])
            yrstd = sa("yrstd", [P, 1])
            r1, r2 = [y[:].rearrange("p h d -> p (h d)")[:, i * D:(i + 1) * D].rearrange(
                "p (k h n) -> p k h n", k=2, h=H) for i in range(2)]
            r3, r4 = [yT[:].rearrange("p k n -> p (k n)")[:, i * D:(i + 1) * D].rearrange(
                "p (k h n) -> p k h n", k=2, h=H) for i in range(2)]
            hst = sa("hst", [P, 4, HP])
        with ExitStack() as dl:
            def sd(name, shape, dt=F32):
                return dl.enter_context(nc.sbuf_tensor(name, shape, dt))
            xnd = sd("xnd", [P, D])
            xTd = sd("xTd", [P, 2, P])
            uw = sd("uw", [P, NT, DH, 2, HD])
            pc = sd("pc", [P, NT, DH, BLK])
            qT = sd("qT", [P, NT, G, P])
            kn = sd("kn", [P, NT, DH, HD])
            ti = sd("ti", [P, BLK, BLK])
            srow = sd("srow", [P, DH])
            rn = sd("rn", [P, DH])
            be = sd("be", [P, DH])
            be1 = sd("be1", [P, DH])
            beta = sd("beta", [P, DH])
            dbst = sd("dbst", [P, 6])
            dmv = sd("dmv", [P, 2])
            dve_ = sd("dve_", [P, 1])
            drs = sd("drs", [P, 1])
            with ExitStack() as d1:
                def s1_(name, shape):
                    return d1.enter_context(nc.sbuf_tensor(name, shape, F32))
                q_sb = s1_("q_sb", [P, D])
                k_sb = s1_("k_sb", [P, DH, HD])
                v_sb = s1_("v_sb", [P, DH, HD])
                ksq = s1_("ksq", [P, DH, HD])
                kT = s1_("kT", [P, G, P])
                kqpad = s1_("kqpad", [P, G, 2, 4, P])
                bmask = s1_("bmask", [P, DH, BLK])
                am = s1_("am", [P, DH, BLK])
            with ExitStack() as d2:
                def s2_(name, shape):
                    return d2.enter_context(nc.sbuf_tensor(name, shape, F32))
                au = s2_("au", [P, BLK, BLK])
                prod = s2_("prod", [P, BLK * BLK])
            with ExitStack() as d3:
                def s3_(name, shape):
                    return d3.enter_context(nc.sbuf_tensor(name, shape, F32))
                tbd = s3_("tbd", [P, DH, P])
                pbd = s3_("pbd", [P, DH, P])
                u_sb = s3_("u_sb", [P, DH, HD])
                w_sb = s3_("w_sb", [P, DH, HD])
                wT = s3_("wT", [P, G, P])
                sbd = s3_("sbd", [P, G, P])
                on = s3_("on", [P, D])

        F = [ctx.enter_context(nc.psum_tensor(f"F{i}", [P, 512], F32)) for i in range(4)]
        Q = [ctx.enter_context(nc.psum_tensor(f"Q{i}", [P, 512], F32)) for i in range(4)]

        w_dma = sem("w_dma")
        wr_dma = sem("wr_dma")
        dve_own, act_own, pool_own = sem("dve_own"), sem("act_own"), sem("pool_own")
        pool_gate = sem("pool_gate")
        const_done = sem("const_done")
        wout_done = sem("wout_done")
        arow_done = sem("arow_done")
        x_loaded = Signal(sem("x_loaded"), 16)
        x_stored = Signal(sem("x_stored"), 16, 16)
        x_final = Signal(sem("x_final"), 1)
        stats = Signal(sem("stats"), 4)
        rstd_ok = Signal(sem("rstd_ok"), 4)
        a_xn = Signal(sem("a_xn"), NT)
        a_xTp = Signal(sem("a_xTp"), NT)
        a_xT = Signal(sem("a_xT"), NT)
        a_proj = Signal(sem("a_proj"), NT)
        a_dtv = Signal(sem("a_dtv"), NT)
        a_soft = Signal(sem("a_soft"), NT)
        a_zx = Signal(sem("a_zx"), NT)
        a_seg = Signal(sem("a_seg"), NT)
        a_sums = Signal(sem("a_sums"), NT)
        a_segp = Signal(sem("a_segp"), NT)
        a_sumc = Signal(sem("a_sumc"), NT)
        a_dec = Signal(sem("a_dec"), NT)
        a_ang = Signal(sem("a_ang"), NT)
        a_trig = Signal(sem("a_trig"), NT)
        a_exp = Signal(sem("a_exp"), NT)
        a_flat = Signal(sem("a_flat"), NT)
        a_hat = Signal(sem("a_hat"), NT)
        a_hatT = Signal(sem("a_hatT"), NT)
        a_bT = Signal(sem("a_bT"), NT)
        a_cT = Signal(sem("a_cT"), NT)
        a_score = Signal(sem("a_score"), NT)
        a_pm = Signal(sem("a_pm"), NT)
        a_wx = Signal(sem("a_wx"), NT)
        a_y = Signal(sem("a_y"), NT)
        a_yv = Signal(sem("a_yv"), NT)
        a_ysq = Signal(sem("a_ysq"), NT)
        a_yr = Signal(sem("a_yr"), NT)
        a_yTp = Signal(sem("a_yTp"), NT)
        a_yT = Signal(sem("a_yT"), NT)
        a_out = Signal(sem("a_out"), NT)
        a_clear = Signal(sem("a_clear"), 1)
        f_xn = Signal(sem("f_xn"), 2 * UNITS)
        f_ps = Signal(sem("f_ps"), 2 * UNITS * SLICES)
        f_free = Signal(sem("f_free"), 2 * UNITS * SLICES, 4)
        f_xhi = Signal(sem("f_xhi"), 2 * UNITS)
        f_xlo = Signal(sem("f_xlo"), 2 * UNITS)
        f_act = Signal(sem("f_act"), 2 * UNITS * HSLICES)
        f_hi = Signal(sem("f_hi"), 2 * UNITS * HSLICES)
        f_lo = Signal(sem("f_lo"), 2 * UNITS * HSLICES, 2)
        d_clear = Signal(sem("d_clear"), 2)
        d_xn = Signal(sem("d_xn"), NT)
        d_xTp = Signal(sem("d_xTp"), NT)
        d_xT = Signal(sem("d_xT"), NT)
        d_proj = Signal(sem("d_proj"), NT)
        d_qkv = Signal(sem("d_qkv"), NT)
        d_ss = Signal(sem("d_ss"), NT)
        d_rn = Signal(sem("d_rn"), NT)
        d_kn = Signal(sem("d_kn"), NT)
        d_beta = Signal(sem("d_beta"), NT)
        d_bm = Signal(sem("d_bm"), NT)
        d_kqT = Signal(sem("d_kqT"), NT)
        d_kqc = Signal(sem("d_kqc"), NT)
        d_padA = Signal(sem("d_padA"), NT)
        d_padV = Signal(sem("d_padV"), NT)
        d_gram = Signal(sem("d_gram"), NT)
        d_am = Signal(sem("d_am"), NT)
        d_ast = Signal(sem("d_ast"), NT * NB * 16)
        d_aun = Signal(sem("d_aun"), 16)
        d_inv = Signal(sem("d_inv"), 1)
        d_tst = Signal(sem("d_tst"), 16)
        d_tbd = Signal(sem("d_tbd"), NT * NB * 16)
        d_pbd = Signal(sem("d_pbd"), NT)
        d_uwp = Signal(sem("d_uwp"), NT)
        d_uwc = Signal(sem("d_uwc"), NT)
        d_wTp = Signal(sem("d_wTp"), NT)
        d_wT = Signal(sem("d_wT"), NT)
        d_ws = Signal(sem("d_ws"), NT * NB)
        d_u = Signal(sem("d_u"), NT * NB)
        d_sp = Signal(sem("d_sp"), NT * NB)
        d_s = Signal(sem("d_s"), NT * NB)
        d_o = Signal(sem("d_o"), NT)
        d_ost = Signal(sem("d_ost"), NT)
        d_ors = Signal(sem("d_ors"), NT)
        d_done = Signal(sem("d_done"), NT)

        x_v = x_in.rearrange("(b t p) d -> p b t d", p=P, t=NT)
        o_v = out.rearrange("(b t p) d -> p b t d", p=P, t=NT)
        a_store = a_scr.rearrange("t c h i j -> t c i h j")
        a_load = a_scr.rearrange("t c h i j -> (t c h) (i j)")
        t_store = t_scr.rearrange("t c h j i -> (t c h) (j i)")
        t_load = t_scr.rearrange("t c h j i -> t c j h i")

        block = ctx.enter_context(nc.Block())

        def ffn_dst(j):
            if j < KT:
                return hA_hi[:, j:j + 1, :], hA_lo[:, j:j + 1, :], 1
            if j < KT + KT // 2:
                k = 2 * (j - KT)
                return hB_hi[:, k:k + 2, :], hB_lo[:, k:k + 2, :], 2
            k = 2 * (j - KT - KT // 2)
            return hA_hi[:, k:k + 2, :], hA_lo[:, k:k + 2, :], 2

        def ffn_slice(j):
            return 1 + j

        @block.sync
        def _(sp):
            sp.dma_start(win_sb[:], w_in.rearrange("(k p) n -> p k n", p=P)).then_inc(w_dma, 16)
            sp.dma_start(wout_sb[:], w_out.rearrange("(k p) n -> p k n", p=P)).then_inc(w_dma, 16)
            sp.dma_start(wqkvb_sb[:], wqkvb.rearrange("(k p) n -> p k n", p=P)).then_inc(w_dma, 16)
            for dst, src in ((s1_sb, w1s), (s2_sb, w2s), (sh1_sb, h1s), (sh2_sb, h2s), (nw_sb, norm_w)):
                sp.dma_start(dst[:], src).then_inc(w_dma, 16)
            for dst, src in ((w3s_row, w3s), (lnw_row, ln_w), (lnb_row, ln_b), (bias_row, dt_bias),
                             (a_row, a_log), (d_row, d_skip)):
                sp.dma_start(dst[:], src.partition_broadcast(P)).then_inc(w_dma, 16)
            with sp.Fori(0, B) as b:
                sp.wait_ge(x_stored.handle, x_stored.at(b, 0))
                sp.dma_start(x_sb[:], x_v[:, bass.ds(b, 1)].squeeze(1)).then_inc(x_loaded.handle, 16)
                for t in range(NT):
                    sp.wait_ge(d_am.handle, d_am.at(b, t + 1))
                    for c in range(NB):
                        sp.dma_start(a_store[t, c], am[BLK * c:BLK * (c + 1)]).then_inc(d_ast.handle, 16)
                sp.wait_ge(d_ast.handle, d_ast.at(b, NT * NB * 16))
                sp.dma_start(au[:].rearrange("p i j -> p (i j)"), a_load).then_inc(d_aun.handle, 16)
                sp.wait_ge(d_inv.handle, d_inv.at(b, 1))
                sp.dma_start(t_store, ti[:].rearrange("p j i -> p (j i)")).then_inc(d_tst.handle, 16)
                sp.wait_ge(d_tst.handle, d_tst.at(b, 16))
                sp.wait_ge(d_clear.handle, d_clear.at(b, 2))
                for t in range(NT):
                    if t:
                        sp.wait_ge(d_uwp.handle, d_uwp.at(b, t))
                    for c in range(NB):
                        sp.dma_start(tbd[BLK * c:BLK * (c + 1), :, BLK * c:BLK * (c + 1)],
                                     t_load[t, c]).then_inc(d_tbd.handle, 16)
                sp.wait_ge(x_final.handle, x_final.at(b, 1))
                sp.dma_start(o_v[:, bass.ds(b, 1)].squeeze(1), x_sb[:]).then_inc(x_stored.handle, 16)
            sp.wait_ge(x_stored.handle, x_stored.credit + 16 * B)

        @block.gpsimd
        def _(pool):
            own = Own(pool, pool_own)
            pool.sem_inc(x_stored.handle, x_stored.credit)
            pool.sem_inc(f_free.handle, f_free.credit)
            pool.sem_inc(f_lo.handle, f_lo.credit)
            for dst, src in ((w1_sb, w1), (w2_sb, w2), (h1_sb, h1), (h2_sb, h2), (w3_sb, w3)):
                pool.dma_start(dst[:], src.rearrange("(k p) o -> p k o", p=P)).then_inc(wr_dma, 16)

            def select(out_, in_, pattern, op, fill, mult, base=0):
                own(pool.affine_select(out=out_, in_=in_, pattern=pattern, compare_op=op, fill=fill,
                                       base=base, channel_multiplier=mult))

            own(pool.memset(ones[:], 1.0))
            own(pool.memset(far_i[:], FAR))
            own(pool.memset(past[:], 1.0))
            own(pool.memset(half_pi[:], PI / 2))
            own(pool.memset(neg_half[:], -0.5))
            own(pool.memset(bdmask[:], 1.0))
            for i in range(PAIRS):
                own(pool.memset(freq[:, i:i + 1], float(1.0 / 10000.0 ** (i / PAIRS))))
            select(ident[:], ones[:], [[-1, P]], ALU.is_equal, 0.0, 1)
            select(far_i[:], far_i[:], [[-1, P]], ALU.is_equal, 0.0, 1)
            select(tri[:], ones[:], [[1, P]], ALU.is_ge, 0.0, -1)
            select(stri[:], ones[:], [[-1, P]], ALU.is_gt, 0.0, 1)
            select(past[:], past[:], [[0, 4], [-1, P]], ALU.is_gt, 0.0, 1)
            for c in range(NB):
                s = slice(BLK * c, BLK * (c + 1))
                select(smask[s], ones[s, 0:BLK], [[-1, BLK]], ALU.is_gt, 0.0, 1)
                select(umask[s], ones[s, 0:BLK], [[1, BLK]], ALU.is_ge, 0.0, -1)
                select(bdmask[s], bdmask[s], [[1, 4]], ALU.is_equal, 0.0, 0, base=-c)
            pool.sem_inc(const_done, 1)

            def rsqrt_stats(b, n):
                pool.wait_ge(stats.handle, stats.at(b, n + 1))
                pool.sem_inc(pool_gate, 1)
                own(pool.tensor_scalar(ve[:], mv[:, :, 1], EPS, None, ALU.add))
                pool.tensor_tensor(rstd[:], ve[:], neg_half[:, 0:NT],
                                   ALU.pow).then_inc(rstd_ok.handle, 1)

            def ffn_lo(b, f):
                for u in range(UNITS):
                    for j in range(HSLICES):
                        n = (f * UNITS + u) * HSLICES + j
                        pool.wait_ge(f_hi.handle, f_hi.at(b, n + 1))
                        hi, lo, w = ffn_dst(j)
                        src = hid[:, n % 2, 0:w, :]
                        pool.tensor_tensor(lo, src, hi.bitcast(F32), ALU.subtract).then_inc(f_lo.handle, 1)

            with pool.Fori(0, B) as b:
                own.restart()
                rsqrt_stats(b, 0)
                own(pool.memset(cT[:], 0.0))
                own(pool.memset(hst[:], 0.0))
                pool.memset(phase[:], 0.0).then_inc(a_clear.handle, 1)
                for t in range(NT):
                    pool.wait_ge(a_zx.handle, a_zx.at(b, t + 1))
                    pool.wait_ge(a_sumc.handle, a_sumc.at(b, t + 1))
                    pool.tensor_tensor(xdt[:], xs[:], bcast(dta[:, 0, :], 2, HP), ALU.mult)
                    pool.tensor_tensor(xD[:], xs[:], bcast(d_row[:], 2, HP), ALU.mult)
                    pool.wait_ge(a_dec.handle, a_dec.at(b, t + 1))
                    own(pool.tensor_tensor(wrow[:], decays[:, 2, :], dta[:, 0, :], ALU.mult))
                    pool.tensor_tensor(wx[:], xs[:], bcast(wrow[:], 2, HP), ALU.mult).then_inc(a_wx.handle, 1)
                    pool.wait_ge(a_ysq.handle, a_ysq.at(b, t + 1))
                    pool.sem_inc(pool_gate, 1)
                    own(pool.tensor_scalar(yve[:], yss[:], 1.0 / DI, EPS, ALU.mult, ALU.add))
                    pool.tensor_tensor(yrstd[:], yve[:], neg_half[:, 0:1], ALU.pow).then_inc(a_yr.handle, 1)
                rsqrt_stats(b, 1)
                ffn_lo(b, 0)
                rsqrt_stats(b, 2)
                own(pool.memset(kqpad[:], 0.0))
                own(pool.memset(ti[:], 0.0))
                own(pool.affine_select(out=ti[:], in_=ti[:], pattern=[[1, BLK], [-1, BLK]],
                                       compare_op=ALU.not_equal, fill=1.0, base=0, channel_multiplier=0))
                pool.sem_inc(d_clear.handle, 1)
                for t in range(NT):
                    pool.wait_ge(d_ss.handle, d_ss.at(b, t + 1))
                    pool.tensor_tensor(rn[:], srow[:], neg_half[:], ALU.pow).then_inc(d_rn.handle, 1)
                    pool.wait_ge(d_beta.handle, d_beta.at(b, t + 1))
                    pool.tensor_tensor(bmask[:], bcast(smask[:], 1, DH), bcast(beta[:], 2, BLK),
                                       ALU.mult).then_inc(d_bm.handle, 1)
                pool.wait_ge(d_inv.handle, d_inv.at(b, 1))
                pool.sem_inc(pool_gate, 1)
                own(pool.memset(tbd[:], 0.0))
                own(pool.memset(sbd[:], 0.0))
                own(pool.memset(pbd[:], 0.0))
                pool.sem_inc(d_clear.handle, 1)
                for t in range(NT):
                    if t:
                        pool.wait_ge(d_o.handle, d_o.at(b, t))
                        pool.wait_ge(d_ors.handle, d_ors.at(b, t))
                        pool.sem_inc(pool_gate, 1)
                    for c in range(NB):
                        s = slice(BLK * c, BLK * (c + 1))
                        own(pool.tensor_copy(pbd[s, :, s], pc[s, t]))
                    pool.sem_inc(d_pbd.handle, 1)
                    pool.wait_ge(d_ost.handle, d_ost.at(b, t + 1))
                    pool.sem_inc(pool_gate, 1)
                    own(pool.tensor_scalar(dve_[:], dmv[:, 1:2], EPS, None, ALU.add))
                    pool.tensor_tensor(drs[:], dve_[:], neg_half[:, 0:1], ALU.pow).then_inc(d_ors.handle, 1)
                rsqrt_stats(b, 3)
                ffn_lo(b, 1)

        @block.scalar
        def _(act):
            own = Own(act, act_own)
            act.wait_ge(w_dma, 16 * 14)
            act.activation(a_row[:], a_row[:], ACT.Exp).then_inc(arow_done, 1)
            act.wait_ge(const_done, 1)

            def ffn(b, f):
                for u in range(UNITS):
                    unit = f * UNITS + u
                    s0 = unit * SLICES
                    act.wait_ge(f_ps.handle, f_ps.at(b, s0 + 1))
                    act.copy(xf_hi[:].rearrange("p t k n -> p (t k n)"), F[s0 % 4][:]).then_inc(f_xhi.handle, 1)
                    for j in range(HSLICES):
                        n = unit * HSLICES + j
                        s = s0 + ffn_slice(j)
                        act.wait_ge(f_ps.handle, f_ps.at(b, s + 1))
                        act.wait_ge(f_lo.handle, f_lo.at(b, n - 1))
                        ps = F[s % 4]
                        if j < KT:
                            act.activation(gate[:, n % 2, :], ps[:, 0:TOK], ACT.Silu,
                                           scale=s1_sb[:, j:j + 1]).then_inc(f_act.handle, 1)
                            continue
                        scales, k = (sh1_sb, 2 * (j - KT)) if j < KT + KT // 2 else (sh2_sb, 2 * (j - KT - KT // 2))
                        act.activation(hid[:, n % 2, 0, :], ps[:, 0:TOK], ACT.Gelu, scale=scales[:, k:k + 1])
                        act.activation(hid[:, n % 2, 1, :], ps[:, TOK:2 * TOK], ACT.Gelu,
                                       scale=scales[:, k + 1:k + 2]).then_inc(f_act.handle, 1)

            with act.Fori(0, B) as b:
                own.restart()
                for t in range(NT):
                    act.wait_ge(a_xTp.handle, a_xTp.at(b, t + 1))
                    act.copy(xT[:].rearrange("p k n -> p (k n)"), Q[0][:, 0:D]).then_inc(a_xT.handle, 1)
                    act.wait_ge(a_dtv.handle, a_dtv.at(b, t + 1))
                    own(act.activation(dtab[:], dtv[:], ACT.Abs))
                    own(act.activation(dte[:], dtab[:], ACT.Exp, scale=-1.0))
                    act.activation(dtl[:], dte[:], ACT.Ln, bias=1.0).then_inc(a_soft.handle, 1)
                    act.copy(bc[:].rearrange("p k n -> p (k n)"), Q[3][:, 0:2 * N])
                    act.copy(xs[:].rearrange("p k n -> p (k n)"), Q[2][:])
                    own(act.activation(sz[:], Q[1][:], ACT.Silu))
                    act.sem_inc(a_zx.handle, 1)
                    act.copy(hat[:, :, :, 2 * PAIRS:N], bcast(bc[:, :, 2 * PAIRS:N], 2, H)).then_inc(a_flat.handle, 1)
                    act.wait_ge(a_ang.handle, a_ang.at(b, t + 1))
                    own(act.activation(anga[:], angr[:], ACT.Abs))
                    act.activation(sinT[:], angr[:], ACT.Sin)
                    act.activation(cosT[:], anga[:], ACT.Sin, scale=-1.0, bias=half_pi[:]).then_inc(a_trig.handle, 1)
                    act.activation(decays[:].rearrange("p k h -> p (k h)"), sums[:, 16:40], ACT.Exp,
                                   scale=-1.0).then_inc(a_dec.handle, 1)
                    act.wait_ge(a_segp.handle, a_segp.at(b, t + 1))
                    act.activation(dec[:, 0:4, :].rearrange("p h t -> p (h t)"), Q[1][:], ACT.Exp, scale=-1.0)
                    act.activation(dec[:, 4:8, :].rearrange("p h t -> p (h t)"), Q[2][:], ACT.Exp,
                                   scale=-1.0).then_inc(a_exp.handle, 1)
                    act.wait_ge(a_hatT.handle, a_hatT.at(b, t + 1))
                    act.copy(bT[:].rearrange("p k n -> p (k n)"), Q[3][:]).then_inc(a_bT.handle, 1)
                    act.wait_ge(a_yv.handle, a_yv.at(b, t + 1))
                    act.activation(yT[:].rearrange("p k n -> p (k n)"), y[:].rearrange("p h d -> p (h d)"), ACT.Square,
                                   accum_out=yss[:]).then_inc(a_ysq.handle, 1)
                    act.wait_ge(a_ysq.handle, a_ysq.at(b, t + 1))
                    act.wait_ge(a_yTp.handle, a_yTp.at(b, t + 1))
                    act.copy(yT[:].rearrange("p k n -> p (k n)"), Q[3][:]).then_inc(a_yT.handle, 1)
                ffn(b, 0)
                for t in range(NT):
                    act.wait_ge(d_xTp.handle, d_xTp.at(b, t + 1))
                    act.copy(xTd[:].rearrange("p k n -> p (k n)"), Q[0][:, 0:D]).then_inc(d_xT.handle, 1)
                    act.wait_ge(d_proj.handle, d_proj.at(b, t + 1))
                    act.copy(q_sb[:], Q[1][:, 0:D])
                    act.copy(k_sb[:].rearrange("p h d -> p (h d)"), Q[1][:, D:2 * D])
                    act.activation(ksq[:].rearrange("p h d -> p (h d)"), Q[1][:, D:2 * D], ACT.Square)
                    act.activation(be[:], Q[2][:, D:D + DH], ACT.Exp, scale=-1.0)
                    act.activation(v_sb[:].rearrange("p h d -> p (h d)"), Q[2][:, 0:D],
                                   ACT.Silu).then_inc(d_qkv.handle, 1)
                    act.wait_ge(d_kqT.handle, d_kqT.at(b, t + 1))
                    act.copy(qT[:, t].rearrange("p g n -> p (g n)"), Q[3][:, 0:D])
                    own(act.copy(kT[:].rearrange("p g n -> p (g n)"), Q[3][:, D:2 * D]))
                    act.sem_inc(d_kqc.handle, 1)
                    for h in range(2):
                        s = slice(HD * h, HD * (h + 1))
                        act.copy(kqpad[s, :, 0, h, :], kT[s])
                        last = act.copy(kqpad[s, :, 1, h, :], qT[s, t])
                    last.then_inc(d_padA.handle, 1)
                for t in range(NT):
                    act.wait_ge(d_uwp.handle, d_uwp.at(b, t + 1))
                    uwp = Q[1][:].rearrange("p (h k d) -> p k h d", h=DH, k=2)
                    act.copy(w_sb[:], uwp[:, 1])
                    act.copy(u_sb[:], uwp[:, 0]).then_inc(d_uwc.handle, 1)
                    act.wait_ge(d_wTp.handle, d_wTp.at(b, t + 1))
                    act.copy(wT[:].rearrange("p g n -> p (g n)"), Q[1][:, 0:D]).then_inc(d_wT.handle, 1)
                ffn(b, 1)

        @block.vector
        def _(dve):
            own = Own(dve, dve_own)
            dve.wait_ge(w_dma, 16 * 14)
            for k in range(4):
                last = dve.tensor_scalar(wout_sb[:, k, :], wout_sb[:, k, :], nw_sb[:, k:k + 1], None, ALU.mult)
            last.then_inc(wout_done, 1)
            dve.wait_ge(const_done, 1)
            dve.wait_ge(arow_done, 1)

            def norm_stats(b, n):
                for t in range(NT):
                    last = dve.bn_stats(bst[:, t, :], x_sb[:, t, :])
                own(last)
                for t in range(NT):
                    last = dve.bn_aggr(mv[:, t, :], bst[:, t, :])
                last.then_inc(stats.handle, 1)

            def normed(dst, t):
                return dve.tensor_scalar(dst, x_sb[:, t, :], mv[:, t, 0:1], rstd[:, t:t + 1],
                                         ALU.subtract, ALU.mult)

            def ffn(b, f):
                norm_stats(b, 2 * f + 1)
                dve.wait_ge(rstd_ok.handle, rstd_ok.at(b, 2 * f + 2))
                for u in range(UNITS):
                    unit = f * UNITS + u
                    s0 = unit * SLICES
                    normed(xnf[:, 0, :], 2 * u)
                    normed(xnf[:, 1, :], 2 * u + 1).then_inc(f_xn.handle, 1)
                    dve.wait_ge(f_xhi.handle, f_xhi.at(b, unit + 1))
                    dve.tensor_tensor(xf_lo[:].rearrange("p t k n -> p (t k n)"), F[s0 % 4][:],
                                      xf_hi[:].rearrange("p t k n -> p (t k n)").bitcast(F32),
                                      ALU.subtract).then_inc(f_xlo.handle, 1)
                    dve.wait_ge(f_xlo.handle, f_xlo.at(b, unit + 1))
                    dve.sem_inc(f_free.handle, 1)
                    for j in range(HSLICES):
                        n = unit * HSLICES + j
                        s = s0 + ffn_slice(j)
                        dve.wait_ge(f_act.handle, f_act.at(b, n + 1))
                        hi, lo, w = ffn_dst(j)
                        if j < KT:
                            dve.wait_ge(f_lo.handle, f_lo.at(b, n - 1))
                            own(dve.scalar_tensor_tensor(hid[:, n % 2, 0, :], F[s % 4][:, TOK:2 * TOK],
                                                         s2_sb[:, j:j + 1], gate[:, n % 2, :],
                                                         ALU.mult, ALU.mult))
                        dve.sem_inc(f_free.handle, 1)
                        dve.tensor_copy(hi, hid[:, n % 2, 0:w, :]).then_inc(f_hi.handle, 1)
                    s = s0 + SLICES - 1
                    dve.wait_ge(f_ps.handle, f_ps.at(b, s + 1))
                    o = F[s % 4][:].rearrange("p (t d) -> p t d", t=2)
                    own(dve.tensor_tensor(ffo[:], o, bcast(w3s_row[:], 1, 2), ALU.mult))
                    dve.sem_inc(f_free.handle, 1)
                    own(dve.tensor_tensor(x_sb[:, 2 * u:2 * u + 2, :], x_sb[:, 2 * u:2 * u + 2, :],
                                          ffo[:], ALU.add))

            with dve.Fori(0, B) as b:
                own.restart()
                dve.wait_ge(x_loaded.handle, x_loaded.at(b, 16))
                norm_stats(b, 0)
                dve.wait_ge(rstd_ok.handle, rstd_ok.at(b, 1))
                dve.wait_ge(a_clear.handle, a_clear.at(b, 1))
                for t in range(NT):
                    normed(xn[:], t).then_inc(a_xn.handle, 1)
                    dve.wait_ge(a_proj.handle, a_proj.at(b, t + 1))
                    dve.tensor_tensor(dtv[:], Q[3][:, 2 * N:2 * N + H], bias_row[:], ALU.add).then_inc(a_dtv.handle, 1)
                    dve.wait_ge(a_soft.handle, a_soft.at(b, t + 1))
                    own(dve.scalar_tensor_tensor(dta[:, 0, :], dtv[:], 0.0, dtl[:], ALU.max, ALU.add))
                    own(dve.tensor_tensor(dta[:, 1, :], dta[:, 0, :], a_row[:], ALU.mult))
                    dve.tensor_tensor(seg[:], bcast(stri[:], 1, H), bcast(dta[:, 1, :], 2, P),
                                      ALU.mult).then_inc(a_seg.handle, 1)
                    dve.wait_ge(a_sums.handle, a_sums.at(b, t + 1))
                    own(dve.tensor_copy(sums[:], Q[0][:, 0:40]))
                    dve.sem_inc(a_sumc.handle, 1)
                    own(dve.tensor_tensor(ang[:], bcast(sums[:, 0:16].rearrange("p (k h) -> p k h", k=2), 3, PAIRS),
                                          freq[:].unsqueeze(1).unsqueeze(1).broadcast_to([P, 2, H, PAIRS]), ALU.mult))
                    own(dve.tensor_tensor(ang[:], ang[:], bcast(phase[:], 1, 2), ALU.add))
                    own(dve.tensor_scalar(angk[:], ang[:], 1.0 / (2 * PI), MAGIC, ALU.mult, ALU.add))
                    own(dve.tensor_scalar(angk[:], angk[:], MAGIC, None, ALU.subtract))
                    own(dve.scalar_tensor_tensor(ang[:], angk[:], -TWO_PI_HI, ang[:], ALU.mult, ALU.add))
                    own(dve.scalar_tensor_tensor(ang[:], angk[:], -TWO_PI_LO, ang[:], ALU.mult, ALU.add))
                    dve.tensor_scalar(angr[:], ang[:, 0], PI_SAFE, -PI_SAFE, ALU.min, ALU.max).then_inc(a_ang.handle, 1)
                    dve.tensor_copy(phase[:], ang[:, 1])
                    dve.wait_ge(a_trig.handle, a_trig.at(b, t + 1))
                    pair = bc[:, :, 0:2 * PAIRS].rearrange("p k (n two) -> p k two n", two=2)
                    v1 = bcast(pair[:, :, 0], 2, H)
                    v2 = bcast(pair[:, :, 1], 2, H)
                    c_, s_ = bcast(cosT[:], 1, 2), bcast(sinT[:], 1, 2)
                    dve.tensor_tensor(r1, v1, c_, ALU.mult)
                    dve.tensor_tensor(r2, v2, s_, ALU.mult)
                    dve.tensor_tensor(r3, v2, c_, ALU.mult)
                    own(dve.tensor_tensor(r4, v1, s_, ALU.mult))
                    rot = hat[:, :, :, 0:2 * PAIRS].rearrange("p k h (n two) -> p k h two n", two=2)
                    dve.tensor_tensor(rot[:, :, :, 0], r1, r2, ALU.add)
                    dve.tensor_tensor(rot[:, :, :, 1], r3, r4, ALU.subtract).then_inc(a_hat.handle, 1)
                    dve.wait_ge(a_hatT.handle, a_hatT.at(b, t + 1))
                    cps = Q[0][:].rearrange("p (k n) -> p k n", k=4)
                    dve.tensor_copy(cT[0:64, :, 0, :], cps[0:64])
                    dve.tensor_copy(cT[64:128, :, 1, :], cps[64:128]).then_inc(a_cT.handle, 1)
                    dve.wait_ge(a_score.handle, a_score.at(b, t + 1))
                    for i in range(2):
                        d_ = dec[:, 4 * i:4 * i + 4, :].rearrange("p h t -> p (h t)")
                        last = dve.tensor_tensor(d_, Q[1 + i][:], d_, ALU.mult)
                    last.then_inc(a_pm.handle, 1)
                    dve.wait_ge(a_y.handle, a_y.at(b, t + 1))
                    own(dve.tensor_tensor(y[:], Q[0][:].rearrange("p (h d) -> p h d", h=H),
                                          bcast(decays[:, 0, :], 2, HP), ALU.mult))
                    own(dve.tensor_tensor(y[:], Q[3][:].rearrange("p (h d) -> p h d", h=H), y[:], ALU.add))
                    own(dve.tensor_tensor(y[:], y[:], xD[:], ALU.add))
                    dve.tensor_tensor(y[:].rearrange("p h d -> p (h d)"), y[:].rearrange("p h d -> p (h d)"), sz[:],
                                      ALU.mult).then_inc(a_yv.handle, 1)
                    dl_ = decays[:, 1, :].rearrange("p (k two) -> p two k", two=2)
                    dve.tensor_tensor(hst[0:64], hst[0:64], bcast(dl_[0:64, 0], 2, HP), ALU.mult)
                    own(dve.tensor_tensor(hst[64:128], hst[64:128], bcast(dl_[64:128, 1], 2, HP), ALU.mult))
                    own(dve.tensor_tensor(hst[:].rearrange("p k d -> p (k d)"), Q[1][:, 0:4 * HP],
                                          hst[:].rearrange("p k d -> p (k d)"), ALU.add))
                    dve.wait_ge(a_out.handle, a_out.at(b, t + 1))
                    dve.wait_ge(a_yr.handle, a_yr.at(b, t + 1))
                    own(dve.scalar_tensor_tensor(x_sb[:, t, :], Q[2][:, 0:D], yrstd[:], x_sb[:, t, :],
                                                 ALU.mult, ALU.add))
                ffn(b, 0)
                norm_stats(b, 2)
                dve.wait_ge(rstd_ok.handle, rstd_ok.at(b, 3))
                dve.wait_ge(d_clear.handle, d_clear.at(b, 1))
                for t in range(NT):
                    normed(xnd[:], t).then_inc(d_xn.handle, 1)
                    dve.wait_ge(d_qkv.handle, d_qkv.at(b, t + 1))
                    own(dve.tensor_reduce(srow[:], ksq[:], AX.X, ALU.add))
                    dve.tensor_scalar(srow[:], srow[:], 1e-24, None, ALU.max).then_inc(d_ss.handle, 1)
                    own(dve.tensor_scalar(be1[:], be[:], 1.0, None, ALU.add))
                    own(dve.reciprocal(beta[:], be1[:]))
                    dve.sem_inc(d_beta.handle, 1)
                    dve.tensor_tensor(uw[:, t, :, 0, :], v_sb[:], bcast(beta[:], 2, HD), ALU.mult)
                    dve.wait_ge(d_rn.handle, d_rn.at(b, t + 1))
                    own(dve.tensor_tensor(kn[:, t], k_sb[:], bcast(rn[:], 2, HD), ALU.mult))
                    dve.sem_inc(d_kn.handle, 1)
                    dve.tensor_tensor(uw[:, t, :, 1, :], kn[:, t], bcast(beta[:], 2, HD), ALU.mult)
                    dve.wait_ge(d_kqc.handle, d_kqc.at(b, t + 1))
                    for h in range(2, 4):
                        s = slice(HD * h, HD * (h + 1))
                        dve.tensor_copy(kqpad[s, :, 0, h, :], kT[s])
                        last = dve.tensor_copy(kqpad[s, :, 1, h, :], qT[s, t])
                    last.then_inc(d_padV.handle, 1)
                    dve.wait_ge(d_gram.handle, d_gram.at(b, t + 1))
                    dve.wait_ge(d_bm.handle, d_bm.at(b, t + 1))
                    if t:
                        dve.wait_ge(d_ast.handle, d_ast.at(b, t * NB * 16))
                    gram = Q[1][:].rearrange("p (g k h i) -> p k g h i", g=G, k=2, h=4)
                    dve.tensor_tensor(am[:].rearrange("p (g h) i -> p g h i", g=G), gram[:, 0],
                                      bmask[:].rearrange("p (g h) i -> p g h i", g=G),
                                      ALU.mult).then_inc(d_am.handle, 1)
                    own(dve.tensor_tensor(pc[:, t].rearrange("p (g h) i -> p g h i", g=G), gram[:, 1],
                                          umask[:].unsqueeze(1).unsqueeze(1).broadcast_to([P, G, 4, BLK]), ALU.mult))
                dve.wait_ge(d_aun.handle, d_aun.at(b, 16))
                for i in range(1, BLK):
                    pr = prod[:, 0:i * i].rearrange("p (c j) -> p c j", c=i)
                    own(dve.tensor_tensor(pr, ti[:, 0:i, 0:i], bcast(au[:, i, 0:i], 1, i), ALU.mult))
                    own(dve.tensor_reduce(ti[:, 0:i, i], pr, AX.X, ALU.add, negate=True))
                dve.sem_inc(d_inv.handle, 1)
                dve.wait_ge(d_clear.handle, d_clear.at(b, 2))
                for t in range(NT):
                    dve.wait_ge(d_uwc.handle, d_uwc.at(b, t + 1))
                    for c in range(NB):
                        n = t * NB + c
                        s = slice(BLK * c, BLK * (c + 1))
                        dve.wait_ge(d_ws.handle, d_ws.at(b, n + 1))
                        us = u_sb[s].rearrange("p h d -> p (h d)")
                        dve.scalar_tensor_tensor(us, Q[0][s, 0:D], -1.0, us, ALU.mult,
                                                 ALU.add).then_inc(d_u.handle, 1)
                        dve.wait_ge(d_sp.handle, d_sp.at(b, n + 1))
                        for g in range(G):
                            last = dve.tensor_tensor(sbd[:, g, :].rearrange("p (h d) -> p h d", h=4),
                                                     Q[3][:, g * P:(g + 1) * P].rearrange("p (h d) -> p h d", h=4),
                                                     bcast(bdmask[:], 2, HD), ALU.mult)
                        last.then_inc(d_s.handle, 1)
                    dve.wait_ge(d_o.handle, d_o.at(b, t + 1))
                    own(dve.bn_stats(dbst[:], Q[2][:, 0:D]))
                    dve.bn_aggr(dmv[:], dbst[:]).then_inc(d_ost.handle, 1)
                    dve.wait_ge(d_ors.handle, d_ors.at(b, t + 1))
                    own(dve.tensor_scalar(on[:], Q[2][:, 0:D], dmv[:, 0:1], drs[:], ALU.subtract, ALU.mult))
                    dve.sem_inc(d_done.handle, 1)
                    own(dve.tensor_tensor(on[:], on[:], lnw_row[:], ALU.mult))
                    own(dve.tensor_tensor(on[:], on[:], lnb_row[:], ALU.add))
                    own(dve.tensor_tensor(x_sb[:, t, :], x_sb[:, t, :], on[:], ALU.add))
                ffn(b, 1)
                dve.sem_inc(x_final.handle, 1)

        @block.tensor
        def _(pe):
            pe.wait_ge(w_dma, 16 * 14)
            pe.wait_ge(const_done, 1)
            pe.wait_ge(wout_done, 1)

            def ffn(b, f):
                for u in range(UNITS):
                    unit = f * UNITS + u
                    s0 = unit * SLICES
                    n0 = unit * HSLICES

                    def bank(s):
                        pe.wait_ge(f_free.handle, f_free.at(b, s - 3))
                        return F[s % 4]

                    pe.wait_ge(f_xn.handle, f_xn.at(b, unit + 1))
                    ps = bank(s0)
                    for t in range(2):
                        for k in range(2):
                            o = (2 * t + k) * P
                            last = pe.transpose(ps[:, o:o + P], xnf[:, t, k * P:(k + 1) * P], ident[:])
                    last.then_inc(f_ps.handle, 1)
                    pe.wait_ge(f_xlo.handle, f_xlo.at(b, unit + 1))
                    for j in range(KT):
                        ps = bank(s0 + 1 + j)
                        for i, w in enumerate((w1_sb, w2_sb)):
                            for k in range(2):
                                for part in (xf_hi, xf_lo):
                                    last = pe.matmul(ps[:, i * TOK:(i + 1) * TOK].rearrange("p (t n) -> p t n", t=2),
                                                     w[:, k, j * P:(j + 1) * P], part[:, :, k, :],
                                                     start=(k == 0 and part is xf_hi), stop=(k == 1 and part is xf_lo))
                        last.then_inc(f_ps.handle, 1)
                    for layer, (w, src) in enumerate(((h1_sb, (hA_hi, hA_lo)), (h2_sb, (hB_hi, hB_lo)))):
                        for j in range(KT // 2):
                            ps = bank(s0 + 1 + KT + layer * (KT // 2) + j)
                            for i in range(2):
                                o = (2 * j + i) * P
                                for k in range(KT):
                                    if j == 0 and i == 0:
                                        done = k + 1 if layer == 0 else KT + k // 2 + 1
                                        pe.wait_ge(f_lo.handle, f_lo.at(b, n0 + done))
                                    for part in src:
                                        last = pe.matmul(ps[:, i * TOK:(i + 1) * TOK], w[:, k, o:o + P], part[:, k, :],
                                                         start=(k == 0 and part is src[0]),
                                                         stop=(k == KT - 1 and part is src[1]))
                            last.then_inc(f_ps.handle, 1)
                    ps = bank(s0 + SLICES - 1)
                    for t in range(2):
                        for k in range(KT):
                            if t == 0:
                                pe.wait_ge(f_lo.handle, f_lo.at(b, n0 + KT + KT // 2 + k // 2 + 1))
                            for part in (hA_hi, hA_lo):
                                last = pe.matmul(ps[:, t * D:(t + 1) * D], part[:, k, t * P:(t + 1) * P], w3_sb[:, k, :],
                                                 start=(k == 0 and part is hA_hi), stop=(k == KT - 1 and part is hA_lo))
                    last.then_inc(f_ps.handle, 1)

            with pe.Fori(0, B) as b:
                for t in range(NT):
                    pe.wait_ge(a_xn.handle, a_xn.at(b, t + 1))
                    for k in range(2):
                        last = pe.transpose(Q[0][:, k * P:(k + 1) * P], xn[:, k * P:(k + 1) * P], ident[:])
                    last.then_inc(a_xTp.handle, 1)
                    pe.wait_ge(a_xT.handle, a_xT.at(b, t + 1))
                    for q, c0, c1 in ((1, 0, DI), (2, DI, 2 * DI), (3, 2 * DI, W_IN)):
                        for k in range(2):
                            last = pe.matmul(Q[q][:, 0:c1 - c0], xT[:, k, :], win_sb[:, k, c0:c1],
                                             start=(k == 0), stop=(k == 1))
                    last.then_inc(a_proj.handle, 1)
                    pe.wait_ge(a_seg.handle, a_seg.at(b, t + 1))
                    kinds = Q[0][:, 0:32].rearrange("p (g k h) -> p k g h", g=2, k=2)
                    both = dta[:]
                    pe.matmul(kinds[:, 0], tri[:], both, start=True, stop=True)
                    pe.matmul(kinds[:, 1], ones[:], both, start=True, stop=True)
                    pe.matmul(Q[0][:, 32:40], stri[:], dta[:, 1, :], start=True, stop=True).then_inc(a_sums.handle, 1)
                    pe.wait_ge(a_zx.handle, a_zx.at(b, t + 1))
                    for h in range(H):
                        q = Q[1 + h // 4]
                        if h % 4 == 0:
                            pe.matmul(q[:], far_i[:], past[:].rearrange("p h t -> p (h t)"), start=True, stop=False,
                                      skip_group_check=True)
                        o = (h % 4) * P
                        last = pe.matmul(q[:, o:o + P], seg[:, h, :], tri[:], start=False, stop=(h % 4 == 3),
                                         skip_group_check=True)
                    last.then_inc(a_segp.handle, 1)
                    pe.wait_ge(a_hat.handle, a_hat.at(b, t + 1))
                    pe.wait_ge(a_flat.handle, a_flat.at(b, t + 1))
                    for i, q in ((0, 3), (1, 0)):
                        for hp in range(4):
                            last = pe.transpose(Q[q][:, hp * P:(hp + 1) * P],
                                                hat[:, i, 2 * hp:2 * hp + 2, :].rearrange("p h n -> p (h n)"), ident[:])
                    last.then_inc(a_hatT.handle, 1)
                    pe.wait_ge(a_bT.handle, a_bT.at(b, t + 1))
                    pe.wait_ge(a_cT.handle, a_cT.at(b, t + 1))
                    for hp in range(4):
                        o = (hp % 2) * 2 * P
                        last = pe.matmul(Q[1 + hp // 2][:, o:o + 2 * P], bT[:, hp, :],
                                         cT[:, hp].rearrange("p e t -> p (e t)"), start=True, stop=True)
                    last.then_inc(a_score.handle, 1)
                    pe.wait_ge(a_pm.handle, a_pm.at(b, t + 1))
                    pe.wait_ge(a_wx.handle, a_wx.at(b, t + 1))
                    for h in range(H):
                        pe.matmul(Q[3][:, h * HP:(h + 1) * HP], dec[:, h, :], xdt[:, h, :], start=True, stop=True)
                    for h in range(H):
                        pe.matmul(Q[0][:, h * HP:(h + 1) * HP], cT[:, h // 2, h % 2, :], hst[:, h // 2, :],
                                  start=True, stop=True)
                    for h in range(H):
                        e, hp = h % 2, h // 2
                        last = pe.matmul(Q[1][64 * e:64 * e + 64, hp * HP:(hp + 1) * HP], hat[:, 0, h, :], wx[:, h, :],
                                         start=True, stop=True)
                    last.then_inc(a_y.handle, 1)
                    pe.wait_ge(a_yv.handle, a_yv.at(b, t + 1))
                    for k in range(4):
                        last = pe.transpose(Q[3][:, k * P:(k + 1) * P],
                                            y[:, 2 * k:2 * k + 2, :].rearrange("p h d -> p (h d)"), ident[:])
                    last.then_inc(a_yTp.handle, 1)
                    pe.wait_ge(a_yT.handle, a_yT.at(b, t + 1))
                    for k in range(4):
                        last = pe.matmul(Q[2][:, 0:D], yT[:, k, :], wout_sb[:, k, :], start=(k == 0), stop=(k == 3))
                    last.then_inc(a_out.handle, 1)
                pe.wait_ge(wr_dma, 16 * 5)
                ffn(b, 0)
                for t in range(NT):
                    pe.wait_ge(d_xn.handle, d_xn.at(b, t + 1))
                    for k in range(2):
                        last = pe.transpose(Q[0][:, k * P:(k + 1) * P], xnd[:, k * P:(k + 1) * P], ident[:])
                    last.then_inc(d_xTp.handle, 1)
                    pe.wait_ge(d_xT.handle, d_xT.at(b, t + 1))
                    for q, c0, c1 in ((1, 0, 2 * D), (2, 2 * D, W_QKVB)):
                        for k in range(2):
                            last = pe.matmul(Q[q][:, 0:c1 - c0], xTd[:, k, :], wqkvb_sb[:, k, c0:c1],
                                             start=(k == 0), stop=(k == 1))
                    last.then_inc(d_proj.handle, 1)
                    pe.wait_ge(d_kn.handle, d_kn.at(b, t + 1))
                    knf = kn[:, t].rearrange("p h d -> p (h d)")
                    for i, src in enumerate((q_sb[:], knf)):
                        for g in range(G):
                            o = (2 * i + g) * P
                            last = pe.transpose(Q[3][:, o:o + P], src[:, g * P:(g + 1) * P], ident[:])
                    last.then_inc(d_kqT.handle, 1)
                    pe.wait_ge(d_padA.handle, d_padA.at(b, t + 1))
                    pe.wait_ge(d_padV.handle, d_padV.at(b, t + 1))
                    for c in range(NB):
                        s = slice(BLK * c, BLK * (c + 1))
                        for g in range(G):
                            last = pe.matmul(Q[1][s, g * 256:(g + 1) * 256].rearrange("p (k i) -> p k i", k=8),
                                             kT[:, g, s], kqpad[:, g, :, :, s].rearrange("p k h i -> p (k h) i"),
                                             start=True, stop=True)
                    last.then_inc(d_gram.handle, 1)
                for t in range(NT):
                    pe.wait_ge(d_tbd.handle, d_tbd.at(b, (t + 1) * NB * 16))
                    if t:
                        pe.wait_ge(d_done.handle, d_done.at(b, t))
                    for h in range(DH):
                        last = pe.matmul(Q[1][:, h * 64:(h + 1) * 64], tbd[:, h, :],
                                         uw[:, t, h].rearrange("p k d -> p (k d)"), start=True, stop=True)
                    last.then_inc(d_uwp.handle, 1)
                    pe.wait_ge(d_uwc.handle, d_uwc.at(b, t + 1))
                    wf = w_sb[:].rearrange("p h d -> p (h d)")
                    for g in range(G):
                        last = pe.transpose(Q[1][:, g * P:(g + 1) * P], wf[:, g * P:(g + 1) * P], ident[:])
                    last.then_inc(d_wTp.handle, 1)
                    pe.wait_ge(d_wT.handle, d_wT.at(b, t + 1))
                    for c in range(NB):
                        n = t * NB + c
                        s = slice(BLK * c, BLK * (c + 1))
                        if n:
                            pe.wait_ge(d_s.handle, d_s.at(b, n))
                        for g in range(G):
                            last = pe.matmul(Q[0][s, g * P:(g + 1) * P], wT[:, g, s], sbd[:, g, :],
                                             start=True, stop=True)
                        last.then_inc(d_ws.handle, 1)
                        for g in range(G):
                            pe.matmul(Q[2][s, g * P:(g + 1) * P], qT[:, t, g, s], sbd[:, g, :],
                                      start=(g == 0), stop=False, skip_group_check=True)
                        pe.wait_ge(d_u.handle, d_u.at(b, n + 1))
                        for g in range(G):
                            last = pe.matmul(Q[3][:, g * P:(g + 1) * P],
                                             kn[s, t].rearrange("p h d -> p (h d)")[:, g * P:(g + 1) * P],
                                             u_sb[s].rearrange("p h d -> p (h d)")[:, g * P:(g + 1) * P],
                                             start=(n == 0 and g == 0), stop=(n == NT * NB - 1),
                                             skip_group_check=True)
                        last.then_inc(d_sp.handle, 1)
                    pe.wait_ge(d_pbd.handle, d_pbd.at(b, t + 1))
                    for h in range(DH):
                        last = pe.matmul(Q[2][:, h * HD:(h + 1) * HD], pbd[:, h, :], u_sb[:, h, :],
                                         start=False, stop=True, skip_group_check=True)
                    last.then_inc(d_o.handle, 1)
                ffn(b, 1)


def kernel(**inputs):
    import numpy as np
    import concourse.bacc as bacc
    from concourse.bass_utils import run_bass_kernel_spmd

    a = {k: np.asarray(v) for k, v in inputs.items()}

    def flat(v):
        return np.ascontiguousarray(v)

    def column(v, k):
        return flat(v.reshape(k, P).T)

    arrays = {
        "x": flat(a["L0_attn_a_x"].reshape(B * L, D)),
        "w_in": flat(a["L0_attn_a_W_in"]),
        "w_out": flat(a["L0_attn_a_W_out"]),
        "dt_bias": flat(a["L0_attn_a_dt_bias"]),
        "a_log": flat(a["L0_attn_a_A_log"]),
        "d_skip": flat(a["L0_attn_a_D_skip"]),
        "norm_w": column(a["L0_attn_a_norm_weight"], 4),
        "wqkvb": flat(np.concatenate([a["L0_attn_b_Wq"], a["L0_attn_b_Wk"], a["L0_attn_b_Wv"], a["L0_attn_b_Wb"]], 1)),
        "ln_w": flat(a["L0_attn_b_ln_w"]),
        "ln_b": flat(a["L0_attn_b_ln_b"]),
        "w1": flat(a["L0_ffn_w1_w"].T),
        "w1s": column(a["L0_ffn_w1_s"], KT),
        "w2": flat(a["L0_ffn_w2_w"].T),
        "w2s": column(a["L0_ffn_w2_s"], KT),
        "h1": flat(a["L0_ffn_h1_w"].T),
        "h1s": column(a["L0_ffn_h1_s"], KT),
        "h2": flat(a["L0_ffn_h2_w"].T),
        "h2s": column(a["L0_ffn_h2_s"], KT),
        "w3": flat(a["L0_ffn_w3_w"].T),
        "w3s": flat(a["L0_ffn_w3_s"]),
    }
    nc = bacc.Bacc("TRN2", target_bir_lowering=False, num_devices=1)
    args = [nc.dram_tensor(f"{k}_dram", v.shape, F32, kind="ExternalInput").ap() for k, v in arrays.items()]
    a_scr = nc.dram_tensor("a_scr", (NT, NB, DH, BLK, BLK), F32, kind="Internal").ap()
    t_scr = nc.dram_tensor("t_scr", (NT, NB, DH, BLK, BLK), F32, kind="Internal").ap()
    out = nc.dram_tensor("out_dram", (B * L, D), F32, kind="ExternalOutput").ap()
    hybrid_kernel(nc, *args, a_scr, t_scr, out)
    r = run_bass_kernel_spmd(nc, [{f"{k}_dram": v for k, v in arrays.items()}], core_ids=[0])
    return r.results[0]["out_dram"].reshape(B, L, D)
```

```python
from contextlib import ExitStack

import concourse.bass as bass
from concourse import mybir

F32 = mybir.dt.float32
F32R = mybir.dt.float32r
BF16 = mybir.dt.bfloat16
ALU = mybir.AluOpType
ACT = mybir.ActivationFunctionType
AX = mybir.AxisListType

P = 128
B, L, D = 8, 512, 256
NT = L // P
SLOTS = 3
EPS = 1e-5
H, HP, N = 8, 64, 64
DI = H * HP
PAIRS = 16
W_IN = 2 * DI + 2 * N + H
DH, HD = 8, 32
BLK = 32
NB = P // BLK
G = 2
W_QKVB = 3 * D + DH
HID = 1024
KT = HID // P
TOK = 256
UNITS = L // TOK
SLICES = 1 + KT + KT // 2 + KT // 2 + 1
HSLICES = KT + KT // 2 + KT // 2

SSM_STEPS = 8
SSM_PLAN = [1, 2, 3, 1, 1, 1, 0, 0] * NT
D1_STEPS, SUB_STEPS, D2_STEPS = 5, 16, 3 + 2 * NB
SUB0 = D1_STEPS * NT
D20 = SUB0 + SUB_STEPS
DELTA_PLAN = [1, 1, 0, 0, 0] * NT + [1] * SUB_STEPS + [1, 1, 0, 0, 0, 0, 1, 0, 0, 0, 0] * NT
assert sum(SSM_PLAN) == sum(DELTA_PLAN) == UNITS * SLICES

PI = 3.141592653589793
TWO_PI_HI = 6.28125
TWO_PI_LO = 2 * PI - TWO_PI_HI
MAGIC = 1.5 * 2.0 ** 23
PI_SAFE = 3.1415925
FAR = 30000.0


class Signal:

    def __init__(self, handle, per_batch, credit=0):
        self.handle, self.per_batch, self.credit = handle, per_batch, credit

    def at(self, b, n):
        return b * self.per_batch + (n + self.credit)


class Own:

    def __init__(self, eng, sem):
        self.eng, self.sem, self.n = eng, sem, 0

    def restart(self):
        self.eng.sem_clear(self.sem)
        self.n = 0

    def __call__(self, ins):
        self.n += 1
        ins.then_inc(self.sem, 1)
        self.eng.wait_ge(self.sem, self.n)


class Steps:

    def __init__(self, steps):
        self.steps = steps
        self.next = next(steps, None)

    def upto(self, n):
        while self.next is not None and self.next <= n:
            self.next = next(self.steps, None)


def window(attention, ffn, plan):
    att, mlp, done = Steps(attention), Steps(ffn), 0
    for step, slices in enumerate(plan):
        att.upto(step)
        done += slices
        mlp.upto(done - 1)


def alone(stage):
    for _ in stage:
        pass


def bcast(ap, axis, n):
    shape = list(ap.unsqueeze(axis).shape)
    shape[axis] = n
    return ap.unsqueeze(axis).broadcast_to(shape)


def hybrid_kernel(nc, x_in, w_in, w_out, dt_bias, a_log, d_skip, norm_w, wqkvb, ln_w, ln_b,
                  w1, w1s, w2, w2s, h1, h1s, h2, h2s, w3, w3s, a_scr, t_scr, out):
    with ExitStack() as ctx:
        def sb(name, shape, dt=F32):
            return ctx.enter_context(nc.sbuf_tensor(name, shape, dt))

        def sem(name):
            return ctx.enter_context(nc.semaphore(name))

        w1_sb = sb("w1_sb", [P, 2, HID], F32R)
        w2_sb = sb("w2_sb", [P, 2, HID], F32R)
        h1_sb = sb("h1_sb", [P, KT, HID], F32R)
        h2_sb = sb("h2_sb", [P, KT, HID], F32R)
        w3_sb = sb("w3_sb", [P, KT, D], F32R)
        win_sb = sb("win_sb", [P, 2, W_IN])
        wout_sb = sb("wout_sb", [P, 4, D])
        wqkvb_sb = sb("wqkvb_sb", [P, 2, W_QKVB])
        s1_sb = sb("s1_sb", [P, KT])
        s2_sb = sb("s2_sb", [P, KT])
        sh1_sb = sb("sh1_sb", [P, KT])
        sh2_sb = sb("sh2_sb", [P, KT])
        nw_sb = sb("nw_sb", [P, 4])
        w3s_row = sb("w3s_row", [P, D])
        lnw_row = sb("lnw_row", [P, D])
        lnb_row = sb("lnb_row", [P, D])
        bias_row = sb("bias_row", [P, H])
        a_row = sb("a_row", [P, H])
        d_row = sb("d_row", [P, H])
        ident = sb("ident", [P, P])
        ones = sb("ones", [P, P])
        tri = sb("tri", [P, P])
        stri = sb("stri", [P, P])
        far_i = sb("far_i", [P, P], BF16)
        past = sb("past", [P, 4, P], BF16)
        freq = sb("freq", [P, PAIRS])
        half_pi = sb("half_pi", [P, 1])
        neg_half = sb("neg_half", [P, 8])
        pool_pad = sb("pool_pad", [P, 1])
        smask = sb("smask", [P, BLK])
        umask = sb("umask", [P, BLK])
        bdmask = sb("bdmask", [P, 4])
        x_sb = sb("x_sb", [P, SLOTS, NT, D])
        bst = sb("bst", [P, NT, 6])
        mv = sb("mv", [P, NT, 2])
        ve = sb("ve", [P, NT])
        rstd = sb("rstd", [P, NT])
        fbst = sb("fbst", [P, 2, 6])
        fmv = sb("fmv", [P, NT, 2])
        fve = sb("fve", [P, NT])
        frstd = sb("frstd", [P, NT])
        xf_hi = sb("xf_hi", [P, 2, 2, P], F32R)
        xf_lo = sb("xf_lo", [P, 2, 2, P], F32R)
        hA_hi = sb("hA_hi", [P, KT, TOK], F32R)
        hA_lo = sb("hA_lo", [P, KT, TOK], F32R)
        hB_hi = sb("hB_hi", [P, KT, TOK], F32R)
        hB_lo = sb("hB_lo", [P, KT, TOK], F32R)
        hid = sb("hid", [P, 2, 2, TOK])
        gate = sb("gate", [P, 2, TOK])
        xnf = sb("xnf", [P, 2, D])

        with ExitStack() as ssm:
            def sa(name, shape, dt=F32):
                return ssm.enter_context(nc.sbuf_tensor(name, shape, dt))
            xn = sa("xn", [P, D])
            xT = sa("xT", [P, 2, P])
            sz = sa("sz", [P, DI])
            xs = sa("xs", [P, H, HP])
            bc = sa("bc", [P, 2, N])
            dtv = sa("dtv", [P, H])
            dtab = sa("dtab", [P, H])
            dte = sa("dte", [P, H])
            dtl = sa("dtl", [P, H])
            dta = sa("dta", [P, 2, H])
            seg = sa("seg", [P, H, P])
            sums = sa("sums", [P, 40])
            decays = sa("decays", [P, 3, H])
            phase = sa("phase", [P, H, PAIRS])
            ang = sa("ang", [P, 2, H, PAIRS])
            angk = sa("angk", [P, 2, H, PAIRS])
            angr = sa("angr", [P, H, PAIRS])
            anga = sa("anga", [P, H, PAIRS])
            cosT = sa("cosT", [P, H, PAIRS])
            sinT = sa("sinT", [P, H, PAIRS])
            hat = sa("hat", [P, 2, H, N])
            bT = sa("bT", [P, 4, P])
            cT = sa("cT", [P, 4, 2, P])
            xdt = sa("xdt", [P, H, HP])
            wrow = sa("wrow", [P, H])
            wx = sa("wx", [P, H, HP])
            xD = sa("xD", [P, H, HP])
            y = sa("y", [P, H, HP])
            yT = sa("yT", [P, 4, P])
            yss = sa("yss", [P, 1])
            yve = sa("yve", [P, 1])
            yrstd = sa("yrstd", [P, 1])
            r1, r2 = [y[:].rearrange("p h d -> p (h d)")[:, i * D:(i + 1) * D].rearrange(
                "p (k h n) -> p k h n", k=2, h=H) for i in range(2)]
            r3, r4 = [yT[:].rearrange("p k n -> p (k n)")[:, i * D:(i + 1) * D].rearrange(
                "p (k h n) -> p k h n", k=2, h=H) for i in range(2)]
            hst = sa("hst", [P, 4, HP])
        with ExitStack() as dl:
            def sd(name, shape, dt=F32):
                return dl.enter_context(nc.sbuf_tensor(name, shape, dt))
            xnd = sd("xnd", [P, D])
            xTd = sd("xTd", [P, 2, P])
            uw = sd("uw", [P, NT, DH, 2, HD])
            pc = sd("pc", [P, NT, DH, BLK])
            qT = sd("qT", [P, NT, G, P])
            kn = sd("kn", [P, NT, DH, HD])
            ti = sd("ti", [P, BLK, BLK])
            srow = sd("srow", [P, DH])
            rn = sd("rn", [P, DH])
            be = sd("be", [P, DH])
            be1 = sd("be1", [P, DH])
            beta = sd("beta", [P, DH])
            dbst = sd("dbst", [P, 6])
            dmv = sd("dmv", [P, 2])
            dve_ = sd("dve_", [P, 1])
            drs = sd("drs", [P, 1])
            with ExitStack() as d1:
                def s1_(name, shape):
                    return d1.enter_context(nc.sbuf_tensor(name, shape, F32))
                q_sb = s1_("q_sb", [P, D])
                k_sb = s1_("k_sb", [P, DH, HD])
                v_sb = s1_("v_sb", [P, DH, HD])
                ksq = s1_("ksq", [P, DH, HD])
                kT = s1_("kT", [P, G, P])
                kqpad = s1_("kqpad", [P, 2, 4, P])
                bmask = ksq
                amv = q_sb[:].rearrange("p (h i) -> p h i", h=DH)
            with ExitStack() as d2:
                def s2_(name, shape):
                    return d2.enter_context(nc.sbuf_tensor(name, shape, F32))
                au = s2_("au", [P, BLK, BLK])
                prod = s2_("prod", [P, BLK * BLK])
            with ExitStack() as d3:
                def s3_(name, shape):
                    return d3.enter_context(nc.sbuf_tensor(name, shape, F32))
                tbd = s3_("tbd", [P, DH, P])
                pbd = s3_("pbd", [P, DH, P])
                u_sb = s3_("u_sb", [P, DH, HD])
                w_sb = s3_("w_sb", [P, DH, HD])
                wT = s3_("wT", [P, G, P])
                sbd = xTd
                on = xnd

        F = [ctx.enter_context(nc.psum_tensor(f"F{i}", [P, 512], F32)) for i in range(4)]
        Q = [ctx.enter_context(nc.psum_tensor(f"Q{i}", [P, 512], F32)) for i in range(4)]

        w_dma = sem("w_dma")
        wr_dma = sem("wr_dma")
        dve_own, act_own, pool_own = sem("dve_own"), sem("act_own"), sem("pool_own")
        pool_gate = sem("pool_gate")
        const_done = sem("const_done")
        wout_done = sem("wout_done")
        arow_done = sem("arow_done")
        x_loaded = Signal(sem("x_loaded"), 16)
        x_stored = Signal(sem("x_stored"), 16, 16)
        x_final = Signal(sem("x_final"), 1)
        a_stats, a_rstd = Signal(sem("a_stats"), 1), Signal(sem("a_rstd"), 1)
        d_stats, d_rstd = Signal(sem("d_stats"), 1), Signal(sem("d_rstd"), 1)
        f_stats, f_rstd = Signal(sem("f_stats"), UNITS), Signal(sem("f_rstd"), UNITS)
        a_xn = Signal(sem("a_xn"), NT)
        a_xTp = Signal(sem("a_xTp"), NT)
        a_xT = Signal(sem("a_xT"), NT)
        a_proj = Signal(sem("a_proj"), NT)
        a_dtv = Signal(sem("a_dtv"), NT)
        a_soft = Signal(sem("a_soft"), NT)
        a_zx = Signal(sem("a_zx"), NT)
        a_seg = Signal(sem("a_seg"), NT)
        a_sums = Signal(sem("a_sums"), NT)
        a_segp = Signal(sem("a_segp"), NT)
        a_sumc = Signal(sem("a_sumc"), NT)
        a_dec = Signal(sem("a_dec"), NT)
        a_ang = Signal(sem("a_ang"), NT)
        a_trig = Signal(sem("a_trig"), NT)
        a_exp = Signal(sem("a_exp"), NT)
        a_flat = Signal(sem("a_flat"), NT)
        a_hat = Signal(sem("a_hat"), NT)
        a_hatT = Signal(sem("a_hatT"), NT)
        a_bT = Signal(sem("a_bT"), NT)
        a_cT = Signal(sem("a_cT"), NT)
        a_score = Signal(sem("a_score"), NT)
        a_pm = Signal(sem("a_pm"), NT)
        a_wx = Signal(sem("a_wx"), NT)
        a_y = Signal(sem("a_y"), NT)
        a_yv = Signal(sem("a_yv"), NT)
        a_ysq = Signal(sem("a_ysq"), NT)
        a_yr = Signal(sem("a_yr"), NT)
        a_yTp = Signal(sem("a_yTp"), NT)
        a_yT = Signal(sem("a_yT"), NT)
        a_out = Signal(sem("a_out"), NT)
        a_res = Signal(sem("a_res"), NT)
        a_clear = Signal(sem("a_clear"), 1)
        f_xn = Signal(sem("f_xn"), UNITS)
        f_ps = Signal(sem("f_ps"), UNITS * SLICES)
        f_free = Signal(sem("f_free"), UNITS * SLICES, 4)
        f_xhi = Signal(sem("f_xhi"), UNITS)
        f_xlo = Signal(sem("f_xlo"), UNITS)
        f_act = Signal(sem("f_act"), UNITS * HSLICES)
        f_hi = Signal(sem("f_hi"), UNITS * HSLICES)
        f_lo = Signal(sem("f_lo"), UNITS * HSLICES, 2)
        d_clear = Signal(sem("d_clear"), 2)
        d_xn = Signal(sem("d_xn"), NT)
        d_xTp = Signal(sem("d_xTp"), NT)
        d_xT = Signal(sem("d_xT"), NT)
        d_proj = Signal(sem("d_proj"), NT)
        d_q = Signal(sem("d_q"), NT)
        d_qkv = Signal(sem("d_qkv"), NT)
        d_ss = Signal(sem("d_ss"), NT)
        d_rn = Signal(sem("d_rn"), NT)
        d_kn = Signal(sem("d_kn"), NT)
        d_beta = Signal(sem("d_beta"), NT)
        d_bm = Signal(sem("d_bm"), NT)
        d_kqT = Signal(sem("d_kqT"), NT)
        d_kqc = Signal(sem("d_kqc"), NT)
        d_padA = Signal(sem("d_padA"), NT)
        d_padV = Signal(sem("d_padV"), NT)
        d_pad2A = Signal(sem("d_pad2A"), NT)
        d_pad2V = Signal(sem("d_pad2V"), NT)
        d_gram = Signal(sem("d_gram"), 2 * NT)
        d_am = Signal(sem("d_am"), NT)
        d_pc = Signal(sem("d_pc"), NT)
        d_ast = Signal(sem("d_ast"), NT * NB * 16)
        d_aun = Signal(sem("d_aun"), 16)
        d_inv = Signal(sem("d_inv"), 1)
        d_tst = Signal(sem("d_tst"), 16)
        d_tbd = Signal(sem("d_tbd"), NT * NB * 16)
        d_pbd = Signal(sem("d_pbd"), NT)
        d_uwp = Signal(sem("d_uwp"), NT)
        d_uwc = Signal(sem("d_uwc"), NT)
        d_wTp = Signal(sem("d_wTp"), NT)
        d_wT = Signal(sem("d_wT"), NT)
        d_ws = Signal(sem("d_ws"), NT * NB)
        d_u = Signal(sem("d_u"), NT * NB)
        d_sp = Signal(sem("d_sp"), NT * NB)
        d_s = Signal(sem("d_s"), NT * NB)
        d_o = Signal(sem("d_o"), NT)
        d_ost = Signal(sem("d_ost"), NT)
        d_ors = Signal(sem("d_ors"), NT)
        d_done = Signal(sem("d_done"), NT)

        x_v = x_in.rearrange("(b t p) d -> p b t d", p=P, t=NT)
        o_v = out.rearrange("(b t p) d -> p b t d", p=P, t=NT)
        a_store = a_scr.rearrange("t c h i j -> t c i h j")
        a_load = a_scr.rearrange("t c h i j -> (t c h) (i j)")
        t_store = t_scr.rearrange("t c h j i -> (t c h) (j i)")
        t_load = t_scr.rearrange("t c h j i -> t c j h i")

        block = ctx.enter_context(nc.Block())

        def ffn_dst(j):
            if j < KT:
                return hA_hi[:, j:j + 1, :], hA_lo[:, j:j + 1, :], 1
            if j < KT + KT // 2:
                k = 2 * (j - KT)
                return hB_hi[:, k:k + 2, :], hB_lo[:, k:k + 2, :], 2
            k = 2 * (j - KT - KT // 2)
            return hA_hi[:, k:k + 2, :], hA_lo[:, k:k + 2, :], 2

        def ffn_slice(j):
            return 1 + j


        @block.sync
        def _(sp):
            sp.dma_start(win_sb[:], w_in.rearrange("(k p) n -> p k n", p=P)).then_inc(w_dma, 16)
            sp.dma_start(wout_sb[:], w_out.rearrange("(k p) n -> p k n", p=P)).then_inc(w_dma, 16)
            sp.dma_start(wqkvb_sb[:], wqkvb.rearrange("(k p) n -> p k n", p=P)).then_inc(w_dma, 16)
            for dst, src in ((s1_sb, w1s), (s2_sb, w2s), (sh1_sb, h1s), (sh2_sb, h2s), (nw_sb, norm_w)):
                sp.dma_start(dst[:], src).then_inc(w_dma, 16)
            for dst, src in ((w3s_row, w3s), (lnw_row, ln_w), (lnb_row, ln_b), (bias_row, dt_bias),
                             (a_row, a_log), (d_row, d_skip)):
                sp.dma_start(dst[:], src.partition_broadcast(P)).then_inc(w_dma, 16)

            def x_dram(ap, b):
                return ap[:, b] if isinstance(b, int) else ap[:, bass.ds(b, 1)].squeeze(1)

            def x_slot(b):
                return x_sb[:, b % SLOTS] if isinstance(b, int) else x_sb[:, bass.ds(sp.snap(b % SLOTS), 1)].squeeze(1)

            def load(b):
                sp.dma_start(x_slot(b), x_dram(x_v, b)).then_inc(x_loaded.handle, 16)

            def store(b):
                sp.wait_ge(x_final.handle, x_final.at(b, 1))
                sp.dma_start(x_dram(o_v, b), x_slot(b)).then_inc(x_stored.handle, 16)

            def delta(b):
                for t in range(NT):
                    sp.wait_ge(d_am.handle, d_am.at(b, t + 1))
                    for c in range(NB):
                        sp.dma_start(a_store[t, c], amv[BLK * c:BLK * (c + 1)]).then_inc(d_ast.handle, 16)
                sp.wait_ge(d_ast.handle, d_ast.at(b, NT * NB * 16))
                sp.dma_start(au[:].rearrange("p i j -> p (i j)"), a_load).then_inc(d_aun.handle, 16)
                sp.wait_ge(d_inv.handle, d_inv.at(b, 1))
                sp.dma_start(t_store, ti[:].rearrange("p j i -> p (j i)")).then_inc(d_tst.handle, 16)
                sp.wait_ge(d_tst.handle, d_tst.at(b, 16))
                sp.wait_ge(d_clear.handle, d_clear.at(b, 2))
                for t in range(NT):
                    if t:
                        sp.wait_ge(d_uwp.handle, d_uwp.at(b, t))
                    for c in range(NB):
                        sp.dma_start(tbd[BLK * c:BLK * (c + 1), :, BLK * c:BLK * (c + 1)],
                                     t_load[t, c]).then_inc(d_tbd.handle, 16)

            load(0)
            sp.wait_ge(x_loaded.handle, 16)
            load(1)
            with sp.Fori(1, B - 1) as b:
                sp.wait_ge(x_loaded.handle, x_loaded.at(b, 16))
                sp.wait_ge(x_stored.handle, x_stored.at(b - 2, 16))
                load(b + 1)
                delta(b - 1)
                store(b - 1)
            delta(B - 2)
            delta(B - 1)
            store(B - 2)
            store(B - 1)
            sp.wait_ge(x_stored.handle, x_stored.credit + 16 * B)

        @block.gpsimd
        def _(pool):
            own = Own(pool, pool_own)
            pool.sem_inc(x_stored.handle, x_stored.credit)
            pool.sem_inc(f_free.handle, f_free.credit)
            pool.sem_inc(f_lo.handle, f_lo.credit)
            for dst, src in ((w1_sb, w1), (w2_sb, w2), (h1_sb, h1), (h2_sb, h2), (w3_sb, w3)):
                pool.dma_start(dst[:], src.rearrange("(k p) o -> p k o", p=P)).then_inc(wr_dma, 16)

            def select(out_, in_, pattern, op, fill, mult, base=0):
                own(pool.affine_select(out=out_, in_=in_, pattern=pattern, compare_op=op, fill=fill,
                                       base=base, channel_multiplier=mult))

            own(pool.memset(ones[:], 1.0))
            own(pool.memset(far_i[:], FAR))
            own(pool.memset(past[:], 1.0))
            own(pool.memset(half_pi[:], PI / 2))
            own(pool.memset(neg_half[:], -0.5))
            own(pool.memset(bdmask[:], 1.0))
            for i in range(PAIRS):
                own(pool.memset(freq[:, i:i + 1], float(1.0 / 10000.0 ** (i / PAIRS))))
            select(ident[:], ones[:], [[-1, P]], ALU.is_equal, 0.0, 1)
            select(far_i[:], far_i[:], [[-1, P]], ALU.is_equal, 0.0, 1)
            select(tri[:], ones[:], [[1, P]], ALU.is_ge, 0.0, -1)
            select(stri[:], ones[:], [[-1, P]], ALU.is_gt, 0.0, 1)
            select(past[:], past[:], [[0, 4], [-1, P]], ALU.is_gt, 0.0, 1)
            for c in range(NB):
                s = slice(BLK * c, BLK * (c + 1))
                select(smask[s], ones[s, 0:BLK], [[-1, BLK]], ALU.is_gt, 0.0, 1)
                select(umask[s], ones[s, 0:BLK], [[1, BLK]], ALU.is_ge, 0.0, -1)
                select(bdmask[s], bdmask[s], [[1, 4]], ALU.is_equal, 0.0, 0, base=-c)
            pool.sem_inc(const_done, 1)

            def rsqrt(ready, value, dst, var, src, done):
                pool.wait_ge(ready.handle, value)
                pool.sem_inc(pool_gate, 1)
                own(pool.tensor_scalar(var, src, EPS, None, ALU.add))
                pool.tensor_tensor(dst, var, neg_half[:, 0:dst.shape[1]], ALU.pow).then_inc(done.handle, 1)

            def rsqrt_ffn(p, u):
                s = slice(2 * u, 2 * u + 2)
                rsqrt(f_stats, f_stats.at(p, u + 1), frstd[:, s], fve[:, s], fmv[:, s, 1], f_rstd)

            def ffn(p, b, final):
                for u in range(UNITS):
                    for j in range(HSLICES):
                        yield u * SLICES + ffn_slice(j)
                        n = u * HSLICES + j
                        pool.wait_ge(f_hi.handle, f_hi.at(p, n + 1))
                        hi, lo, w = ffn_dst(j)
                        pool.tensor_tensor(lo, hid[:, n % 2, 0:w, :], hi.bitcast(F32),
                                           ALU.subtract).then_inc(f_lo.handle, 1)

            def ssm_stage(b, p):
                yield 0
                own(pool.memset(cT[:], 0.0))
                own(pool.memset(hst[:], 0.0))
                own(pool.memset(phase[:], 0.0))
                pool.sem_inc(a_clear.handle, 1)
                rsqrt(a_stats, a_stats.at(b, 1), rstd[:], ve[:], mv[:, :, 1], a_rstd)
                for t in range(NT):
                    yield SSM_STEPS * t + 2
                    pool.wait_ge(a_zx.handle, a_zx.at(b, t + 1))
                    pool.wait_ge(a_sumc.handle, a_sumc.at(b, t + 1))
                    pool.tensor_tensor(xdt[:], xs[:], bcast(dta[:, 0, :], 2, HP), ALU.mult)
                    pool.tensor_tensor(xD[:], xs[:], bcast(d_row[:], 2, HP), ALU.mult)
                    pool.wait_ge(a_dec.handle, a_dec.at(b, t + 1))
                    own(pool.tensor_tensor(wrow[:], decays[:, 2, :], dta[:, 0, :], ALU.mult))
                    pool.tensor_tensor(wx[:], xs[:], bcast(wrow[:], 2, HP), ALU.mult).then_inc(a_wx.handle, 1)
                    yield SSM_STEPS * t + 5
                    pool.wait_ge(a_ysq.handle, a_ysq.at(b, t + 1))
                    pool.sem_inc(pool_gate, 1)
                    own(pool.tensor_scalar(yve[:], yss[:], 1.0 / DI, EPS, ALU.mult, ALU.add))
                    pool.tensor_tensor(yrstd[:], yve[:], neg_half[:, 0:1], ALU.pow).then_inc(a_yr.handle, 1)
                    yield SSM_STEPS * t + 7
                    if t % 2:
                        rsqrt_ffn(p, t // 2)

            def delta_stage(b, p):
                yield 0
                own(pool.memset(kqpad[:], 0.0))
                own(pool.memset(ti[:], 0.0))
                own(pool.affine_select(out=ti[:], in_=ti[:], pattern=[[1, BLK], [-1, BLK]],
                                       compare_op=ALU.not_equal, fill=1.0, base=0, channel_multiplier=0))
                pool.sem_inc(d_clear.handle, 1)
                rsqrt(d_stats, d_stats.at(b, 1), rstd[:], ve[:], mv[:, :, 1], d_rstd)
                for t in range(NT):
                    yield D1_STEPS * t + 1
                    pool.wait_ge(d_ss.handle, d_ss.at(b, t + 1))
                    pool.tensor_tensor(rn[:], srow[:], neg_half[:], ALU.pow).then_inc(d_rn.handle, 1)
                    pool.wait_ge(d_beta.handle, d_beta.at(b, t + 1))
                    pool.tensor_tensor(bmask[:], bcast(smask[:], 1, DH), bcast(beta[:], 2, BLK),
                                       ALU.mult).then_inc(d_bm.handle, 1)
                yield D20 - 1
                pool.wait_ge(d_inv.handle, d_inv.at(b, 1))
                pool.sem_inc(pool_gate, 1)
                own(pool.memset(tbd[:], 0.0))
                own(pool.memset(sbd[:], 0.0))
                own(pool.memset(pbd[:], 0.0))
                pool.sem_inc(d_clear.handle, 1)
                for t in range(NT):
                    yield D20 + D2_STEPS * t + 1
                    if t:
                        pool.wait_ge(d_o.handle, d_o.at(b, t))
                        pool.sem_inc(pool_gate, 1)
                    own(pool.memset(pool_pad[:], 0.0))
                    for c in range(NB):
                        s = slice(BLK * c, BLK * (c + 1))
                        own(pool.tensor_copy(pbd[s, :, s], pc[s, t]))
                    pool.sem_inc(d_pbd.handle, 1)
                    yield D20 + D2_STEPS * t + D2_STEPS - 1
                    rsqrt(d_ost, d_ost.at(b, t + 1), drs[:], dve_[:], dmv[:, 1:2], d_ors)
                    if t % 2:
                        rsqrt_ffn(p, t // 2)

            own.restart()
            alone(ssm_stage(0, 0))
            window(ssm_stage(1, 1), ffn(0, 0, False), SSM_PLAN)
            with pool.Fori(1, B - 1) as b:
                own.restart()
                window(delta_stage(b - 1, 2 * b), ffn(2 * b - 1, b, False), DELTA_PLAN)
                window(ssm_stage(b + 1, 2 * b + 1), ffn(2 * b, b - 1, True), SSM_PLAN)
            own.restart()
            window(delta_stage(B - 2, 2 * B - 2), ffn(2 * B - 3, B - 1, False), DELTA_PLAN)
            window(delta_stage(B - 1, 2 * B - 1), ffn(2 * B - 2, B - 2, True), DELTA_PLAN)
            alone(ffn(2 * B - 1, B - 1, True))

        @block.scalar
        def _(act):
            own = Own(act, act_own)
            act.wait_ge(w_dma, 16 * 14)
            act.activation(a_row[:], a_row[:], ACT.Exp).then_inc(arow_done, 1)
            act.wait_ge(const_done, 1)

            def ffn(p, b, final):
                for u in range(UNITS):
                    s0 = u * SLICES
                    yield s0
                    act.wait_ge(f_ps.handle, f_ps.at(p, s0 + 1))
                    act.copy(xf_hi[:].rearrange("p t k n -> p (t k n)"), F[s0 % 4][:]).then_inc(f_xhi.handle, 1)
                    for j in range(HSLICES):
                        n = u * HSLICES + j
                        s = s0 + ffn_slice(j)
                        yield s
                        act.wait_ge(f_ps.handle, f_ps.at(p, s + 1))
                        act.wait_ge(f_lo.handle, f_lo.at(p, n - 1))
                        ps = F[s % 4]
                        if j < KT:
                            act.activation(gate[:, n % 2, :], ps[:, 0:TOK], ACT.Silu,
                                           scale=s1_sb[:, j:j + 1]).then_inc(f_act.handle, 1)
                            continue
                        scales, k = (sh1_sb, 2 * (j - KT)) if j < KT + KT // 2 else (sh2_sb, 2 * (j - KT - KT // 2))
                        act.activation(hid[:, n % 2, 0, :], ps[:, 0:TOK], ACT.Gelu, scale=scales[:, k:k + 1])
                        act.activation(hid[:, n % 2, 1, :], ps[:, TOK:2 * TOK], ACT.Gelu,
                                       scale=scales[:, k + 1:k + 2]).then_inc(f_act.handle, 1)

            def ssm_stage(b, p):
                for t in range(NT):
                    yield SSM_STEPS * t
                    act.wait_ge(a_xTp.handle, a_xTp.at(b, t + 1))
                    act.copy(xT[:].rearrange("p k n -> p (k n)"), Q[0][:, 0:D]).then_inc(a_xT.handle, 1)
                    yield SSM_STEPS * t + 1
                    act.wait_ge(a_dtv.handle, a_dtv.at(b, t + 1))
                    own(act.activation(dtab[:], dtv[:], ACT.Abs))
                    own(act.activation(dte[:], dtab[:], ACT.Exp, scale=-1.0))
                    act.activation(dtl[:], dte[:], ACT.Ln, bias=1.0).then_inc(a_soft.handle, 1)
                    act.copy(bc[:].rearrange("p k n -> p (k n)"), Q[3][:, 0:2 * N])
                    act.copy(xs[:].rearrange("p k n -> p (k n)"), Q[2][:])
                    own(act.activation(sz[:], Q[1][:], ACT.Silu))
                    act.sem_inc(a_zx.handle, 1)
                    act.copy(hat[:, :, :, 2 * PAIRS:N], bcast(bc[:, :, 2 * PAIRS:N], 2, H)).then_inc(a_flat.handle, 1)
                    yield SSM_STEPS * t + 2
                    act.wait_ge(a_ang.handle, a_ang.at(b, t + 1))
                    own(act.activation(anga[:], angr[:], ACT.Abs))
                    act.activation(sinT[:], angr[:], ACT.Sin)
                    act.activation(cosT[:], anga[:], ACT.Sin, scale=-1.0, bias=half_pi[:]).then_inc(a_trig.handle, 1)
                    act.activation(decays[:].rearrange("p k h -> p (k h)"), sums[:, 16:40], ACT.Exp,
                                   scale=-1.0).then_inc(a_dec.handle, 1)
                    act.wait_ge(a_segp.handle, a_segp.at(b, t + 1))
                    act.activation(seg[:, 0:4, :].rearrange("p h t -> p (h t)"), Q[1][:], ACT.Exp, scale=-1.0)
                    act.activation(seg[:, 4:8, :].rearrange("p h t -> p (h t)"), Q[2][:], ACT.Exp,
                                   scale=-1.0).then_inc(a_exp.handle, 1)
                    yield SSM_STEPS * t + 3
                    act.wait_ge(a_hatT.handle, a_hatT.at(b, t + 1))
                    act.copy(bT[:].rearrange("p k n -> p (k n)"), Q[3][:]).then_inc(a_bT.handle, 1)
                    yield SSM_STEPS * t + 5
                    act.wait_ge(a_yv.handle, a_yv.at(b, t + 1))
                    act.activation(yT[:].rearrange("p k n -> p (k n)"), y[:].rearrange("p h d -> p (h d)"),
                                   ACT.Square, accum_out=yss[:]).then_inc(a_ysq.handle, 1)
                    yield SSM_STEPS * t + 6
                    act.wait_ge(a_ysq.handle, a_ysq.at(b, t + 1))
                    act.wait_ge(a_yTp.handle, a_yTp.at(b, t + 1))
                    act.copy(yT[:].rearrange("p k n -> p (k n)"), Q[3][:]).then_inc(a_yT.handle, 1)

            def pads(g, t):
                for h in range(2):
                    s = slice(HD * h, HD * (h + 1))
                    act.copy(kqpad[s, 0, h, :], kT[s, g])
                    last = act.copy(kqpad[s, 1, h, :], qT[s, t, g])
                return last

            def delta_stage(b, p):
                for t in range(NT):
                    yield D1_STEPS * t
                    act.wait_ge(d_xTp.handle, d_xTp.at(b, t + 1))
                    act.copy(xTd[:].rearrange("p k n -> p (k n)"), Q[0][:, 0:D]).then_inc(d_xT.handle, 1)
                    yield D1_STEPS * t + 1
                    act.wait_ge(d_proj.handle, d_proj.at(b, t + 1))
                    act.activation(ksq[:].rearrange("p h d -> p (h d)"), Q[1][:, D:2 * D], ACT.Square)
                    act.copy(k_sb[:].rearrange("p h d -> p (h d)"), Q[1][:, D:2 * D])
                    act.activation(be[:], Q[2][:, D:D + DH], ACT.Exp, scale=-1.0)
                    act.activation(v_sb[:].rearrange("p h d -> p (h d)"), Q[2][:, 0:D],
                                   ACT.Silu).then_inc(d_qkv.handle, 1)
                    if t:
                        act.wait_ge(d_ast.handle, d_ast.at(b, t * NB * 16))
                    act.copy(q_sb[:], Q[1][:, 0:D]).then_inc(d_q.handle, 1)
                    yield D1_STEPS * t + 2
                    act.wait_ge(d_kqT.handle, d_kqT.at(b, t + 1))
                    act.copy(qT[:, t].rearrange("p g n -> p (g n)"), Q[3][:, 0:D])
                    own(act.copy(kT[:].rearrange("p g n -> p (g n)"), Q[3][:, D:2 * D]))
                    act.sem_inc(d_kqc.handle, 1)
                    pads(0, t).then_inc(d_padA.handle, 1)
                    yield D1_STEPS * t + 3
                    act.wait_ge(d_gram.handle, d_gram.at(b, 2 * t + 1))
                    pads(1, t).then_inc(d_pad2A.handle, 1)
                for t in range(NT):
                    yield D20 + D2_STEPS * t
                    act.wait_ge(d_uwp.handle, d_uwp.at(b, t + 1))
                    uwp = Q[1][:].rearrange("p (h k d) -> p k h d", h=DH, k=2)
                    act.copy(w_sb[:], uwp[:, 1])
                    act.copy(u_sb[:], uwp[:, 0]).then_inc(d_uwc.handle, 1)
                    yield D20 + D2_STEPS * t + 1
                    act.wait_ge(d_wTp.handle, d_wTp.at(b, t + 1))
                    act.copy(wT[:].rearrange("p g n -> p (g n)"), Q[1][:, 0:D]).then_inc(d_wT.handle, 1)

            own.restart()
            alone(ssm_stage(0, 0))
            window(ssm_stage(1, 1), ffn(0, 0, False), SSM_PLAN)
            with act.Fori(1, B - 1) as b:
                own.restart()
                window(delta_stage(b - 1, 2 * b), ffn(2 * b - 1, b, False), DELTA_PLAN)
                window(ssm_stage(b + 1, 2 * b + 1), ffn(2 * b, b - 1, True), SSM_PLAN)
            own.restart()
            window(delta_stage(B - 2, 2 * B - 2), ffn(2 * B - 3, B - 1, False), DELTA_PLAN)
            window(delta_stage(B - 1, 2 * B - 1), ffn(2 * B - 2, B - 2, True), DELTA_PLAN)
            alone(ffn(2 * B - 1, B - 1, True))

        @block.vector
        def _(dve):
            own = Own(dve, dve_own)
            dve.wait_ge(w_dma, 16 * 14)
            for k in range(4):
                last = dve.tensor_scalar(wout_sb[:, k, :], wout_sb[:, k, :], nw_sb[:, k:k + 1], None, ALU.mult)
            last.then_inc(wout_done, 1)
            dve.wait_ge(const_done, 1)
            dve.wait_ge(arow_done, 1)

            def x_slot(b):
                if isinstance(b, int):
                    return x_sb[:, b % SLOTS]
                return x_sb[:, bass.ds(dve.snap(b % SLOTS), 1)].squeeze(1)

            def norm_stats(x, done):
                for t in range(NT):
                    last = dve.bn_stats(bst[:, t, :], x[:, t, :])
                own(last)
                for t in range(NT):
                    last = dve.bn_aggr(mv[:, t, :], bst[:, t, :])
                last.then_inc(done.handle, 1)

            def ffn_stats(x, t):
                if t % 2:
                    for i in range(2):
                        last = dve.bn_stats(fbst[:, i, :], x[:, t - 1 + i, :])
                    own(last)
                    for i in range(2):
                        last = dve.bn_aggr(fmv[:, t - 1 + i, :], fbst[:, i, :])
                    last.then_inc(f_stats.handle, 1)

            def normed(dst, x, t, mean, dev):
                return dve.tensor_scalar(dst, x[:, t, :], mean[:, t, 0:1], dev[:, t:t + 1],
                                         ALU.subtract, ALU.mult)

            def ffn(p, b, final):
                x = x_slot(b)

                def norm_unit(u):
                    dve.wait_ge(f_rstd.handle, f_rstd.at(p, u + 1))
                    normed(xnf[:, 0, :], x, 2 * u, fmv, frstd)
                    normed(xnf[:, 1, :], x, 2 * u + 1, fmv, frstd).then_inc(f_xn.handle, 1)

                for u in range(UNITS):
                    s0 = u * SLICES
                    yield s0
                    if u == 0:
                        norm_unit(0)
                    dve.wait_ge(f_xhi.handle, f_xhi.at(p, u + 1))
                    dve.tensor_tensor(xf_lo[:].rearrange("p t k n -> p (t k n)"), F[s0 % 4][:],
                                      xf_hi[:].rearrange("p t k n -> p (t k n)").bitcast(F32),
                                      ALU.subtract).then_inc(f_xlo.handle, 1)
                    dve.wait_ge(f_xlo.handle, f_xlo.at(p, u + 1))
                    dve.sem_inc(f_free.handle, 1)
                    for j in range(HSLICES):
                        n = u * HSLICES + j
                        s = s0 + ffn_slice(j)
                        yield s
                        dve.wait_ge(f_act.handle, f_act.at(p, n + 1))
                        hi, lo, w = ffn_dst(j)
                        if j < KT:
                            dve.wait_ge(f_lo.handle, f_lo.at(p, n - 1))
                            own(dve.scalar_tensor_tensor(hid[:, n % 2, 0, :], F[s % 4][:, TOK:2 * TOK],
                                                         s2_sb[:, j:j + 1], gate[:, n % 2, :],
                                                         ALU.mult, ALU.mult))
                        dve.sem_inc(f_free.handle, 1)
                        dve.tensor_copy(hi, hid[:, n % 2, 0:w, :]).then_inc(f_hi.handle, 1)
                        if u + 1 < UNITS and j == HSLICES - 2:
                            norm_unit(u + 1)
                    s = s0 + SLICES - 1
                    yield s
                    dve.wait_ge(f_ps.handle, f_ps.at(p, s + 1))
                    o = F[s % 4][:].rearrange("p (t d) -> p t d", t=2)
                    own(dve.tensor_tensor(hid[:, 0], o, bcast(w3s_row[:], 1, 2), ALU.mult))
                    dve.sem_inc(f_free.handle, 1)
                    xu = x[:, 2 * u:2 * u + 2, :]
                    own(dve.tensor_tensor(xu, xu, hid[:, 0], ALU.add))
                if final:
                    dve.sem_inc(x_final.handle, 1)

            def ssm_stage(b, p):
                yield 0
                x = x_slot(b)
                dve.wait_ge(x_loaded.handle, x_loaded.at(b, 16))
                norm_stats(x, a_stats)
                dve.wait_ge(a_clear.handle, a_clear.at(b, 1))
                for t in range(NT):
                    yield SSM_STEPS * t
                    if t == 0:
                        dve.wait_ge(a_rstd.handle, a_rstd.at(b, 1))
                        normed(xn[:], x, t, mv, rstd).then_inc(a_xn.handle, 1)
                    yield SSM_STEPS * t + 1
                    dve.wait_ge(a_proj.handle, a_proj.at(b, t + 1))
                    dve.tensor_tensor(dtv[:], Q[3][:, 2 * N:2 * N + H], bias_row[:], ALU.add).then_inc(a_dtv.handle, 1)
                    dve.wait_ge(a_soft.handle, a_soft.at(b, t + 1))
                    own(dve.scalar_tensor_tensor(dta[:, 0, :], dtv[:], 0.0, dtl[:], ALU.max, ALU.add))
                    own(dve.tensor_tensor(dta[:, 1, :], dta[:, 0, :], a_row[:], ALU.mult))
                    dve.tensor_tensor(seg[:], bcast(stri[:], 1, H), bcast(dta[:, 1, :], 2, P),
                                      ALU.mult).then_inc(a_seg.handle, 1)
                    yield SSM_STEPS * t + 2
                    dve.wait_ge(a_sums.handle, a_sums.at(b, t + 1))
                    own(dve.tensor_copy(sums[:], Q[0][:, 0:40]))
                    dve.sem_inc(a_sumc.handle, 1)
                    own(dve.tensor_tensor(ang[:], bcast(sums[:, 0:16].rearrange("p (k h) -> p k h", k=2), 3, PAIRS),
                                          freq[:].unsqueeze(1).unsqueeze(1).broadcast_to([P, 2, H, PAIRS]), ALU.mult))
                    own(dve.tensor_tensor(ang[:], ang[:], bcast(phase[:], 1, 2), ALU.add))
                    own(dve.tensor_scalar(angk[:], ang[:], 1.0 / (2 * PI), MAGIC, ALU.mult, ALU.add))
                    own(dve.tensor_scalar(angk[:], angk[:], MAGIC, None, ALU.subtract))
                    own(dve.scalar_tensor_tensor(ang[:], angk[:], -TWO_PI_HI, ang[:], ALU.mult, ALU.add))
                    own(dve.scalar_tensor_tensor(ang[:], angk[:], -TWO_PI_LO, ang[:], ALU.mult, ALU.add))
                    dve.tensor_scalar(angr[:], ang[:, 0], PI_SAFE, -PI_SAFE, ALU.min, ALU.max).then_inc(a_ang.handle, 1)
                    dve.tensor_copy(phase[:], ang[:, 1])
                    dve.wait_ge(a_trig.handle, a_trig.at(b, t + 1))
                    pair = bc[:, :, 0:2 * PAIRS].rearrange("p k (n two) -> p k two n", two=2)
                    v1 = bcast(pair[:, :, 0], 2, H)
                    v2 = bcast(pair[:, :, 1], 2, H)
                    c_, s_ = bcast(cosT[:], 1, 2), bcast(sinT[:], 1, 2)
                    dve.tensor_tensor(r1, v1, c_, ALU.mult)
                    dve.tensor_tensor(r2, v2, s_, ALU.mult)
                    dve.tensor_tensor(r3, v2, c_, ALU.mult)
                    own(dve.tensor_tensor(r4, v1, s_, ALU.mult))
                    rot = hat[:, :, :, 0:2 * PAIRS].rearrange("p k h (n two) -> p k h two n", two=2)
                    dve.tensor_tensor(rot[:, :, :, 0], r1, r2, ALU.add)
                    dve.tensor_tensor(rot[:, :, :, 1], r3, r4, ALU.subtract).then_inc(a_hat.handle, 1)
                    yield SSM_STEPS * t + 3
                    dve.wait_ge(a_hatT.handle, a_hatT.at(b, t + 1))
                    cps = Q[0][:].rearrange("p (k n) -> p k n", k=4)
                    dve.tensor_copy(cT[0:64, :, 0, :], cps[0:64])
                    dve.tensor_copy(cT[64:128, :, 1, :], cps[64:128]).then_inc(a_cT.handle, 1)
                    yield SSM_STEPS * t + 4
                    dve.wait_ge(a_score.handle, a_score.at(b, t + 1))
                    for i in range(2):
                        d_ = seg[:, 4 * i:4 * i + 4, :].rearrange("p h t -> p (h t)")
                        last = dve.tensor_tensor(d_, Q[1 + i][:], d_, ALU.mult)
                    last.then_inc(a_pm.handle, 1)
                    yield SSM_STEPS * t + 5
                    dve.wait_ge(a_y.handle, a_y.at(b, t + 1))
                    own(dve.tensor_tensor(y[:], Q[0][:].rearrange("p (h d) -> p h d", h=H),
                                          bcast(decays[:, 0, :], 2, HP), ALU.mult))
                    own(dve.tensor_tensor(y[:], Q[3][:].rearrange("p (h d) -> p h d", h=H), y[:], ALU.add))
                    own(dve.tensor_tensor(y[:], y[:], xD[:], ALU.add))
                    dve.tensor_tensor(y[:].rearrange("p h d -> p (h d)"), y[:].rearrange("p h d -> p (h d)"), sz[:],
                                      ALU.mult).then_inc(a_yv.handle, 1)
                    dl_ = decays[:, 1, :].rearrange("p (k two) -> p two k", two=2)
                    dve.tensor_tensor(hst[0:64], hst[0:64], bcast(dl_[0:64, 0], 2, HP), ALU.mult)
                    own(dve.tensor_tensor(hst[64:128], hst[64:128], bcast(dl_[64:128, 1], 2, HP), ALU.mult))
                    own(dve.tensor_tensor(hst[:].rearrange("p k d -> p (k d)"), Q[1][:, 0:4 * HP],
                                          hst[:].rearrange("p k d -> p (k d)"), ALU.add))
                    if t + 1 < NT:
                        normed(xn[:], x, t + 1, mv, rstd).then_inc(a_xn.handle, 1)
                    yield SSM_STEPS * t + 7
                    dve.wait_ge(a_out.handle, a_out.at(b, t + 1))
                    dve.wait_ge(a_yr.handle, a_yr.at(b, t + 1))
                    own(dve.scalar_tensor_tensor(x[:, t, :], Q[2][:, 0:D], yrstd[:], x[:, t, :],
                                                 ALU.mult, ALU.add))
                    dve.sem_inc(a_res.handle, 1)
                    ffn_stats(x, t)

            def pads(g, t):
                for h in range(2, 4):
                    s = slice(HD * h, HD * (h + 1))
                    dve.tensor_copy(kqpad[s, 0, h, :], kT[s, g])
                    last = dve.tensor_copy(kqpad[s, 1, h, :], qT[s, t, g])
                return last

            def delta_stage(b, p):
                yield 0
                x = x_slot(b)
                norm_stats(x, d_stats)
                dve.wait_ge(d_clear.handle, d_clear.at(b, 1))
                for t in range(NT):
                    yield D1_STEPS * t
                    if t == 0:
                        dve.wait_ge(d_rstd.handle, d_rstd.at(b, 1))
                        normed(xnd[:], x, t, mv, rstd).then_inc(d_xn.handle, 1)
                    yield D1_STEPS * t + 1
                    dve.wait_ge(d_qkv.handle, d_qkv.at(b, t + 1))
                    own(dve.tensor_reduce(srow[:], ksq[:], AX.X, ALU.add))
                    dve.tensor_scalar(srow[:], srow[:], 1e-24, None, ALU.max).then_inc(d_ss.handle, 1)
                    own(dve.tensor_scalar(be1[:], be[:], 1.0, None, ALU.add))
                    own(dve.reciprocal(beta[:], be1[:]))
                    dve.sem_inc(d_beta.handle, 1)
                    dve.tensor_tensor(uw[:, t, :, 0, :], v_sb[:], bcast(beta[:], 2, HD), ALU.mult)
                    dve.wait_ge(d_rn.handle, d_rn.at(b, t + 1))
                    own(dve.tensor_tensor(kn[:, t], k_sb[:], bcast(rn[:], 2, HD), ALU.mult))
                    dve.sem_inc(d_kn.handle, 1)
                    dve.tensor_tensor(uw[:, t, :, 1, :], kn[:, t], bcast(beta[:], 2, HD), ALU.mult)
                    if t + 1 < NT:
                        normed(xnd[:], x, t + 1, mv, rstd).then_inc(d_xn.handle, 1)
                    yield D1_STEPS * t + 2
                    dve.wait_ge(d_kqc.handle, d_kqc.at(b, t + 1))
                    pads(0, t).then_inc(d_padV.handle, 1)
                    yield D1_STEPS * t + 3
                    dve.wait_ge(d_gram.handle, d_gram.at(b, 2 * t + 1))
                    pads(1, t).then_inc(d_pad2V.handle, 1)
                    yield D1_STEPS * t + 4
                    dve.wait_ge(d_gram.handle, d_gram.at(b, 2 * t + 2))
                    dve.wait_ge(d_bm.handle, d_bm.at(b, t + 1))
                    gram = Q[1][:].rearrange("p (g k h i) -> p k g h i", g=G, k=2, h=4)
                    dve.tensor_tensor(amv.rearrange("p (g h) i -> p g h i", g=G), gram[:, 0],
                                      bmask[:].rearrange("p (g h) i -> p g h i", g=G),
                                      ALU.mult).then_inc(d_am.handle, 1)
                    own(dve.tensor_tensor(pc[:, t].rearrange("p (g h) i -> p g h i", g=G), gram[:, 1],
                                          umask[:].unsqueeze(1).unsqueeze(1).broadcast_to([P, G, 4, BLK]), ALU.mult))
                    dve.sem_inc(d_pc.handle, 1)
                for i in range(1, BLK):
                    yield SUB0 + (i - 1) // 2
                    if i == 1:
                        dve.wait_ge(d_aun.handle, d_aun.at(b, 16))
                    pr = prod[:, 0:i * i].rearrange("p (c j) -> p c j", c=i)
                    own(dve.tensor_tensor(pr, ti[:, 0:i, 0:i], bcast(au[:, i, 0:i], 1, i), ALU.mult))
                    own(dve.tensor_reduce(ti[:, 0:i, i], pr, AX.X, ALU.add, negate=True))
                dve.sem_inc(d_inv.handle, 1)
                for t in range(NT):
                    yield D20 + D2_STEPS * t
                    if t == 0:
                        dve.wait_ge(d_clear.handle, d_clear.at(b, 2))
                    dve.wait_ge(d_uwc.handle, d_uwc.at(b, t + 1))
                    for c in range(NB):
                        n = t * NB + c
                        s = slice(BLK * c, BLK * (c + 1))
                        yield D20 + D2_STEPS * t + 2 + 2 * c
                        dve.wait_ge(d_ws.handle, d_ws.at(b, n + 1))
                        us = u_sb[s].rearrange("p h d -> p (h d)")
                        dve.scalar_tensor_tensor(us, Q[0][s, 0:D], -1.0, us, ALU.mult,
                                                 ALU.add).then_inc(d_u.handle, 1)
                        yield D20 + D2_STEPS * t + 3 + 2 * c
                        dve.wait_ge(d_sp.handle, d_sp.at(b, n + 1))
                        for g in range(G):
                            last = dve.tensor_tensor(sbd[:, g, :].rearrange("p (h d) -> p h d", h=4),
                                                     Q[3][:, g * P:(g + 1) * P].rearrange("p (h d) -> p h d", h=4),
                                                     bcast(bdmask[:], 2, HD), ALU.mult)
                        last.then_inc(d_s.handle, 1)
                    yield D20 + D2_STEPS * t + D2_STEPS - 1
                    dve.wait_ge(d_o.handle, d_o.at(b, t + 1))
                    own(dve.bn_stats(dbst[:], Q[2][:, 0:D]))
                    dve.bn_aggr(dmv[:], dbst[:]).then_inc(d_ost.handle, 1)
                    dve.wait_ge(d_ors.handle, d_ors.at(b, t + 1))
                    own(dve.tensor_scalar(on[:], Q[2][:, 0:D], dmv[:, 0:1], drs[:], ALU.subtract, ALU.mult))
                    dve.sem_inc(d_done.handle, 1)
                    own(dve.tensor_tensor(on[:], on[:], lnw_row[:], ALU.mult))
                    own(dve.tensor_tensor(on[:], on[:], lnb_row[:], ALU.add))
                    own(dve.tensor_tensor(x[:, t, :], x[:, t, :], on[:], ALU.add))
                    ffn_stats(x, t)

            own.restart()
            alone(ssm_stage(0, 0))
            window(ssm_stage(1, 1), ffn(0, 0, False), SSM_PLAN)
            with dve.Fori(1, B - 1) as b:
                own.restart()
                window(delta_stage(b - 1, 2 * b), ffn(2 * b - 1, b, False), DELTA_PLAN)
                window(ssm_stage(b + 1, 2 * b + 1), ffn(2 * b, b - 1, True), SSM_PLAN)
            own.restart()
            window(delta_stage(B - 2, 2 * B - 2), ffn(2 * B - 3, B - 1, False), DELTA_PLAN)
            window(delta_stage(B - 1, 2 * B - 1), ffn(2 * B - 2, B - 2, True), DELTA_PLAN)
            alone(ffn(2 * B - 1, B - 1, True))

        @block.tensor
        def _(pe):
            pe.wait_ge(w_dma, 16 * 14)
            pe.wait_ge(const_done, 1)
            pe.wait_ge(wout_done, 1)

            def ffn(p, b, final):
                def bank(s):
                    pe.wait_ge(f_free.handle, f_free.at(p, s - 3))
                    return F[s % 4]

                for u in range(UNITS):
                    s0 = u * SLICES
                    n0 = u * HSLICES
                    yield s0
                    pe.wait_ge(f_xn.handle, f_xn.at(p, u + 1))
                    ps = bank(s0)
                    for t in range(2):
                        for k in range(2):
                            o = (2 * t + k) * P
                            last = pe.transpose(ps[:, o:o + P], xnf[:, t, k * P:(k + 1) * P], ident[:])
                    last.then_inc(f_ps.handle, 1)
                    for j in range(KT):
                        yield s0 + 1 + j
                        if j == 0:
                            pe.wait_ge(f_xlo.handle, f_xlo.at(p, u + 1))
                        ps = bank(s0 + 1 + j)
                        for i, w in enumerate((w1_sb, w2_sb)):
                            for k in range(2):
                                for part in (xf_hi, xf_lo):
                                    last = pe.matmul(ps[:, i * TOK:(i + 1) * TOK].rearrange("p (t n) -> p t n", t=2),
                                                     w[:, k, j * P:(j + 1) * P], part[:, :, k, :],
                                                     start=(k == 0 and part is xf_hi), stop=(k == 1 and part is xf_lo))
                        last.then_inc(f_ps.handle, 1)
                    for layer, (w, src) in enumerate(((h1_sb, (hA_hi, hA_lo)), (h2_sb, (hB_hi, hB_lo)))):
                        for j in range(KT // 2):
                            s = s0 + 1 + KT + layer * (KT // 2) + j
                            yield s
                            ps = bank(s)
                            for i in range(2):
                                o = (2 * j + i) * P
                                for k in range(KT):
                                    if j == 0 and i == 0:
                                        done = k + 1 if layer == 0 else KT + k // 2 + 1
                                        pe.wait_ge(f_lo.handle, f_lo.at(p, n0 + done))
                                    for part in src:
                                        last = pe.matmul(ps[:, i * TOK:(i + 1) * TOK], w[:, k, o:o + P], part[:, k, :],
                                                         start=(k == 0 and part is src[0]),
                                                         stop=(k == KT - 1 and part is src[1]))
                            last.then_inc(f_ps.handle, 1)
                    yield s0 + SLICES - 1
                    ps = bank(s0 + SLICES - 1)
                    for t in range(2):
                        for k in range(KT):
                            if t == 0:
                                pe.wait_ge(f_lo.handle, f_lo.at(p, n0 + KT + KT // 2 + k // 2 + 1))
                            for part in (hA_hi, hA_lo):
                                last = pe.matmul(ps[:, t * D:(t + 1) * D], part[:, k, t * P:(t + 1) * P], w3_sb[:, k, :],
                                                 start=(k == 0 and part is hA_hi), stop=(k == KT - 1 and part is hA_lo))
                    last.then_inc(f_ps.handle, 1)

            def ssm_stage(b, p):
                for t in range(NT):
                    yield SSM_STEPS * t
                    pe.wait_ge(a_xn.handle, a_xn.at(b, t + 1))
                    for k in range(2):
                        last = pe.transpose(Q[0][:, k * P:(k + 1) * P], xn[:, k * P:(k + 1) * P], ident[:])
                    last.then_inc(a_xTp.handle, 1)
                    yield SSM_STEPS * t + 1
                    pe.wait_ge(a_xT.handle, a_xT.at(b, t + 1))
                    if t:
                        pe.wait_ge(a_res.handle, a_res.at(b, t))
                    for q, c0, c1 in ((1, 0, DI), (2, DI, 2 * DI), (3, 2 * DI, W_IN)):
                        for k in range(2):
                            last = pe.matmul(Q[q][:, 0:c1 - c0], xT[:, k, :], win_sb[:, k, c0:c1],
                                             start=(k == 0), stop=(k == 1))
                    last.then_inc(a_proj.handle, 1)
                    yield SSM_STEPS * t + 2
                    pe.wait_ge(a_seg.handle, a_seg.at(b, t + 1))
                    kinds = Q[0][:, 0:32].rearrange("p (g k h) -> p k g h", g=2, k=2)
                    both = dta[:]
                    pe.matmul(kinds[:, 0], tri[:], both, start=True, stop=True)
                    pe.matmul(kinds[:, 1], ones[:], both, start=True, stop=True)
                    pe.matmul(Q[0][:, 32:40], stri[:], dta[:, 1, :], start=True, stop=True).then_inc(a_sums.handle, 1)
                    pe.wait_ge(a_zx.handle, a_zx.at(b, t + 1))
                    for h in range(H):
                        q = Q[1 + h // 4]
                        if h % 4 == 0:
                            pe.matmul(q[:], far_i[:], past[:].rearrange("p h t -> p (h t)"), start=True, stop=False,
                                      skip_group_check=True)
                        o = (h % 4) * P
                        last = pe.matmul(q[:, o:o + P], seg[:, h, :], tri[:], start=False, stop=(h % 4 == 3),
                                         skip_group_check=True)
                    last.then_inc(a_segp.handle, 1)
                    yield SSM_STEPS * t + 3
                    pe.wait_ge(a_hat.handle, a_hat.at(b, t + 1))
                    pe.wait_ge(a_flat.handle, a_flat.at(b, t + 1))
                    for i, q in ((0, 3), (1, 0)):
                        for hp in range(4):
                            last = pe.transpose(Q[q][:, hp * P:(hp + 1) * P],
                                                hat[:, i, 2 * hp:2 * hp + 2, :].rearrange("p h n -> p (h n)"), ident[:])
                    last.then_inc(a_hatT.handle, 1)
                    yield SSM_STEPS * t + 4
                    pe.wait_ge(a_bT.handle, a_bT.at(b, t + 1))
                    pe.wait_ge(a_cT.handle, a_cT.at(b, t + 1))
                    for hp in range(4):
                        o = (hp % 2) * 2 * P
                        last = pe.matmul(Q[1 + hp // 2][:, o:o + 2 * P], bT[:, hp, :],
                                         cT[:, hp].rearrange("p e t -> p (e t)"), start=True, stop=True)
                    last.then_inc(a_score.handle, 1)
                    yield SSM_STEPS * t + 5
                    pe.wait_ge(a_pm.handle, a_pm.at(b, t + 1))
                    pe.wait_ge(a_wx.handle, a_wx.at(b, t + 1))
                    for h in range(H):
                        pe.matmul(Q[3][:, h * HP:(h + 1) * HP], seg[:, h, :], xdt[:, h, :], start=True, stop=True)
                    for h in range(H):
                        pe.matmul(Q[0][:, h * HP:(h + 1) * HP], cT[:, h // 2, h % 2, :], hst[:, h // 2, :],
                                  start=True, stop=True)
                    for h in range(H):
                        e, hp = h % 2, h // 2
                        last = pe.matmul(Q[1][64 * e:64 * e + 64, hp * HP:(hp + 1) * HP], hat[:, 0, h, :], wx[:, h, :],
                                         start=True, stop=True)
                    last.then_inc(a_y.handle, 1)
                    yield SSM_STEPS * t + 6
                    pe.wait_ge(a_yv.handle, a_yv.at(b, t + 1))
                    for k in range(4):
                        last = pe.transpose(Q[3][:, k * P:(k + 1) * P],
                                            y[:, 2 * k:2 * k + 2, :].rearrange("p h d -> p (h d)"), ident[:])
                    last.then_inc(a_yTp.handle, 1)
                    yield SSM_STEPS * t + 7
                    pe.wait_ge(a_yT.handle, a_yT.at(b, t + 1))
                    for k in range(4):
                        last = pe.matmul(Q[2][:, 0:D], yT[:, k, :], wout_sb[:, k, :], start=(k == 0), stop=(k == 3))
                    last.then_inc(a_out.handle, 1)

            def delta_stage(b, p):
                for t in range(NT):
                    yield D1_STEPS * t
                    pe.wait_ge(d_xn.handle, d_xn.at(b, t + 1))
                    for k in range(2):
                        last = pe.transpose(Q[0][:, k * P:(k + 1) * P], xnd[:, k * P:(k + 1) * P], ident[:])
                    last.then_inc(d_xTp.handle, 1)
                    yield D1_STEPS * t + 1
                    pe.wait_ge(d_xT.handle, d_xT.at(b, t + 1))
                    if t:
                        pe.wait_ge(d_pc.handle, d_pc.at(b, t))
                    for q, c0, c1 in ((1, 0, 2 * D), (2, 2 * D, W_QKVB)):
                        for k in range(2):
                            last = pe.matmul(Q[q][:, 0:c1 - c0], xTd[:, k, :], wqkvb_sb[:, k, c0:c1],
                                             start=(k == 0), stop=(k == 1))
                    last.then_inc(d_proj.handle, 1)
                    yield D1_STEPS * t + 2
                    pe.wait_ge(d_kn.handle, d_kn.at(b, t + 1))
                    pe.wait_ge(d_q.handle, d_q.at(b, t + 1))
                    knf = kn[:, t].rearrange("p h d -> p (h d)")
                    for i, src in enumerate((q_sb[:], knf)):
                        for g in range(G):
                            o = (2 * i + g) * P
                            last = pe.transpose(Q[3][:, o:o + P], src[:, g * P:(g + 1) * P], ident[:])
                    last.then_inc(d_kqT.handle, 1)
                    for g in range(G):
                        yield D1_STEPS * t + 3 + g
                        padA, padV = ((d_padA, d_padV), (d_pad2A, d_pad2V))[g]
                        pe.wait_ge(padA.handle, padA.at(b, t + 1))
                        pe.wait_ge(padV.handle, padV.at(b, t + 1))
                        for c in range(NB):
                            s = slice(BLK * c, BLK * (c + 1))
                            last = pe.matmul(Q[1][s, g * 256:(g + 1) * 256].rearrange("p (k i) -> p k i", k=8),
                                             kT[:, g, s], kqpad[:, :, :, s].rearrange("p k h i -> p (k h) i"),
                                             start=True, stop=True)
                        last.then_inc(d_gram.handle, 1)
                for t in range(NT):
                    yield D20 + D2_STEPS * t
                    pe.wait_ge(d_tbd.handle, d_tbd.at(b, (t + 1) * NB * 16))
                    for h in range(DH):
                        last = pe.matmul(Q[1][:, h * 64:(h + 1) * 64], tbd[:, h, :],
                                         uw[:, t, h].rearrange("p k d -> p (k d)"), start=True, stop=True)
                    last.then_inc(d_uwp.handle, 1)
                    yield D20 + D2_STEPS * t + 1
                    pe.wait_ge(d_uwc.handle, d_uwc.at(b, t + 1))
                    wf = w_sb[:].rearrange("p h d -> p (h d)")
                    for g in range(G):
                        last = pe.transpose(Q[1][:, g * P:(g + 1) * P], wf[:, g * P:(g + 1) * P], ident[:])
                    last.then_inc(d_wTp.handle, 1)
                    for c in range(NB):
                        n = t * NB + c
                        s = slice(BLK * c, BLK * (c + 1))
                        yield D20 + D2_STEPS * t + 2 + 2 * c
                        if c == 0:
                            pe.wait_ge(d_wT.handle, d_wT.at(b, t + 1))
                            if t:
                                pe.wait_ge(d_done.handle, d_done.at(b, t))
                        if n:
                            pe.wait_ge(d_s.handle, d_s.at(b, n))
                        for g in range(G):
                            last = pe.matmul(Q[0][s, g * P:(g + 1) * P], wT[:, g, s], sbd[:, g, :],
                                             start=True, stop=True)
                        last.then_inc(d_ws.handle, 1)
                        for g in range(G):
                            pe.matmul(Q[2][s, g * P:(g + 1) * P], qT[:, t, g, s], sbd[:, g, :],
                                      start=(g == 0), stop=False, skip_group_check=True)
                        yield D20 + D2_STEPS * t + 3 + 2 * c
                        pe.wait_ge(d_u.handle, d_u.at(b, n + 1))
                        for g in range(G):
                            last = pe.matmul(Q[3][:, g * P:(g + 1) * P],
                                             kn[s, t].rearrange("p h d -> p (h d)")[:, g * P:(g + 1) * P],
                                             u_sb[s].rearrange("p h d -> p (h d)")[:, g * P:(g + 1) * P],
                                             start=(n == 0 and g == 0), stop=(n == NT * NB - 1),
                                             skip_group_check=True)
                        last.then_inc(d_sp.handle, 1)
                    yield D20 + D2_STEPS * t + D2_STEPS - 1
                    pe.wait_ge(d_pbd.handle, d_pbd.at(b, t + 1))
                    for h in range(DH):
                        last = pe.matmul(Q[2][:, h * HD:(h + 1) * HD], pbd[:, h, :], u_sb[:, h, :],
                                         start=False, stop=True, skip_group_check=True)
                    last.then_inc(d_o.handle, 1)

            alone(ssm_stage(0, 0))
            pe.wait_ge(wr_dma, 16 * 5)
            window(ssm_stage(1, 1), ffn(0, 0, False), SSM_PLAN)
            with pe.Fori(1, B - 1) as b:
                window(delta_stage(b - 1, 2 * b), ffn(2 * b - 1, b, False), DELTA_PLAN)
                window(ssm_stage(b + 1, 2 * b + 1), ffn(2 * b, b - 1, True), SSM_PLAN)
            window(delta_stage(B - 2, 2 * B - 2), ffn(2 * B - 3, B - 1, False), DELTA_PLAN)
            window(delta_stage(B - 1, 2 * B - 1), ffn(2 * B - 2, B - 2, True), DELTA_PLAN)
            alone(ffn(2 * B - 1, B - 1, True))


def kernel(**inputs):
    import numpy as np
    import concourse.bacc as bacc
    from concourse.bass_utils import run_bass_kernel_spmd

    a = {k: np.asarray(v) for k, v in inputs.items()}

    def flat(v):
        return np.ascontiguousarray(v)

    def column(v, k):
        return flat(v.reshape(k, P).T)

    arrays = {
        "x": flat(a["L0_attn_a_x"].reshape(B * L, D)),
        "w_in": flat(a["L0_attn_a_W_in"]),
        "w_out": flat(a["L0_attn_a_W_out"]),
        "dt_bias": flat(a["L0_attn_a_dt_bias"]),
        "a_log": flat(a["L0_attn_a_A_log"]),
        "d_skip": flat(a["L0_attn_a_D_skip"]),
        "norm_w": column(a["L0_attn_a_norm_weight"], 4),
        "wqkvb": flat(np.concatenate([a["L0_attn_b_Wq"], a["L0_attn_b_Wk"], a["L0_attn_b_Wv"], a["L0_attn_b_Wb"]], 1)),
        "ln_w": flat(a["L0_attn_b_ln_w"]),
        "ln_b": flat(a["L0_attn_b_ln_b"]),
        "w1": flat(a["L0_ffn_w1_w"].T),
        "w1s": column(a["L0_ffn_w1_s"], KT),
        "w2": flat(a["L0_ffn_w2_w"].T),
        "w2s": column(a["L0_ffn_w2_s"], KT),
        "h1": flat(a["L0_ffn_h1_w"].T),
        "h1s": column(a["L0_ffn_h1_s"], KT),
        "h2": flat(a["L0_ffn_h2_w"].T),
        "h2s": column(a["L0_ffn_h2_s"], KT),
        "w3": flat(a["L0_ffn_w3_w"].T),
        "w3s": flat(a["L0_ffn_w3_s"]),
    }
    nc = bacc.Bacc("TRN2", target_bir_lowering=False, num_devices=1)
    args = [nc.dram_tensor(f"{k}_dram", v.shape, F32, kind="ExternalInput").ap() for k, v in arrays.items()]
    a_scr = nc.dram_tensor("a_scr", (NT, NB, DH, BLK, BLK), F32, kind="Internal").ap()
    t_scr = nc.dram_tensor("t_scr", (NT, NB, DH, BLK, BLK), F32, kind="Internal").ap()
    out = nc.dram_tensor("out_dram", (B * L, D), F32, kind="ExternalOutput").ap()
    hybrid_kernel(nc, *args, a_scr, t_scr, out)
    r = run_bass_kernel_spmd(nc, [{f"{k}_dram": v for k, v in arrays.items()}], core_ids=[0])
    return r.results[0]["out_dram"].reshape(B, L, D)
```

```python
from contextlib import ExitStack

import concourse.bass as bass
from concourse import mybir

F32 = mybir.dt.float32
F32R = mybir.dt.float32r
BF16 = mybir.dt.bfloat16
ALU = mybir.AluOpType
ACT = mybir.ActivationFunctionType
AX = mybir.AxisListType

P = 128
B, L, D = 8, 512, 256
NT = L // P
SLOTS = 3
EPS = 1e-5
H, HP, N = 8, 64, 64
DI = H * HP
PAIRS = 16
W_IN = 2 * DI + 2 * N + H
DH, HD = 8, 32
BLK = 32
NB = P // BLK
G = 2
W_QKVB = 3 * D + DH
HID = 1024
KT = HID // P
TOK = 256
UNITS = L // TOK
SLICES = KT + KT // 2 + KT // 2 + 1 + 1
HSLICES = KT + KT // 2 + KT // 2

SSM_STEPS = 8
D1_STEPS, SUB_STEPS, D2_STEPS = 5, BLK - 1, 2 * NB + 1
SUB0 = D1_STEPS * NT
D20 = SUB0 + SUB_STEPS + 2
U_AHEAD, WT_AHEAD = 3, 5


def spread(shares):
    unit = [(1, 4)] * KT + [(0.5, 8)] * (2 * KT) + [(1, 1)] + [(0.5, 8)] * 2
    parts = unit * UNITS
    total, whole = sum(c for _, c in parts), sum(shares)
    plan, spent, due, i = [], 0, 0, 0
    for share in shares:
        due += share * total / whole
        done = 0
        while i < len(parts) and spent + parts[i][1] / 2 <= due + 1e-6:
            done += parts[i][0]
            spent += parts[i][1]
            i += 1
        plan.append(done)
    plan[-1] += sum(p for p, _ in parts[i:])
    return plan


SSM_PLAN = spread([1, 5.9, 8.7, 3, 2, 3, 1, 0] * NT)
DELTA_PLAN = spread([2.8, 4, 2, 2, 1] * NT + [0.5] * 8 + [0.5] * (SUB_STEPS - 9) + [6]
                    + [2, 1] + ([1.2, 1.2] * NB + [2]) * NT)
assert sum(SSM_PLAN) == sum(DELTA_PLAN) == UNITS * SLICES

PI = 3.141592653589793
TWO_PI_HI = 6.28125
TWO_PI_LO = 2 * PI - TWO_PI_HI
MAGIC = 1.5 * 2.0 ** 23
PI_SAFE = 3.1415925
FAR = 30000.0


class Signal:

    def __init__(self, handle, per_batch, credit=0):
        self.handle, self.per_batch, self.credit = handle, per_batch, credit

    def at(self, b, n):
        return b * self.per_batch + (n + self.credit)


class Own:

    def __init__(self, eng, sem):
        self.eng, self.sem, self.n = eng, sem, 0

    def restart(self):
        self.eng.sem_clear(self.sem)
        self.n = 0

    def __call__(self, ins):
        self.n += 1
        ins.then_inc(self.sem, 1)
        self.eng.wait_ge(self.sem, self.n)


class Steps:

    def __init__(self, steps):
        self.steps = steps
        self.next = next(steps, None)

    def before(self, position):
        while self.next is not None and self.next < position:
            self.next = next(self.steps, None)


def window(attention, ffn, plan):
    att, mlp, done = Steps(attention), Steps(ffn), 0
    for step, slices in enumerate(plan):
        att.before(step + 1)
        done += slices
        mlp.before(done)


def alone(stage):
    for _ in stage:
        pass


def bcast(ap, axis, n):
    shape = list(ap.unsqueeze(axis).shape)
    shape[axis] = n
    return ap.unsqueeze(axis).broadcast_to(shape)


def hybrid_kernel(nc, x_in, w_in, w_out, dt_bias, a_log, d_skip, norm_w, wqkvb, ln_w, ln_b,
                  w1, w1s, w2, w2s, h1, h1s, h2, h2s, w3, w3s, a_scr, t_scr, out):
    with ExitStack() as ctx:
        def sb(name, shape, dt=F32):
            return ctx.enter_context(nc.sbuf_tensor(name, shape, dt))

        def sem(name):
            return ctx.enter_context(nc.semaphore(name))

        w1_sb = sb("w1_sb", [P, 2, HID], F32R)
        w2_sb = sb("w2_sb", [P, 2, HID], F32R)
        h1_sb = sb("h1_sb", [P, KT, HID], F32R)
        h2_sb = sb("h2_sb", [P, KT, HID], F32R)
        w3_sb = sb("w3_sb", [P, KT, D], F32R)
        win_sb = sb("win_sb", [P, 2, W_IN])
        wout_sb = sb("wout_sb", [P, 4, D])
        wqkvb_sb = sb("wqkvb_sb", [P, 2, W_QKVB])
        s1_sb = sb("s1_sb", [P, KT])
        s2_sb = sb("s2_sb", [P, KT])
        sh1_sb = sb("sh1_sb", [P, KT])
        sh2_sb = sb("sh2_sb", [P, KT])
        nw_sb = sb("nw_sb", [P, 4])
        w3s_row = sb("w3s_row", [P, D])
        lnw_row = sb("lnw_row", [P, D])
        lnb_row = sb("lnb_row", [P, D])
        bias_row = sb("bias_row", [P, H])
        a_row = sb("a_row", [P, H])
        d_row = sb("d_row", [P, H])
        ident = sb("ident", [P, P])
        ones = sb("ones", [P, P])
        tri = sb("tri", [P, P])
        stri = sb("stri", [P, P])
        far_i = sb("far_i", [P, P], BF16)
        past = sb("past", [P, 4, P], BF16)
        freq = sb("freq", [P, PAIRS])
        half_pi = sb("half_pi", [P, 1])
        neg_half = sb("neg_half", [P, 8])
        pool_pad = sb("pool_pad", [P, 1])
        smask = sb("smask", [P, BLK])
        umask = sb("umask", [P, BLK])
        bdmask = sb("bdmask", [P, 4])
        x_sb = sb("x_sb", [P, SLOTS, NT, D])
        bst = sb("bst", [P, NT, 6])
        mv = sb("mv", [P, NT, 2])
        ve = sb("ve", [P, NT])
        rstd = sb("rstd", [P, NT])
        fbst = sb("fbst", [P, 2, 6])
        fmv = sb("fmv", [P, NT, 2])
        fve = sb("fve", [P, NT])
        frstd = sb("frstd", [P, NT])
        in_mv = sb("in_mv", [P, NT, 2])
        in_ve = sb("in_ve", [P, NT])
        drstd = sb("drstd", [P, NT])
        xf_hi = sb("xf_hi", [P, 2, 2, P], F32R)
        xf_lo = sb("xf_lo", [P, 2, 2, P], F32R)
        hA_hi = sb("hA_hi", [P, KT, TOK], F32R)
        hA_lo = sb("hA_lo", [P, KT, TOK], F32R)
        hB_hi = sb("hB_hi", [P, KT, TOK], F32R)
        hB_lo = sb("hB_lo", [P, KT, TOK], F32R)
        hid = sb("hid", [P, 2, 2, TOK])
        gate = sb("gate", [P, 2, TOK])
        xnf = sb("xnf", [P, 2, D])

        with ExitStack() as ssm:
            def sa(name, shape, dt=F32):
                return ssm.enter_context(nc.sbuf_tensor(name, shape, dt))
            xn = sa("xn", [P, D])
            xT = sa("xT", [P, 2, P])
            sz = sa("sz", [P, DI])
            xs = sa("xs", [P, H, HP])
            bc = sa("bc", [P, 2, N])
            dtv = sa("dtv", [P, H])
            dtab = sa("dtab", [P, H])
            dte = sa("dte", [P, H])
            dtl = sa("dtl", [P, H])
            dta = sa("dta", [P, 2, H])
            seg = sa("seg", [P, H, P])
            sums = sa("sums", [P, 40])
            decays = sa("decays", [P, 3, H])
            phase = sa("phase", [P, H, PAIRS])
            ang = sa("ang", [P, 2, H, PAIRS])
            angk = sa("angk", [P, 2, H, PAIRS])
            angr = sa("angr", [P, H, PAIRS])
            anga = sa("anga", [P, H, PAIRS])
            cosT = sa("cosT", [P, H, PAIRS])
            sinT = sa("sinT", [P, H, PAIRS])
            hat = sa("hat", [P, 2, H, N])
            bT = sa("bT", [P, 4, P])
            cT = sa("cT", [P, 4, 2, P])
            xdt = sa("xdt", [P, H, HP])
            wrow = sa("wrow", [P, H])
            wx = sa("wx", [P, H, HP])
            xD = sa("xD", [P, H, HP])
            y = sa("y", [P, H, HP])
            yT = sa("yT", [P, 4, P])
            yss = sa("yss", [P, 1])
            yve = sa("yve", [P, 1])
            yrstd = sa("yrstd", [P, 1])
            r1, r2 = [y[:].rearrange("p h d -> p (h d)")[:, i * D:(i + 1) * D].rearrange(
                "p (k h n) -> p k h n", k=2, h=H) for i in range(2)]
            r3, r4 = [yT[:].rearrange("p k n -> p (k n)")[:, i * D:(i + 1) * D].rearrange(
                "p (k h n) -> p k h n", k=2, h=H) for i in range(2)]
            hst = sa("hst", [P, 4, HP])
        with ExitStack() as dl:
            def sd(name, shape, dt=F32):
                return dl.enter_context(nc.sbuf_tensor(name, shape, dt))
            xnd = sd("xnd", [P, D])
            xTd = sd("xTd", [P, 2, P])
            uw = sd("uw", [P, NT, DH, 2, HD])
            pc = sd("pc", [P, NT, DH, BLK])
            qT = sd("qT", [P, NT, G, P])
            kn = sd("kn", [P, NT, DH, HD])
            ti = sd("ti", [P, BLK, BLK])
            srow = sd("srow", [P, DH])
            rn = sd("rn", [P, DH])
            dbst = sd("dbst", [P, 6])
            dmv = sd("dmv", [P, 2])
            dve_ = sd("dve_", [P, 1])
            drs = sd("drs", [P, 1])
            with ExitStack() as d1:
                def s1_(name, shape):
                    return d1.enter_context(nc.sbuf_tensor(name, shape, F32))
                q_sb = s1_("q_sb", [P, D])
                k_sb = s1_("k_sb", [P, DH, HD])
                sig = s1_("sig", [P, D + DH])
                beta = sig[:, D:]
                ksq = s1_("ksq", [P, DH, HD])
                kT = s1_("kT", [P, G, P])
                kqpad = s1_("kqpad", [P, 2, 4, P])
                bmask = ksq
                amv = q_sb[:].rearrange("p (h i) -> p h i", h=DH)
            with ExitStack() as d2:
                def s2_(name, shape):
                    return d2.enter_context(nc.sbuf_tensor(name, shape, F32))
                au = s2_("au", [P, BLK, BLK])
                prod = s2_("prod", [P, BLK * BLK])
            with ExitStack() as d3:
                def s3_(name, shape):
                    return d3.enter_context(nc.sbuf_tensor(name, shape, F32))
                tbd = s3_("tbd", [P, DH, P])
                pbd = s3_("pbd", [P, DH, P])
                w_sb = s3_("w_sb", [P, DH, HD])
                tif = ti[:].rearrange("p j i -> p (j i)")
                u_sb = [s3_("u_sb", [P, DH, HD])[:], tif[:, 0:D].rearrange("p (h d) -> p h d", h=DH)]
                wT = [s3_("wT", [P, G, P])[:], tif[:, D:2 * D].rearrange("p (g n) -> p g n", g=G)]
                sbd = xTd
                on = xnd

        F = [ctx.enter_context(nc.psum_tensor(f"F{i}", [P, 512], F32)) for i in range(4)]
        Q = [ctx.enter_context(nc.psum_tensor(f"Q{i}", [P, 512], F32)) for i in range(4)]

        w_dma = sem("w_dma")
        wd_dma = sem("wd_dma")
        wr_dma = sem("wr_dma")
        dve_own, act_own, pool_own = sem("dve_own"), sem("act_own"), sem("pool_own")
        pool_gate = sem("pool_gate")
        const_done = sem("const_done")
        wout_done = sem("wout_done")
        arow_done = sem("arow_done")
        x_loaded = Signal(sem("x_loaded"), 16)
        x_stored = Signal(sem("x_stored"), 16, 16)
        x_final = Signal(sem("x_final"), 1)
        a_stats, a_rstd = Signal(sem("a_stats"), 1), Signal(sem("a_rstd"), 1)
        d_stats, d_rstd = Signal(sem("d_stats"), UNITS), Signal(sem("d_rstd"), UNITS)
        f_stats, f_rstd = Signal(sem("f_stats"), UNITS), Signal(sem("f_rstd"), UNITS)
        a_xn = Signal(sem("a_xn"), NT)
        a_xTp = Signal(sem("a_xTp"), NT)
        a_xT = Signal(sem("a_xT"), NT)
        a_proj = Signal(sem("a_proj"), NT)
        a_dtv = Signal(sem("a_dtv"), NT)
        a_soft = Signal(sem("a_soft"), NT)
        a_zx = Signal(sem("a_zx"), NT)
        a_seg = Signal(sem("a_seg"), NT)
        a_sums = Signal(sem("a_sums"), NT)
        a_segp = Signal(sem("a_segp"), NT)
        a_sumc = Signal(sem("a_sumc"), NT)
        a_dec = Signal(sem("a_dec"), NT)
        a_ang = Signal(sem("a_ang"), NT)
        a_trig = Signal(sem("a_trig"), NT)
        a_exp = Signal(sem("a_exp"), NT)
        a_flat = Signal(sem("a_flat"), NT)
        a_hat = Signal(sem("a_hat"), NT)
        a_hatT = Signal(sem("a_hatT"), NT)
        a_bT = Signal(sem("a_bT"), NT)
        a_cT = Signal(sem("a_cT"), NT)
        a_score = Signal(sem("a_score"), NT)
        a_pm = Signal(sem("a_pm"), NT)
        a_wx = Signal(sem("a_wx"), NT)
        a_y = Signal(sem("a_y"), NT)
        a_yv = Signal(sem("a_yv"), NT)
        a_ysq = Signal(sem("a_ysq"), NT)
        a_yr = Signal(sem("a_yr"), NT)
        a_yTp = Signal(sem("a_yTp"), NT)
        a_yT = Signal(sem("a_yT"), NT)
        a_out = Signal(sem("a_out"), NT)
        a_res = Signal(sem("a_res"), NT)
        a_clear = Signal(sem("a_clear"), 1)
        f_xn = Signal(sem("f_xn"), UNITS)
        f_ps = Signal(sem("f_ps"), UNITS * SLICES, 1)
        f_freeV = Signal(sem("f_freeV"), UNITS * (KT + 2), 1)
        f_freeA = Signal(sem("f_freeA"), UNITS * KT)
        f_xhi = Signal(sem("f_xhi"), UNITS)
        f_xlo = Signal(sem("f_xlo"), UNITS)
        f_act = Signal(sem("f_act"), UNITS * KT)
        f_hi = Signal(sem("f_hi"), UNITS * KT)
        f_hiA = Signal(sem("f_hiA"), UNITS * KT)
        f_lo = Signal(sem("f_lo"), UNITS * HSLICES, 2)
        d_clear = Signal(sem("d_clear"), 2)
        d_xn = Signal(sem("d_xn"), NT)
        d_xTp = Signal(sem("d_xTp"), NT)
        d_xT = Signal(sem("d_xT"), NT)
        d_proj = Signal(sem("d_proj"), NT)
        d_q = Signal(sem("d_q"), NT)
        d_qkv = Signal(sem("d_qkv"), NT)
        d_ss = Signal(sem("d_ss"), NT)
        d_rn = Signal(sem("d_rn"), NT)
        d_kn = Signal(sem("d_kn"), NT)
        d_beta = Signal(sem("d_beta"), NT)
        d_bm = Signal(sem("d_bm"), NT)
        d_kqT = Signal(sem("d_kqT"), NT)
        d_kqc = Signal(sem("d_kqc"), NT)
        d_padA = Signal(sem("d_padA"), NT)
        d_padV = Signal(sem("d_padV"), NT)
        d_pad2A = Signal(sem("d_pad2A"), NT)
        d_pad2V = Signal(sem("d_pad2V"), NT)
        d_gram = Signal(sem("d_gram"), 2 * NT)
        d_am = Signal(sem("d_am"), NT)
        d_pc = Signal(sem("d_pc"), NT)
        d_ast = Signal(sem("d_ast"), NT * NB * 16)
        d_aun = Signal(sem("d_aun"), 16)
        d_inv = Signal(sem("d_inv"), 1)
        d_tst = Signal(sem("d_tst"), 16)
        d_tbd = Signal(sem("d_tbd"), NT * NB * 16)
        d_pbd = Signal(sem("d_pbd"), NT)
        d_uwp = Signal(sem("d_uwp"), NT)
        d_uwc = Signal(sem("d_uwc"), NT)
        d_wTp = Signal(sem("d_wTp"), NT)
        d_wT = Signal(sem("d_wT"), NT)
        d_ws = Signal(sem("d_ws"), NT * NB)
        d_u = Signal(sem("d_u"), NT * NB)
        d_sp = Signal(sem("d_sp"), NT * NB)
        d_s = Signal(sem("d_s"), NT * NB)
        d_o = Signal(sem("d_o"), NT)
        d_ost = Signal(sem("d_ost"), NT)
        d_ors = Signal(sem("d_ors"), NT)
        d_done = Signal(sem("d_done"), NT)

        x_v = x_in.rearrange("(b t p) d -> p b t d", p=P, t=NT)
        o_v = out.rearrange("(b t p) d -> p b t d", p=P, t=NT)
        a_store = a_scr.rearrange("t c h i j -> t c i h j")
        a_load = a_scr.rearrange("t c h i j -> (t c h) (i j)")
        t_store = t_scr.rearrange("t c h j i -> (t c h) (j i)")
        t_load = t_scr.rearrange("t c h j i -> t c j h i")

        def uw_step(t):
            return D20 + D2_STEPS * (t - 1) + U_AHEAD if t else D20 - 2

        def wt_step(t):
            return D20 + D2_STEPS * (t - 1) + WT_AHEAD if t else D20 - 1

        block = ctx.enter_context(nc.Block())

        def ffn_dst(j):
            if j < KT:
                return hA_hi[:, j:j + 1, :], hA_lo[:, j:j + 1, :], 1
            if j < KT + KT // 2:
                k = 2 * (j - KT)
                return hB_hi[:, k:k + 2, :], hB_lo[:, k:k + 2, :], 2
            k = 2 * (j - KT - KT // 2)
            return hA_hi[:, k:k + 2, :], hA_lo[:, k:k + 2, :], 2

        XT_SLICE, W3_SLICE = HSLICES, HSLICES + 1

        def bank_of(s):
            return F[(s + 1) % 4]

        @block.sync
        def _(sp):
            sp.dma_start(x_sb[:, 0], x_v[:, 0]).then_inc(x_loaded.handle, 16)
            sp.dma_start(win_sb[:], w_in.rearrange("(k p) n -> p k n", p=P)).then_inc(w_dma, 16)
            sp.dma_start(wout_sb[:], w_out.rearrange("(k p) n -> p k n", p=P)).then_inc(w_dma, 16)
            for dst, src in ((s1_sb, w1s), (s2_sb, w2s), (sh1_sb, h1s), (sh2_sb, h2s), (nw_sb, norm_w)):
                sp.dma_start(dst[:], src).then_inc(w_dma, 16)
            for dst, src in ((w3s_row, w3s), (lnw_row, ln_w), (lnb_row, ln_b), (bias_row, dt_bias),
                             (a_row, a_log), (d_row, d_skip)):
                sp.dma_start(dst[:], src.partition_broadcast(P)).then_inc(w_dma, 16)
            sp.dma_start(wqkvb_sb[:], wqkvb.rearrange("(k p) n -> p k n", p=P)).then_inc(wd_dma, 16)

            def x_dram(ap, b):
                return ap[:, b] if isinstance(b, int) else ap[:, bass.ds(b, 1)].squeeze(1)

            def x_slot(b):
                return x_sb[:, b % SLOTS] if isinstance(b, int) else x_sb[:, bass.ds(sp.snap(b % SLOTS), 1)].squeeze(1)

            def load(b):
                sp.dma_start(x_slot(b), x_dram(x_v, b)).then_inc(x_loaded.handle, 16)

            def store(b):
                sp.wait_ge(x_final.handle, x_final.at(b, 1))
                sp.dma_start(x_dram(o_v, b), x_slot(b)).then_inc(x_stored.handle, 16)

            def delta(b):
                for t in range(NT):
                    sp.wait_ge(d_am.handle, d_am.at(b, t + 1))
                    for c in range(NB):
                        sp.dma_start(a_store[t, c], amv[BLK * c:BLK * (c + 1)]).then_inc(d_ast.handle, 16)
                sp.wait_ge(d_ast.handle, d_ast.at(b, NT * NB * 16))
                sp.dma_start(au[:].rearrange("p i j -> p (i j)"), a_load).then_inc(d_aun.handle, 16)
                sp.wait_ge(d_inv.handle, d_inv.at(b, 1))
                sp.dma_start(t_store, ti[:].rearrange("p j i -> p (j i)")).then_inc(d_tst.handle, 16)
                sp.wait_ge(d_tst.handle, d_tst.at(b, 16))
                sp.wait_ge(d_clear.handle, d_clear.at(b, 2))
                for t in range(NT):
                    if t:
                        sp.wait_ge(d_uwp.handle, d_uwp.at(b, t))
                    for c in range(NB):
                        sp.dma_start(tbd[BLK * c:BLK * (c + 1), :, BLK * c:BLK * (c + 1)],
                                     t_load[t, c]).then_inc(d_tbd.handle, 16)

            sp.wait_ge(x_loaded.handle, 16)
            load(1)
            with sp.Fori(1, B - 1) as b:
                sp.wait_ge(x_loaded.handle, x_loaded.at(b, 16))
                sp.wait_ge(x_stored.handle, x_stored.at(b - 2, 16))
                load(b + 1)
                delta(b - 1)
                store(b - 1)
            delta(B - 2)
            delta(B - 1)
            store(B - 2)
            store(B - 1)
            sp.wait_ge(x_stored.handle, x_stored.credit + 16 * B)

        @block.gpsimd
        def _(pool):
            own = Own(pool, pool_own)
            pool.sem_inc(x_stored.handle, x_stored.credit)
            pool.sem_inc(f_lo.handle, f_lo.credit)

            def select(out_, in_, pattern, op, fill, mult, base=0):
                own(pool.affine_select(out=out_, in_=in_, pattern=pattern, compare_op=op, fill=fill,
                                       base=base, channel_multiplier=mult))

            own(pool.memset(ones[:], 1.0))
            own(pool.memset(far_i[:], FAR))
            own(pool.memset(past[:], 1.0))
            own(pool.memset(half_pi[:], PI / 2))
            own(pool.memset(neg_half[:], -0.5))
            own(pool.memset(bdmask[:], 1.0))
            for i in range(PAIRS):
                own(pool.memset(freq[:, i:i + 1], float(1.0 / 10000.0 ** (i / PAIRS))))
            select(ident[:], ones[:], [[-1, P]], ALU.is_equal, 0.0, 1)
            select(far_i[:], far_i[:], [[-1, P]], ALU.is_equal, 0.0, 1)
            select(tri[:], ones[:], [[1, P]], ALU.is_ge, 0.0, -1)
            select(stri[:], ones[:], [[-1, P]], ALU.is_gt, 0.0, 1)
            select(past[:], past[:], [[0, 4], [-1, P]], ALU.is_gt, 0.0, 1)
            for c in range(NB):
                s = slice(BLK * c, BLK * (c + 1))
                select(smask[s], ones[s, 0:BLK], [[-1, BLK]], ALU.is_gt, 0.0, 1)
                select(umask[s], ones[s, 0:BLK], [[1, BLK]], ALU.is_ge, 0.0, -1)
                select(bdmask[s], bdmask[s], [[1, 4]], ALU.is_equal, 0.0, 0, base=-c)
            pool.sem_inc(const_done, 1)
            pool.wait_ge(w_dma, 16 * 13)
            for dst, src in ((w1_sb, w1), (w2_sb, w2), (h1_sb, h1), (h2_sb, h2), (w3_sb, w3)):
                pool.dma_start(dst[:], src.rearrange("(k p) o -> p k o", p=P)).then_inc(wr_dma, 16)

            def rsqrt(ready, value, dst, var, src, done):
                pool.wait_ge(ready.handle, value)
                pool.sem_inc(pool_gate, 1)
                own(pool.tensor_scalar(var, src, EPS, None, ALU.add))
                pool.tensor_tensor(dst, var, neg_half[:, 0:dst.shape[1]], ALU.pow).then_inc(done.handle, 1)

            def rsqrt_delta(b, u):
                s = slice(2 * u, 2 * u + 2)
                rsqrt(d_stats, d_stats.at(b, u + 1), drstd[:, s], in_ve[:, s], in_mv[:, s, 1], d_rstd)

            def rsqrt_ssm(b):
                rsqrt(a_stats, a_stats.at(b, 1), rstd[:], ve[:], mv[:, :, 1], a_rstd)

            def rsqrt_ffn(p, u):
                s = slice(2 * u, 2 * u + 2)
                rsqrt(f_stats, f_stats.at(p, u + 1), frstd[:, s], fve[:, s], fmv[:, s, 1], f_rstd)

            def ffn(p, b, final):
                for u in range(UNITS):
                    for j in range(HSLICES):
                        yield u * SLICES + j + 0.5
                        n = u * HSLICES + j
                        if j < KT:
                            pool.wait_ge(f_hi.handle, f_hi.at(p, u * KT + j + 1))
                        else:
                            pool.wait_ge(f_hiA.handle, f_hiA.at(p, u * KT + j - KT + 1))
                        hi, lo, w = ffn_dst(j)
                        pool.tensor_tensor(lo, hid[:, n % 2, 0:w, :], hi.bitcast(F32),
                                           ALU.subtract).then_inc(f_lo.handle, 1)
                    yield u * SLICES + W3_SLICE + 0.5
                    if not final:
                        rsqrt_delta(b, u)

            def ssm_stage(b, p):
                yield 0
                own(pool.memset(cT[:], 0.0))
                own(pool.memset(hst[:], 0.0))
                own(pool.memset(phase[:], 0.0))
                pool.sem_inc(a_clear.handle, 1)
                for t in range(NT):
                    yield SSM_STEPS * t + 2
                    pool.wait_ge(a_zx.handle, a_zx.at(b, t + 1))
                    pool.wait_ge(a_sumc.handle, a_sumc.at(b, t + 1))
                    pool.tensor_tensor(xdt[:], xs[:], bcast(dta[:, 0, :], 2, HP), ALU.mult)
                    pool.tensor_tensor(xD[:], xs[:], bcast(d_row[:], 2, HP), ALU.mult)
                    pool.wait_ge(a_dec.handle, a_dec.at(b, t + 1))
                    own(pool.tensor_tensor(wrow[:], decays[:, 2, :], dta[:, 0, :], ALU.mult))
                    pool.tensor_tensor(wx[:], xs[:], bcast(wrow[:], 2, HP), ALU.mult).then_inc(a_wx.handle, 1)
                    yield SSM_STEPS * t + 5
                    pool.wait_ge(a_ysq.handle, a_ysq.at(b, t + 1))
                    pool.sem_inc(pool_gate, 1)
                    own(pool.tensor_scalar(yve[:], yss[:], 1.0 / DI, EPS, ALU.mult, ALU.add))
                    pool.tensor_tensor(yrstd[:], yve[:], neg_half[:, 0:1], ALU.pow).then_inc(a_yr.handle, 1)
                    yield SSM_STEPS * t + 7
                    if t % 2:
                        rsqrt_ffn(p, t // 2)

            def delta_stage(b, p, next_ssm=True):
                yield 0
                own(pool.memset(kqpad[:], 0.0))
                own(pool.memset(ti[:], 0.0))
                own(pool.affine_select(out=ti[:], in_=ti[:], pattern=[[1, BLK], [-1, BLK]],
                                       compare_op=ALU.not_equal, fill=1.0, base=0, channel_multiplier=0))
                pool.sem_inc(d_clear.handle, 1)
                for t in range(NT):
                    yield D1_STEPS * t + 1
                    pool.wait_ge(d_ss.handle, d_ss.at(b, t + 1))
                    pool.tensor_tensor(rn[:], srow[:], neg_half[:], ALU.pow).then_inc(d_rn.handle, 1)
                    pool.wait_ge(d_beta.handle, d_beta.at(b, t + 1))
                    pool.tensor_tensor(bmask[:], bcast(smask[:], 1, DH), bcast(beta, 2, BLK),
                                       ALU.mult).then_inc(d_bm.handle, 1)
                yield SUB0 + SUB_STEPS - 1
                pool.wait_ge(d_inv.handle, d_inv.at(b, 1))
                pool.sem_inc(pool_gate, 1)
                own(pool.memset(tbd[:], 0.0))
                own(pool.memset(sbd[:], 0.0))
                own(pool.memset(pbd[:], 0.0))
                pool.sem_inc(d_clear.handle, 1)
                for t in range(NT):
                    yield D20 + D2_STEPS * t
                    if t:
                        pool.wait_ge(d_o.handle, d_o.at(b, t))
                        pool.sem_inc(pool_gate, 1)
                    own(pool.memset(pool_pad[:], 0.0))
                    for c in range(NB):
                        s = slice(BLK * c, BLK * (c + 1))
                        own(pool.tensor_copy(pbd[s, :, s], pc[s, t]))
                    pool.sem_inc(d_pbd.handle, 1)
                    if t == 2:
                        rsqrt_ffn(p, 0)
                    yield D20 + D2_STEPS * t + D2_STEPS - 1
                    if t == NT - 1 and next_ssm:
                        rsqrt_ssm(b + 2)
                    rsqrt(d_ost, d_ost.at(b, t + 1), drs[:], dve_[:], dmv[:, 1:2], d_ors)
                rsqrt_ffn(p, 1)

            own.restart()
            rsqrt_ssm(0)
            alone(ssm_stage(0, 0))
            rsqrt_ssm(1)
            window(ssm_stage(1, 1), ffn(0, 0, False), SSM_PLAN)
            with pool.Fori(1, B - 1) as b:
                own.restart()
                window(delta_stage(b - 1, 2 * b), ffn(2 * b - 1, b, False), DELTA_PLAN)
                window(ssm_stage(b + 1, 2 * b + 1), ffn(2 * b, b - 1, True), SSM_PLAN)
            own.restart()
            window(delta_stage(B - 2, 2 * B - 2, False), ffn(2 * B - 3, B - 1, False), DELTA_PLAN)
            window(delta_stage(B - 1, 2 * B - 1, False), ffn(2 * B - 2, B - 2, True), DELTA_PLAN)
            alone(ffn(2 * B - 1, B - 1, True))

        @block.scalar
        def _(act):
            own = Own(act, act_own)
            act.wait_ge(w_dma, 16 * 13)
            nc.scalar.preload_act_table_set("natural_log_exp_and_others")
            act.activation(a_row[:], a_row[:], ACT.Exp).then_inc(arow_done, 1)
            act.wait_ge(const_done, 1)

            def xt_high(p, s):
                act.wait_ge(f_ps.handle, f_ps.at(p, s + 1))
                act.copy(xf_hi[:].rearrange("p t k n -> p (t k n)"), bank_of(s)[:]).then_inc(f_xhi.handle, 1)

            def ffn(p, b, more=True):
                for u in range(UNITS):
                    s0 = u * SLICES
                    for j in range(HSLICES):
                        n = u * HSLICES + j
                        s = s0 + j
                        yield s + 0.5
                        act.wait_ge(f_ps.handle, f_ps.at(p, s + 1))
                        act.wait_ge(f_lo.handle, f_lo.at(p, n - 1))
                        ps = bank_of(s)
                        if j < KT:
                            act.activation(gate[:, n % 2, :], ps[:, 0:TOK], ACT.Silu,
                                           scale=s1_sb[:, j:j + 1]).then_inc(f_act.handle, 1)
                            continue
                        scales, k = (sh1_sb, 2 * (j - KT)) if j < KT + KT // 2 else (sh2_sb, 2 * (j - KT - KT // 2))
                        act.activation(hid[:, n % 2, 0, :], ps[:, 0:TOK], ACT.Gelu, scale=scales[:, k:k + 1])
                        own(act.activation(hid[:, n % 2, 1, :], ps[:, TOK:2 * TOK], ACT.Gelu,
                                           scale=scales[:, k + 1:k + 2]))
                        act.sem_inc(f_freeA.handle, 1)
                        act.copy(ffn_dst(j)[0], hid[:, n % 2]).then_inc(f_hiA.handle, 1)
                    yield s0 + XT_SLICE + 0.5
                    if u + 1 < UNITS or more:
                        xt_high(p, s0 + XT_SLICE)

            def ssm_stage(b, p):
                for t in range(NT):
                    yield SSM_STEPS * t
                    act.wait_ge(a_xTp.handle, a_xTp.at(b, t + 1))
                    act.copy(xT[:].rearrange("p k n -> p (k n)"), Q[0][:, 0:D]).then_inc(a_xT.handle, 1)
                    yield SSM_STEPS * t + 1
                    nc.scalar.preload_act_table_set("natural_log_exp_and_others")
                    act.wait_ge(a_dtv.handle, a_dtv.at(b, t + 1))
                    own(act.activation(dtab[:], dtv[:], ACT.Abs))
                    own(act.activation(dte[:], dtab[:], ACT.Exp, scale=-1.0))
                    act.activation(dtl[:], dte[:], ACT.Ln, bias=1.0).then_inc(a_soft.handle, 1)
                    act.copy(bc[:].rearrange("p k n -> p (k n)"), Q[3][:, 0:2 * N])
                    act.copy(xs[:].rearrange("p k n -> p (k n)"), Q[2][:])
                    own(act.activation(sz[:], Q[1][:], ACT.Silu))
                    act.sem_inc(a_zx.handle, 1)
                    act.copy(hat[:, :, :, 2 * PAIRS:N], bcast(bc[:, :, 2 * PAIRS:N], 2, H)).then_inc(a_flat.handle, 1)
                    yield SSM_STEPS * t + 2
                    act.wait_ge(a_ang.handle, a_ang.at(b, t + 1))
                    own(act.activation(anga[:], angr[:], ACT.Abs))
                    act.activation(sinT[:], angr[:], ACT.Sin)
                    act.activation(cosT[:], anga[:], ACT.Sin, scale=-1.0, bias=half_pi[:]).then_inc(a_trig.handle, 1)
                    nc.scalar.preload_act_table_set("natural_log_exp_and_others")
                    act.activation(decays[:].rearrange("p k h -> p (k h)"), sums[:, 16:40], ACT.Exp,
                                   scale=-1.0).then_inc(a_dec.handle, 1)
                    act.wait_ge(a_segp.handle, a_segp.at(b, t + 1))
                    act.activation(seg[:, 0:4, :].rearrange("p h t -> p (h t)"), Q[1][:], ACT.Exp, scale=-1.0)
                    act.activation(seg[:, 4:8, :].rearrange("p h t -> p (h t)"), Q[2][:], ACT.Exp,
                                   scale=-1.0).then_inc(a_exp.handle, 1)
                    yield SSM_STEPS * t + 3
                    act.wait_ge(a_hatT.handle, a_hatT.at(b, t + 1))
                    act.copy(bT[:].rearrange("p k n -> p (k n)"), Q[3][:]).then_inc(a_bT.handle, 1)
                    yield SSM_STEPS * t + 5
                    act.wait_ge(a_yv.handle, a_yv.at(b, t + 1))
                    act.activation(yT[:].rearrange("p k n -> p (k n)"), y[:].rearrange("p h d -> p (h d)"),
                                   ACT.Square, accum_out=yss[:]).then_inc(a_ysq.handle, 1)
                    yield SSM_STEPS * t + 6
                    act.wait_ge(a_ysq.handle, a_ysq.at(b, t + 1))
                    act.wait_ge(a_yTp.handle, a_yTp.at(b, t + 1))
                    act.copy(yT[:].rearrange("p k n -> p (k n)"), Q[3][:]).then_inc(a_yT.handle, 1)

            def pads(g, t):
                for h in range(2):
                    s = slice(HD * h, HD * (h + 1))
                    act.copy(kqpad[s, 0, h, :], kT[s, g])
                    last = act.copy(kqpad[s, 1, h, :], qT[s, t, g])
                return last

            def delta_stage(b, p, next_ssm=True):
                for t in range(NT):
                    yield D1_STEPS * t
                    act.wait_ge(d_xTp.handle, d_xTp.at(b, t + 1))
                    act.copy(xTd[:].rearrange("p k n -> p (k n)"), Q[0][:, 0:D]).then_inc(d_xT.handle, 1)
                    yield D1_STEPS * t + 1
                    act.wait_ge(d_proj.handle, d_proj.at(b, t + 1))
                    act.activation(ksq[:].rearrange("p h d -> p (h d)"), Q[1][:, D:2 * D], ACT.Square)
                    act.copy(k_sb[:].rearrange("p h d -> p (h d)"), Q[1][:, D:2 * D])
                    act.activation(sig[:], Q[2][:, 0:D + DH], ACT.Tanh, scale=0.5).then_inc(d_qkv.handle, 1)
                    if t:
                        act.wait_ge(d_ast.handle, d_ast.at(b, t * NB * 16))
                    act.copy(q_sb[:], Q[1][:, 0:D]).then_inc(d_q.handle, 1)
                    yield D1_STEPS * t + 2
                    act.wait_ge(d_kqT.handle, d_kqT.at(b, t + 1))
                    act.copy(qT[:, t].rearrange("p g n -> p (g n)"), Q[3][:, 0:D])
                    own(act.copy(kT[:].rearrange("p g n -> p (g n)"), Q[3][:, D:2 * D]))
                    act.sem_inc(d_kqc.handle, 1)
                    pads(0, t).then_inc(d_padA.handle, 1)
                    yield D1_STEPS * t + 3
                    act.wait_ge(d_gram.handle, d_gram.at(b, 2 * t + 1))
                    pads(1, t).then_inc(d_pad2A.handle, 1)
                for t in range(NT):
                    yield uw_step(t)
                    act.wait_ge(d_uwp.handle, d_uwp.at(b, t + 1))
                    uwp = Q[1][:].rearrange("p (h k d) -> p k h d", h=DH, k=2)
                    act.copy(w_sb[:], uwp[:, 1])
                    act.copy(u_sb[t % 2], uwp[:, 0]).then_inc(d_uwc.handle, 1)
                    yield wt_step(t)
                    act.wait_ge(d_wTp.handle, d_wTp.at(b, t + 1))
                    act.copy(wT[t % 2].rearrange("p g n -> p (g n)"), Q[1][:, 0:D]).then_inc(d_wT.handle, 1)

            own.restart()
            alone(ssm_stage(0, 0))
            xt_high(0, -1)
            window(ssm_stage(1, 1), ffn(0, 0), SSM_PLAN)
            with act.Fori(1, B - 1) as b:
                own.restart()
                window(delta_stage(b - 1, 2 * b), ffn(2 * b - 1, b), DELTA_PLAN)
                window(ssm_stage(b + 1, 2 * b + 1), ffn(2 * b, b - 1), SSM_PLAN)
            own.restart()
            window(delta_stage(B - 2, 2 * B - 2, False), ffn(2 * B - 3, B - 1), DELTA_PLAN)
            window(delta_stage(B - 1, 2 * B - 1, False), ffn(2 * B - 2, B - 2), DELTA_PLAN)
            alone(ffn(2 * B - 1, B - 1, False))

        @block.vector
        def _(dve):
            own = Own(dve, dve_own)
            dve.wait_ge(w_dma, 16 * 13)
            for k in range(4):
                last = dve.tensor_scalar(wout_sb[:, k, :], wout_sb[:, k, :], nw_sb[:, k:k + 1], None, ALU.mult)
            last.then_inc(wout_done, 1)
            dve.wait_ge(const_done, 1)
            dve.wait_ge(arow_done, 1)

            def x_slot(b):
                if isinstance(b, int):
                    return x_sb[:, b % SLOTS]
                return x_sb[:, bass.ds(dve.snap(b % SLOTS), 1)].squeeze(1)

            def ssm_stats(b):
                dve.wait_ge(x_loaded.handle, x_loaded.at(b, 16))
                x = x_slot(b)
                for t in range(NT):
                    last = dve.bn_stats(bst[:, t, :], x[:, t, :])
                own(last)
                for t in range(NT):
                    last = dve.bn_aggr(mv[:, t, :], bst[:, t, :])
                last.then_inc(a_stats.handle, 1)

            def unit_stats(x, t, means, done):
                for i in range(2):
                    last = dve.bn_stats(fbst[:, i, :], x[:, t + i, :])
                own(last)
                for i in range(2):
                    last = dve.bn_aggr(means[:, t + i, :], fbst[:, i, :])
                last.then_inc(done.handle, 1)

            def normed(dst, x, t, mean, dev):
                return dve.tensor_scalar(dst, x[:, t, :], mean[:, t, 0:1], dev[:, t:t + 1],
                                         ALU.subtract, ALU.mult)

            def first_ssm(b):
                dve.wait_ge(a_rstd.handle, a_rstd.at(b, 1))
                normed(xn[:], x_slot(b), 0, mv, rstd).then_inc(a_xn.handle, 1)

            def first_delta(b):
                dve.wait_ge(d_rstd.handle, d_rstd.at(b, UNITS))
                normed(xnd[:], x_slot(b), 0, in_mv, drstd).then_inc(d_xn.handle, 1)

            def norm_unit(p, x, u):
                dve.wait_ge(f_rstd.handle, f_rstd.at(p, u + 1))
                normed(xnf[:, 0, :], x, 2 * u, fmv, frstd)
                normed(xnf[:, 1, :], x, 2 * u + 1, fmv, frstd).then_inc(f_xn.handle, 1)

            def xt_low(p, s, p_to, u):
                dve.wait_ge(f_xhi.handle, f_xhi.at(p_to, u + 1))
                dve.tensor_tensor(xf_lo[:].rearrange("p t k n -> p (t k n)"), bank_of(s)[:],
                                  xf_hi[:].rearrange("p t k n -> p (t k n)").bitcast(F32),
                                  ALU.subtract).then_inc(f_xlo.handle, 1)
                dve.wait_ge(f_xlo.handle, f_xlo.at(p_to, u + 1))
                dve.sem_inc(f_freeV.handle, 1)

            def ffn(p, b, final, b_next=None):
                x = x_slot(b)
                for u in range(UNITS):
                    s0 = u * SLICES
                    for j in range(HSLICES):
                        n = u * HSLICES + j
                        s = s0 + j
                        yield s + 0.5
                        if j < KT:
                            dve.wait_ge(f_act.handle, f_act.at(p, u * KT + j + 1))
                            dve.wait_ge(f_lo.handle, f_lo.at(p, n - 1))
                            own(dve.scalar_tensor_tensor(hid[:, n % 2, 0, :], bank_of(s)[:, TOK:2 * TOK],
                                                         s2_sb[:, j:j + 1], gate[:, n % 2, :],
                                                         ALU.mult, ALU.mult))
                            dve.sem_inc(f_freeV.handle, 1)
                            dve.tensor_copy(ffn_dst(j)[0], hid[:, n % 2, 0:1, :]).then_inc(f_hi.handle, 1)
                        if j == HSLICES - 2:
                            if u + 1 < UNITS:
                                norm_unit(p, x, u + 1)
                            elif b_next is not None:
                                norm_unit(p + 1, x_slot(b_next), 0)
                    s = s0 + XT_SLICE
                    yield s + 0.5
                    if u + 1 < UNITS:
                        xt_low(p, s, p, u + 1)
                    elif b_next is not None:
                        xt_low(p, s, p + 1, 0)
                    else:
                        dve.sem_inc(f_freeV.handle, 1)
                    s = s0 + W3_SLICE
                    yield s + 0.5
                    dve.wait_ge(f_ps.handle, f_ps.at(p, s + 1))
                    o = bank_of(s)[:].rearrange("p (t d) -> p t d", t=2)
                    own(dve.tensor_tensor(hid[:, 0], o, bcast(w3s_row[:], 1, 2), ALU.mult))
                    dve.sem_inc(f_freeV.handle, 1)
                    xu = x[:, 2 * u:2 * u + 2, :]
                    own(dve.tensor_tensor(xu, xu, hid[:, 0], ALU.add))
                    if not final:
                        unit_stats(x, 2 * u, in_mv, d_stats)
                if final:
                    dve.sem_inc(x_final.handle, 1)

            def ssm_stage(b, p, next_delta=None):
                yield 0
                x = x_slot(b)
                for t in range(NT):
                    yield SSM_STEPS * t
                    if t == 0:
                        dve.wait_ge(a_clear.handle, a_clear.at(b, 1))
                    yield SSM_STEPS * t + 1
                    dve.wait_ge(a_proj.handle, a_proj.at(b, t + 1))
                    dve.tensor_tensor(dtv[:], Q[3][:, 2 * N:2 * N + H], bias_row[:], ALU.add).then_inc(a_dtv.handle, 1)
                    dve.wait_ge(a_soft.handle, a_soft.at(b, t + 1))
                    own(dve.scalar_tensor_tensor(dta[:, 0, :], dtv[:], 0.0, dtl[:], ALU.max, ALU.add))
                    own(dve.tensor_tensor(dta[:, 1, :], dta[:, 0, :], a_row[:], ALU.mult))
                    dve.tensor_tensor(seg[:], bcast(stri[:], 1, H), bcast(dta[:, 1, :], 2, P),
                                      ALU.mult).then_inc(a_seg.handle, 1)
                    yield SSM_STEPS * t + 2
                    dve.wait_ge(a_sums.handle, a_sums.at(b, t + 1))
                    own(dve.tensor_copy(sums[:], Q[0][:, 0:40]))
                    dve.sem_inc(a_sumc.handle, 1)
                    own(dve.tensor_tensor(ang[:], bcast(sums[:, 0:16].rearrange("p (k h) -> p k h", k=2), 3, PAIRS),
                                          freq[:].unsqueeze(1).unsqueeze(1).broadcast_to([P, 2, H, PAIRS]), ALU.mult))
                    own(dve.tensor_tensor(ang[:], ang[:], bcast(phase[:], 1, 2), ALU.add))
                    own(dve.tensor_scalar(angk[:], ang[:], 1.0 / (2 * PI), MAGIC, ALU.mult, ALU.add))
                    own(dve.tensor_scalar(angk[:], angk[:], MAGIC, None, ALU.subtract))
                    own(dve.scalar_tensor_tensor(ang[:], angk[:], -TWO_PI_HI, ang[:], ALU.mult, ALU.add))
                    own(dve.scalar_tensor_tensor(ang[:], angk[:], -TWO_PI_LO, ang[:], ALU.mult, ALU.add))
                    dve.tensor_scalar(angr[:], ang[:, 0], PI_SAFE, -PI_SAFE, ALU.min, ALU.max).then_inc(a_ang.handle, 1)
                    dve.tensor_copy(phase[:], ang[:, 1])
                    dve.wait_ge(a_trig.handle, a_trig.at(b, t + 1))
                    pair = bc[:, :, 0:2 * PAIRS].rearrange("p k (n two) -> p k two n", two=2)
                    v1 = bcast(pair[:, :, 0], 2, H)
                    v2 = bcast(pair[:, :, 1], 2, H)
                    c_, s_ = bcast(cosT[:], 1, 2), bcast(sinT[:], 1, 2)
                    dve.tensor_tensor(r1, v1, c_, ALU.mult)
                    dve.tensor_tensor(r2, v2, s_, ALU.mult)
                    dve.tensor_tensor(r3, v2, c_, ALU.mult)
                    own(dve.tensor_tensor(r4, v1, s_, ALU.mult))
                    rot = hat[:, :, :, 0:2 * PAIRS].rearrange("p k h (n two) -> p k h two n", two=2)
                    dve.tensor_tensor(rot[:, :, :, 0], r1, r2, ALU.add)
                    dve.tensor_tensor(rot[:, :, :, 1], r3, r4, ALU.subtract).then_inc(a_hat.handle, 1)
                    yield SSM_STEPS * t + 3
                    dve.wait_ge(a_hatT.handle, a_hatT.at(b, t + 1))
                    cps = Q[0][:].rearrange("p (k n) -> p k n", k=4)
                    dve.tensor_copy(cT[0:64, :, 0, :], cps[0:64])
                    dve.tensor_copy(cT[64:128, :, 1, :], cps[64:128]).then_inc(a_cT.handle, 1)
                    yield SSM_STEPS * t + 4
                    dve.wait_ge(a_score.handle, a_score.at(b, t + 1))
                    for i in range(2):
                        d_ = seg[:, 4 * i:4 * i + 4, :].rearrange("p h t -> p (h t)")
                        last = dve.tensor_tensor(d_, Q[1 + i][:], d_, ALU.mult)
                    last.then_inc(a_pm.handle, 1)
                    yield SSM_STEPS * t + 5
                    dve.wait_ge(a_y.handle, a_y.at(b, t + 1))
                    own(dve.tensor_tensor(y[:], Q[0][:].rearrange("p (h d) -> p h d", h=H),
                                          bcast(decays[:, 0, :], 2, HP), ALU.mult))
                    own(dve.tensor_tensor(y[:], Q[3][:].rearrange("p (h d) -> p h d", h=H), y[:], ALU.add))
                    own(dve.tensor_tensor(y[:], y[:], xD[:], ALU.add))
                    dve.tensor_tensor(y[:].rearrange("p h d -> p (h d)"), y[:].rearrange("p h d -> p (h d)"), sz[:],
                                      ALU.mult).then_inc(a_yv.handle, 1)
                    dl_ = decays[:, 1, :].rearrange("p (k two) -> p two k", two=2)
                    dve.tensor_tensor(hst[0:64], hst[0:64], bcast(dl_[0:64, 0], 2, HP), ALU.mult)
                    own(dve.tensor_tensor(hst[64:128], hst[64:128], bcast(dl_[64:128, 1], 2, HP), ALU.mult))
                    own(dve.tensor_tensor(hst[:].rearrange("p k d -> p (k d)"), Q[1][:, 0:4 * HP],
                                          hst[:].rearrange("p k d -> p (k d)"), ALU.add))
                    if t + 1 < NT:
                        normed(xn[:], x, t + 1, mv, rstd).then_inc(a_xn.handle, 1)
                    yield SSM_STEPS * t + 7
                    dve.wait_ge(a_out.handle, a_out.at(b, t + 1))
                    dve.wait_ge(a_yr.handle, a_yr.at(b, t + 1))
                    own(dve.scalar_tensor_tensor(x[:, t, :], Q[2][:, 0:D], yrstd[:], x[:, t, :],
                                                 ALU.mult, ALU.add))
                    dve.sem_inc(a_res.handle, 1)
                    if t % 2:
                        unit_stats(x, t - 1, fmv, f_stats)
                if next_delta is not None:
                    first_delta(next_delta)

            def pads(g, t):
                for h in range(2, 4):
                    s = slice(HD * h, HD * (h + 1))
                    dve.tensor_copy(kqpad[s, 0, h, :], kT[s, g])
                    last = dve.tensor_copy(kqpad[s, 1, h, :], qT[s, t, g])
                return last

            def delta_stage(b, p, next_ssm=True):
                yield 0
                x = x_slot(b)
                for t in range(NT):
                    yield D1_STEPS * t
                    if t == 0:
                        dve.wait_ge(d_clear.handle, d_clear.at(b, 1))
                    yield D1_STEPS * t + 1
                    dve.wait_ge(d_qkv.handle, d_qkv.at(b, t + 1))
                    own(dve.tensor_reduce(srow[:], ksq[:], AX.X, ALU.add))
                    dve.tensor_scalar(srow[:], srow[:], 1e-24, None, ALU.max).then_inc(d_ss.handle, 1)
                    own(dve.tensor_scalar(sig[:], sig[:], 0.5, 0.5, ALU.mult, ALU.add))
                    dve.sem_inc(d_beta.handle, 1)
                    own(dve.tensor_tensor(sig[:, 0:D], Q[2][:, 0:D], sig[:, 0:D], ALU.mult))
                    dve.tensor_tensor(uw[:, t, :, 0, :], sig[:, 0:D].rearrange("p (h d) -> p h d", h=DH),
                                      bcast(beta, 2, HD), ALU.mult)
                    dve.wait_ge(d_rn.handle, d_rn.at(b, t + 1))
                    own(dve.tensor_tensor(kn[:, t], k_sb[:], bcast(rn[:], 2, HD), ALU.mult))
                    dve.sem_inc(d_kn.handle, 1)
                    dve.tensor_tensor(uw[:, t, :, 1, :], kn[:, t], bcast(beta, 2, HD), ALU.mult)
                    if t + 1 < NT:
                        normed(xnd[:], x, t + 1, in_mv, drstd).then_inc(d_xn.handle, 1)
                    yield D1_STEPS * t + 2
                    dve.wait_ge(d_kqc.handle, d_kqc.at(b, t + 1))
                    pads(0, t).then_inc(d_padV.handle, 1)
                    yield D1_STEPS * t + 3
                    dve.wait_ge(d_gram.handle, d_gram.at(b, 2 * t + 1))
                    pads(1, t).then_inc(d_pad2V.handle, 1)
                    yield D1_STEPS * t + 4
                    dve.wait_ge(d_gram.handle, d_gram.at(b, 2 * t + 2))
                    dve.wait_ge(d_bm.handle, d_bm.at(b, t + 1))
                    gram = Q[1][:].rearrange("p (g k h i) -> p k g h i", g=G, k=2, h=4)
                    dve.tensor_tensor(amv.rearrange("p (g h) i -> p g h i", g=G), gram[:, 0],
                                      bmask[:].rearrange("p (g h) i -> p g h i", g=G),
                                      ALU.mult).then_inc(d_am.handle, 1)
                    own(dve.tensor_tensor(pc[:, t].rearrange("p (g h) i -> p g h i", g=G), gram[:, 1],
                                          umask[:].unsqueeze(1).unsqueeze(1).broadcast_to([P, G, 4, BLK]), ALU.mult))
                    dve.sem_inc(d_pc.handle, 1)
                for i in range(1, BLK):
                    yield SUB0 + i - 1
                    if i == 1:
                        dve.wait_ge(d_aun.handle, d_aun.at(b, 16))
                    pr = prod[:, 0:i * i].rearrange("p (c j) -> p c j", c=i)
                    own(dve.tensor_tensor(pr, ti[:, 0:i, 0:i], bcast(au[:, i, 0:i], 1, i), ALU.mult))
                    own(dve.tensor_reduce(ti[:, 0:i, i], pr, AX.X, ALU.add, negate=True))
                dve.sem_inc(d_inv.handle, 1)

                def normed_o(t):
                    dve.wait_ge(d_ors.handle, d_ors.at(b, t + 1))
                    own(dve.tensor_scalar(on[:], Q[2][:, 0:D], dmv[:, 0:1], drs[:], ALU.subtract, ALU.mult))
                    dve.sem_inc(d_done.handle, 1)
                    own(dve.tensor_tensor(on[:], on[:], lnw_row[:], ALU.mult))
                    own(dve.tensor_tensor(on[:], on[:], lnb_row[:], ALU.add))
                    own(dve.tensor_tensor(x[:, t, :], x[:, t, :], on[:], ALU.add))
                    if t % 2:
                        unit_stats(x, t - 1, fmv, f_stats)

                for t in range(NT):
                    for c in range(NB):
                        n = t * NB + c
                        s = slice(BLK * c, BLK * (c + 1))
                        yield D20 + D2_STEPS * t + 2 * c
                        if c == 0:
                            if t == 0:
                                dve.wait_ge(d_clear.handle, d_clear.at(b, 2))
                            dve.wait_ge(d_uwc.handle, d_uwc.at(b, t + 1))
                        dve.wait_ge(d_ws.handle, d_ws.at(b, n + 1))
                        us = u_sb[t % 2][s].rearrange("p h d -> p (h d)")
                        dve.scalar_tensor_tensor(us, Q[0][s, 0:D], -1.0, us, ALU.mult,
                                                 ALU.add).then_inc(d_u.handle, 1)
                        if c == 0 and t:
                            normed_o(t - 1)
                        yield D20 + D2_STEPS * t + 2 * c + 1
                        dve.wait_ge(d_sp.handle, d_sp.at(b, n + 1))
                        for g in range(G):
                            last = dve.tensor_tensor(sbd[:, g, :].rearrange("p (h d) -> p h d", h=4),
                                                     Q[3][:, g * P:(g + 1) * P].rearrange("p (h d) -> p h d", h=4),
                                                     bcast(bdmask[:], 2, HD), ALU.mult)
                        last.then_inc(d_s.handle, 1)
                    yield D20 + D2_STEPS * t + D2_STEPS - 1
                    if t == NT - 1 and next_ssm:
                        ssm_stats(b + 2)
                    dve.wait_ge(d_o.handle, d_o.at(b, t + 1))
                    own(dve.bn_stats(dbst[:], Q[2][:, 0:D]))
                    dve.bn_aggr(dmv[:], dbst[:]).then_inc(d_ost.handle, 1)
                normed_o(NT - 1)
                if next_ssm:
                    first_ssm(b + 2)

            own.restart()
            ssm_stats(0)
            first_ssm(0)
            alone(ssm_stage(0, 0))
            ssm_stats(1)
            first_ssm(1)
            norm_unit(0, x_slot(0), 0)
            xt_low(0, -1, 0, 0)
            window(ssm_stage(1, 1), ffn(0, 0, False, 1), SSM_PLAN)
            first_delta(0)
            with dve.Fori(1, B - 1) as b:
                own.restart()
                window(delta_stage(b - 1, 2 * b), ffn(2 * b - 1, b, False, b - 1), DELTA_PLAN)
                window(ssm_stage(b + 1, 2 * b + 1, b), ffn(2 * b, b - 1, True, b + 1), SSM_PLAN)
            own.restart()
            window(delta_stage(B - 2, 2 * B - 2, False), ffn(2 * B - 3, B - 1, False, B - 2), DELTA_PLAN)
            first_delta(B - 1)
            window(delta_stage(B - 1, 2 * B - 1, False), ffn(2 * B - 2, B - 2, True, B - 1), DELTA_PLAN)
            alone(ffn(2 * B - 1, B - 1, True))

        @block.tensor
        def _(pe):
            pe.wait_ge(w_dma, 16 * 13)
            pe.wait_ge(const_done, 1)
            pe.wait_ge(wout_done, 1)

            def bank(p, s):
                before = s - 4
                if before >= -1 or not isinstance(p, int) or p:
                    if before < -1:
                        before, p = before + UNITS * SLICES, p - 1
                    u, j = divmod(before, SLICES) if before >= 0 else (0, None)
                    if j is None:
                        pe.wait_ge(f_freeV.handle, f_freeV.at(p, 0))
                    elif KT <= j < HSLICES:
                        pe.wait_ge(f_freeA.handle, f_freeA.at(p, u * KT + j - KT + 1))
                    else:
                        done = j + 1 if j < KT else KT + 1 + j - XT_SLICE
                        pe.wait_ge(f_freeV.handle, f_freeV.at(p, u * (KT + 2) + done))
                return bank_of(s)

            def xt(p, s, p_to, u):
                pe.wait_ge(f_xn.handle, f_xn.at(p_to, u + 1))
                ps = bank(p, s)
                for t in range(2):
                    for k in range(2):
                        o = (2 * t + k) * P
                        last = pe.transpose(ps[:, o:o + P], xnf[:, t, k * P:(k + 1) * P], ident[:])
                last.then_inc(f_ps.handle, 1)

            def ffn(p, b, more=True):
                for u in range(UNITS):
                    s0 = u * SLICES
                    n0 = u * HSLICES
                    for j in range(KT):
                        yield s0 + j
                        if j == 0:
                            pe.wait_ge(f_xlo.handle, f_xlo.at(p, u + 1))
                        ps = bank(p, s0 + j)
                        for i, w in enumerate((w1_sb, w2_sb)):
                            for k in range(2):
                                for part in (xf_hi, xf_lo):
                                    last = pe.matmul(ps[:, i * TOK:(i + 1) * TOK].rearrange("p (t n) -> p t n", t=2),
                                                     w[:, k, j * P:(j + 1) * P], part[:, :, k, :],
                                                     start=(k == 0 and part is xf_hi), stop=(k == 1 and part is xf_lo))
                        last.then_inc(f_ps.handle, 1)
                    for layer, (w, src) in enumerate(((h1_sb, (hA_hi, hA_lo)), (h2_sb, (hB_hi, hB_lo)))):
                        for j in range(KT // 2):
                            s = s0 + KT + layer * (KT // 2) + j
                            yield s
                            ps = bank(p, s)
                            for ks in (range(KT - 2), range(KT - 2, KT)):
                                for i in range(2):
                                    o = (2 * j + i) * P
                                    for k in ks:
                                        if j == 0 and i == 0:
                                            done = k + 1 if layer == 0 else KT + k // 2 + 1
                                            pe.wait_ge(f_lo.handle, f_lo.at(p, n0 + done))
                                        for part in src:
                                            last = pe.matmul(ps[:, i * TOK:(i + 1) * TOK], w[:, k, o:o + P],
                                                             part[:, k, :], start=(i == 0 and k == 0 and part is src[0]),
                                                             stop=(i == 1 and k == KT - 1 and part is src[1]),
                                                             skip_group_check=True)
                                    if ks.start == 0 and i == 0:
                                        yield s + 0.5
                            last.then_inc(f_ps.handle, 1)
                    yield s0 + XT_SLICE
                    if u + 1 < UNITS:
                        xt(p, s0 + XT_SLICE, p, u + 1)
                    elif more:
                        xt(p, s0 + XT_SLICE, p + 1, 0)
                    yield s0 + W3_SLICE
                    ps = bank(p, s0 + W3_SLICE)
                    for t in range(2):
                        if t:
                            yield s0 + W3_SLICE + 0.5
                        for k in range(KT):
                            if t == 0:
                                pe.wait_ge(f_lo.handle, f_lo.at(p, n0 + KT + KT // 2 + k // 2 + 1))
                            for part in (hA_hi, hA_lo):
                                last = pe.matmul(ps[:, t * D:(t + 1) * D], part[:, k, t * P:(t + 1) * P], w3_sb[:, k, :],
                                                 start=(k == 0 and part is hA_hi), stop=(k == KT - 1 and part is hA_lo))
                    last.then_inc(f_ps.handle, 1 if u + 1 < UNITS or more else 2)

            def ssm_stage(b, p):
                for t in range(NT):
                    yield SSM_STEPS * t
                    pe.wait_ge(a_xn.handle, a_xn.at(b, t + 1))
                    for k in range(2):
                        last = pe.transpose(Q[0][:, k * P:(k + 1) * P], xn[:, k * P:(k + 1) * P], ident[:])
                    last.then_inc(a_xTp.handle, 1)
                    yield SSM_STEPS * t + 1
                    pe.wait_ge(a_xT.handle, a_xT.at(b, t + 1))
                    if t:
                        pe.wait_ge(a_res.handle, a_res.at(b, t))
                    for q, c0, c1 in ((1, 0, DI), (2, DI, 2 * DI), (3, 2 * DI, W_IN)):
                        for k in range(2):
                            last = pe.matmul(Q[q][:, 0:c1 - c0], xT[:, k, :], win_sb[:, k, c0:c1],
                                             start=(k == 0), stop=(k == 1))
                    last.then_inc(a_proj.handle, 1)
                    yield SSM_STEPS * t + 2
                    pe.wait_ge(a_seg.handle, a_seg.at(b, t + 1))
                    kinds = Q[0][:, 0:32].rearrange("p (g k h) -> p k g h", g=2, k=2)
                    both = dta[:]
                    pe.matmul(kinds[:, 0], tri[:], both, start=True, stop=True)
                    pe.matmul(kinds[:, 1], ones[:], both, start=True, stop=True)
                    pe.matmul(Q[0][:, 32:40], stri[:], dta[:, 1, :], start=True, stop=True).then_inc(a_sums.handle, 1)
                    pe.wait_ge(a_zx.handle, a_zx.at(b, t + 1))
                    for h in range(H):
                        q = Q[1 + h // 4]
                        if h % 4 == 0:
                            pe.matmul(q[:], far_i[:], past[:].rearrange("p h t -> p (h t)"), start=True, stop=False,
                                      skip_group_check=True)
                        o = (h % 4) * P
                        last = pe.matmul(q[:, o:o + P], seg[:, h, :], tri[:], start=False, stop=(h % 4 == 3),
                                         skip_group_check=True)
                    last.then_inc(a_segp.handle, 1)
                    yield SSM_STEPS * t + 3
                    pe.wait_ge(a_hat.handle, a_hat.at(b, t + 1))
                    pe.wait_ge(a_flat.handle, a_flat.at(b, t + 1))
                    for i, q in ((0, 3), (1, 0)):
                        for hp in range(4):
                            last = pe.transpose(Q[q][:, hp * P:(hp + 1) * P],
                                                hat[:, i, 2 * hp:2 * hp + 2, :].rearrange("p h n -> p (h n)"), ident[:])
                    last.then_inc(a_hatT.handle, 1)
                    yield SSM_STEPS * t + 4
                    pe.wait_ge(a_bT.handle, a_bT.at(b, t + 1))
                    pe.wait_ge(a_cT.handle, a_cT.at(b, t + 1))
                    for hp in range(4):
                        o = (hp % 2) * 2 * P
                        last = pe.matmul(Q[1 + hp // 2][:, o:o + 2 * P], bT[:, hp, :],
                                         cT[:, hp].rearrange("p e t -> p (e t)"), start=True, stop=True)
                    last.then_inc(a_score.handle, 1)
                    yield SSM_STEPS * t + 5
                    pe.wait_ge(a_pm.handle, a_pm.at(b, t + 1))
                    pe.wait_ge(a_wx.handle, a_wx.at(b, t + 1))
                    for h in range(H):
                        pe.matmul(Q[3][:, h * HP:(h + 1) * HP], seg[:, h, :], xdt[:, h, :], start=True, stop=True)
                    for h in range(H):
                        pe.matmul(Q[0][:, h * HP:(h + 1) * HP], cT[:, h // 2, h % 2, :], hst[:, h // 2, :],
                                  start=True, stop=True)
                    for h in range(H):
                        e, hp = h % 2, h // 2
                        last = pe.matmul(Q[1][64 * e:64 * e + 64, hp * HP:(hp + 1) * HP], hat[:, 0, h, :], wx[:, h, :],
                                         start=True, stop=True)
                    last.then_inc(a_y.handle, 1)
                    yield SSM_STEPS * t + 6
                    pe.wait_ge(a_yv.handle, a_yv.at(b, t + 1))
                    for k in range(4):
                        last = pe.transpose(Q[3][:, k * P:(k + 1) * P],
                                            y[:, 2 * k:2 * k + 2, :].rearrange("p h d -> p (h d)"), ident[:])
                    last.then_inc(a_yTp.handle, 1)
                    yield SSM_STEPS * t + 7
                    pe.wait_ge(a_yT.handle, a_yT.at(b, t + 1))
                    for k in range(4):
                        last = pe.matmul(Q[2][:, 0:D], yT[:, k, :], wout_sb[:, k, :], start=(k == 0), stop=(k == 3))
                    last.then_inc(a_out.handle, 1)

            def delta_stage(b, p, next_ssm=True):
                for t in range(NT):
                    yield D1_STEPS * t
                    pe.wait_ge(d_xn.handle, d_xn.at(b, t + 1))
                    for k in range(2):
                        last = pe.transpose(Q[0][:, k * P:(k + 1) * P], xnd[:, k * P:(k + 1) * P], ident[:])
                    last.then_inc(d_xTp.handle, 1)
                    yield D1_STEPS * t + 1
                    pe.wait_ge(d_xT.handle, d_xT.at(b, t + 1))
                    if t:
                        pe.wait_ge(d_pc.handle, d_pc.at(b, t))
                    for q, c0, c1 in ((1, 0, 2 * D), (2, 2 * D, W_QKVB)):
                        for k in range(2):
                            last = pe.matmul(Q[q][:, 0:c1 - c0], xTd[:, k, :], wqkvb_sb[:, k, c0:c1],
                                             start=(k == 0), stop=(k == 1))
                    last.then_inc(d_proj.handle, 1)
                    yield D1_STEPS * t + 2
                    pe.wait_ge(d_kn.handle, d_kn.at(b, t + 1))
                    pe.wait_ge(d_q.handle, d_q.at(b, t + 1))
                    knf = kn[:, t].rearrange("p h d -> p (h d)")
                    for i, src in enumerate((q_sb[:], knf)):
                        for g in range(G):
                            o = (2 * i + g) * P
                            last = pe.transpose(Q[3][:, o:o + P], src[:, g * P:(g + 1) * P], ident[:])
                    last.then_inc(d_kqT.handle, 1)
                    for g in range(G):
                        yield D1_STEPS * t + 3 + g
                        padA, padV = ((d_padA, d_padV), (d_pad2A, d_pad2V))[g]
                        pe.wait_ge(padA.handle, padA.at(b, t + 1))
                        pe.wait_ge(padV.handle, padV.at(b, t + 1))
                        for c in range(NB):
                            s = slice(BLK * c, BLK * (c + 1))
                            last = pe.matmul(Q[1][s, g * 256:(g + 1) * 256].rearrange("p (k i) -> p k i", k=8),
                                             kT[:, g, s], kqpad[:, :, :, s].rearrange("p k h i -> p (k h) i"),
                                             start=True, stop=True)
                        last.then_inc(d_gram.handle, 1)
                def form_uw(t):
                    pe.wait_ge(d_tbd.handle, d_tbd.at(b, (t + 1) * NB * 16))
                    if t:
                        pe.wait_ge(d_wT.handle, d_wT.at(b, t))
                    for h in range(DH):
                        last = pe.matmul(Q[1][:, h * 64:(h + 1) * 64], tbd[:, h, :],
                                         uw[:, t, h].rearrange("p k d -> p (k d)"), start=True, stop=True)
                    last.then_inc(d_uwp.handle, 1)

                def transpose_w(t):
                    pe.wait_ge(d_uwc.handle, d_uwc.at(b, t + 1))
                    wf = w_sb[:].rearrange("p h d -> p (h d)")
                    for g in range(G):
                        last = pe.transpose(Q[1][:, g * P:(g + 1) * P], wf[:, g * P:(g + 1) * P], ident[:])
                    last.then_inc(d_wTp.handle, 1)

                def query(t, c):
                    s = slice(BLK * c, BLK * (c + 1))
                    for g in range(G):
                        pe.matmul(Q[2][s, g * P:(g + 1) * P], qT[:, t, g, s], sbd[:, g, :],
                                  start=(g == 0), stop=False, skip_group_check=True)

                yield uw_step(0)
                form_uw(0)
                yield wt_step(0)
                transpose_w(0)
                for t in range(NT):
                    for c in range(NB):
                        n = t * NB + c
                        s = slice(BLK * c, BLK * (c + 1))
                        step = D20 + D2_STEPS * t + 2 * c
                        yield step
                        if c == 0:
                            pe.wait_ge(d_wT.handle, d_wT.at(b, t + 1))
                        if n:
                            pe.wait_ge(d_s.handle, d_s.at(b, n))
                        for g in range(G):
                            last = pe.matmul(Q[0][s, g * P:(g + 1) * P], wT[t % 2][:, g, s], sbd[:, g, :],
                                             start=True, stop=True)
                        last.then_inc(d_ws.handle, 1)
                        if c:
                            query(t, c)
                        yield step + 1
                        if c == 0:
                            if t:
                                pe.wait_ge(d_done.handle, d_done.at(b, t))
                            query(t, c)
                        pe.wait_ge(d_u.handle, d_u.at(b, n + 1))
                        for g in range(G):
                            last = pe.matmul(Q[3][:, g * P:(g + 1) * P],
                                             kn[s, t].rearrange("p h d -> p (h d)")[:, g * P:(g + 1) * P],
                                             u_sb[t % 2][s].rearrange("p h d -> p (h d)")[:, g * P:(g + 1) * P],
                                             start=(n == 0 and g == 0), stop=(n == NT * NB - 1),
                                             skip_group_check=True)
                        last.then_inc(d_sp.handle, 1)
                        if t + 1 < NT:
                            if step + 1 == uw_step(t + 1):
                                form_uw(t + 1)
                            if step + 1 == wt_step(t + 1):
                                transpose_w(t + 1)
                    yield D20 + D2_STEPS * t + D2_STEPS - 1
                    pe.wait_ge(d_pbd.handle, d_pbd.at(b, t + 1))
                    for h in range(DH):
                        last = pe.matmul(Q[2][:, h * HD:(h + 1) * HD], pbd[:, h, :], u_sb[t % 2][:, h, :],
                                         start=False, stop=True, skip_group_check=True)
                    last.then_inc(d_o.handle, 1)

            alone(ssm_stage(0, 0))
            xt(0, -1, 0, 0)
            pe.wait_ge(wr_dma, 16 * 5)
            pe.wait_ge(wd_dma, 16)
            window(ssm_stage(1, 1), ffn(0, 0), SSM_PLAN)
            with pe.Fori(1, B - 1) as b:
                window(delta_stage(b - 1, 2 * b), ffn(2 * b - 1, b), DELTA_PLAN)
                window(ssm_stage(b + 1, 2 * b + 1), ffn(2 * b, b - 1), SSM_PLAN)
            window(delta_stage(B - 2, 2 * B - 2, False), ffn(2 * B - 3, B - 1), DELTA_PLAN)
            window(delta_stage(B - 1, 2 * B - 1, False), ffn(2 * B - 2, B - 2), DELTA_PLAN)
            alone(ffn(2 * B - 1, B - 1, False))


def kernel(**inputs):
    import numpy as np
    import concourse.bacc as bacc
    from concourse.bass_utils import run_bass_kernel_spmd

    a = {k: np.asarray(v) for k, v in inputs.items()}

    def flat(v):
        return np.ascontiguousarray(v)

    def column(v, k):
        return flat(v.reshape(k, P).T)

    arrays = {
        "x": flat(a["L0_attn_a_x"].reshape(B * L, D)),
        "w_in": flat(a["L0_attn_a_W_in"]),
        "w_out": flat(a["L0_attn_a_W_out"]),
        "dt_bias": flat(a["L0_attn_a_dt_bias"]),
        "a_log": flat(a["L0_attn_a_A_log"]),
        "d_skip": flat(a["L0_attn_a_D_skip"]),
        "norm_w": column(a["L0_attn_a_norm_weight"], 4),
        "wqkvb": flat(np.concatenate([a["L0_attn_b_Wq"], a["L0_attn_b_Wk"], a["L0_attn_b_Wv"], a["L0_attn_b_Wb"]], 1)),
        "ln_w": flat(a["L0_attn_b_ln_w"]),
        "ln_b": flat(a["L0_attn_b_ln_b"]),
        "w1": flat(a["L0_ffn_w1_w"].T),
        "w1s": column(a["L0_ffn_w1_s"], KT),
        "w2": flat(a["L0_ffn_w2_w"].T),
        "w2s": column(a["L0_ffn_w2_s"], KT),
        "h1": flat(a["L0_ffn_h1_w"].T),
        "h1s": column(a["L0_ffn_h1_s"], KT),
        "h2": flat(a["L0_ffn_h2_w"].T),
        "h2s": column(a["L0_ffn_h2_s"], KT),
        "w3": flat(a["L0_ffn_w3_w"].T),
        "w3s": flat(a["L0_ffn_w3_s"]),
    }
    nc = bacc.Bacc("TRN2", target_bir_lowering=False, num_devices=1)
    args = [nc.dram_tensor(f"{k}_dram", v.shape, F32, kind="ExternalInput").ap() for k, v in arrays.items()]
    a_scr = nc.dram_tensor("a_scr", (NT, NB, DH, BLK, BLK), F32, kind="Internal").ap()
    t_scr = nc.dram_tensor("t_scr", (NT, NB, DH, BLK, BLK), F32, kind="Internal").ap()
    out = nc.dram_tensor("out_dram", (B * L, D), F32, kind="ExternalOutput").ap()
    hybrid_kernel(nc, *args, a_scr, t_scr, out)
    r = run_bass_kernel_spmd(nc, [{f"{k}_dram": v for k, v in arrays.items()}], core_ids=[0])
    return r.results[0]["out_dram"].reshape(B, L, D)
```
